# Optimizing a Trainium2 kernel written in Bass

```python
import numpy as np
import jax
import jax.numpy as jnp

def _softmax(x, axis=-1):
    return jax.nn.softmax(x, axis=axis)

def _gelu(x):
    return jax.nn.gelu(x, approximate=True)

def _silu(x):
    return jax.nn.silu(x)

def _sigmoid(x):
    return jax.nn.sigmoid(x)

def _layernorm(x, axis=-1, eps=1e-05):
    m = jnp.mean(x, axis=axis, keepdims=True)
    v = jnp.var(x, axis=axis, keepdims=True)
    return (x - m) / jnp.sqrt(v + eps)

def _scatter_add(tgt, idx, src, axis=0):
    return tgt.at[idx].add(src)

def _segment_sum(src, seg, n):
    return jax.ops.segment_sum(src, seg, n)
kernel_name = 'mk_vit_tower_cls_d2_tok_img768_r4_6e920d'

def setup_inputs(seed: int=0):
    np.random.seed(seed)
    _w = jnp.asarray

    def _rec_inputs():
        import jax
        import jax.numpy as jnp
        _rk = jax.random.key(seed)
        x = 7.57192e-06 + 1.00007 * jax.random.normal(jax.random.fold_in(_rk, 1), (64, 3, 224, 224), jnp.float32)
        cls_tok = 0.02 * jax.random.normal(jax.random.fold_in(_rk, 5), (1, 1, 192), jnp.float32)
        return (x, cls_tok)
    x, cls_tok = _rec_inputs()

    def _L0_tok_setup():
        import jax, jax.numpy as jnp
        import numpy as np
        IMG = 224
        PS = 16
        C = 3
        E = 192
        N = IMG // PS * (IMG // PS)
        PD = PS * PS
        key = jax.random.key(seed)
        ks = jax.random.split(key, 6)
        B = 64
        pixel_values = jax.random.normal(ks[0], (B, C, IMG, IMG), dtype=jnp.float32)
        decode_weights = 0.01 * jax.random.normal(ks[1], (N, E, PD), dtype=jnp.float32)
        decode_biases = jnp.zeros((N, E), dtype=jnp.float32)
        merge_weights = 0.01 * jax.random.normal(ks[2], (N, C), dtype=jnp.float32)
        merge_biases = jnp.zeros((N,), dtype=jnp.float32)
        cls_embedding = jax.random.normal(ks[3], (E,), dtype=jnp.float32)
        pos_embedding = 0.02 * jax.random.normal(ks[4], (N + 1, E), dtype=jnp.float32)
        return {'pixel_values': pixel_values, 'decode_weights': decode_weights, 'decode_biases': decode_biases, 'merge_weights': merge_weights, 'merge_biases': merge_biases, 'cls_embedding': cls_embedding, 'pos_embedding': pos_embedding}
    _L0_tok_all = _L0_tok_setup()
    _L0_tok_in = {k: v for k, v in _L0_tok_all.items() if k in ('decode_weights', 'decode_biases', 'merge_weights', 'merge_biases', 'cls_embedding', 'pos_embedding')}
    del _L0_tok_all

    def _L0_attn_setup():
        import jax, jax.numpy as jnp
        import numpy as np
        from jax import lax
        K = 12
        K_Q = 6
        M = 1
        N_REP = K // K_Q
        D = 192
        H = D // (K * M)
        KSZ = 4
        OUT_EXPAND = 3
        DIM_MEMORY = K * H
        DIM_QUERY_TOTAL = K_Q * H * M * 2
        DIM_MEM_TOTAL = DIM_MEMORY + K
        DIM_CONV_TOTAL = DIM_MEM_TOTAL + DIM_QUERY_TOTAL
        DIM_EXPAND = H * OUT_EXPAND
        DIM_SWIGLU_HEAD = DIM_EXPAND * 2
        DIM_SWIGLU_TOTAL = K * DIM_SWIGLU_HEAD
        DIM_SKIP = D // 4
        DIM_GATE = K
        DIM_TOTAL = DIM_CONV_TOTAL + DIM_SKIP + DIM_GATE
        THETA_MIN, THETA_MAX = (0.001, 3.0)

        def _rmsnorm(v, w, eps=1e-06):
            return v * lax.rsqrt(jnp.mean(v * v, axis=-1, keepdims=True) + eps) * w
        key = jax.random.key(seed)
        ks = jax.random.split(key, 8)
        B, L = (4, 1024)
        x = jax.random.normal(ks[0], (B, L, D), dtype=jnp.float32)
        W_in = jax.random.normal(ks[1], (D, DIM_TOTAL), dtype=jnp.float32) * 0.02
        conv_w = jax.random.normal(ks[2], (KSZ, DIM_CONV_TOTAL), dtype=jnp.float32) * 0.2
        k_norm_w = jnp.ones((H,), jnp.float32)
        q_norm_w = jnp.ones((DIM_QUERY_TOTAL,), jnp.float32)
        grid = np.geomspace(THETA_MIN, THETA_MAX, K).reshape(1, 1, K, 1, 1)
        base = np.tile(grid, (1, 1, 1, H, 1))
        u = np.clip((base - THETA_MIN) / (THETA_MAX - THETA_MIN), 0.0001, 1 - 0.0001)
        theta_raw = jnp.asarray(np.log(u) - np.log(1 - u), dtype=jnp.float32)
        w_int_raw = jnp.zeros((1, 1, K_Q, N_REP, H, M), jnp.float32)
        decay_slopes = jnp.asarray(np.log(np.exp(np.geomspace(0.001, 0.1, K)) - 1), dtype=jnp.float32)
        score_scale = jnp.ones((K,), jnp.float32)
        score_bias = jnp.zeros((K,), jnp.float32)
        tanh_scale = jnp.ones((K,), jnp.float32)
        W_readout = jax.random.normal(ks[3], (K, 2 * H, DIM_SWIGLU_HEAD), dtype=jnp.float32) * 0.05
        W_gate = jax.random.normal(ks[4], (DIM_GATE, K * 2 * H), dtype=jnp.float32) * 0.02
        gnorm_w = jnp.ones((K * 2 * H,), jnp.float32)
        W_skip = jax.random.normal(ks[5], (DIM_SKIP, DIM_SWIGLU_TOTAL), dtype=jnp.float32) * 0.02
        highway_scale = jnp.ones((K,), jnp.float32)
        W_out = jax.random.normal(ks[6], (K * DIM_EXPAND, D), dtype=jnp.float32) * 0.02
        return {'x': x, 'W_in': W_in, 'conv_w': conv_w, 'k_norm_w': k_norm_w, 'q_norm_w': q_norm_w, 'theta_raw': theta_raw, 'w_int_raw': w_int_raw, 'decay_slopes': decay_slopes, 'score_scale': score_scale, 'score_bias': score_bias, 'tanh_scale': tanh_scale, 'W_readout': W_readout, 'W_gate': W_gate, 'gnorm_w': gnorm_w, 'W_skip': W_skip, 'highway_scale': highway_scale, 'W_out': W_out}
    _L0_attn_all = _L0_attn_setup()
    _L0_attn_in = {k: v for k, v in _L0_attn_all.items() if k in ('W_in', 'conv_w', 'k_norm_w', 'q_norm_w', 'theta_raw', 'w_int_raw', 'decay_slopes', 'score_scale', 'score_bias', 'tanh_scale', 'W_readout', 'W_gate', 'gnorm_w', 'W_skip', 'highway_scale', 'W_out')}
    del _L0_attn_all

    def _L0_ffn_setup():
        import jax, jax.numpy as jnp
        import numpy as np
        EPS_NORM = 1e-06
        EPS_Q = 1e-05

        def rmsnorm(x, g):
            return x * jax.lax.rsqrt(jnp.mean(x * x, axis=-1, keepdims=True) + EPS_NORM) * g

        def activation_quant(x):
            scale = 127.0 / jnp.maximum(jnp.max(jnp.abs(x), axis=-1, keepdims=True), EPS_Q)
            return jnp.clip(jnp.round(x * scale), -128, 127) / scale

        def weight_quant(w):
            scale = 1.0 / jnp.maximum(jnp.mean(jnp.abs(w)), EPS_Q)
            return jnp.clip(jnp.round(w * scale), -1, 1) / scale

        def bitlinear(x, w, g):
            x_norm = rmsnorm(x, g)
            x_q = x_norm + jax.lax.stop_gradient(activation_quant(x_norm) - x_norm)
            w_q = w + jax.lax.stop_gradient(weight_quant(w) - w)
            return jnp.einsum('bsd,od->bso', x_q, w_q)
        key = jax.random.key(seed)
        k1, k2, k3 = jax.random.split(key, 3)
        B, S, D, H = (8, 1024, 192, 512)
        x = jax.random.normal(k1, (B, S, D), dtype=jnp.float32)
        w_in = jax.random.normal(k2, (2 * H, D), dtype=jnp.float32) * 0.002
        w_out = jax.random.normal(k3, (D, H), dtype=jnp.float32) * 0.002
        g_in = jnp.ones((D,), dtype=jnp.float32)
        g_out = jnp.ones((H,), dtype=jnp.float32)
        return {'x': x, 'w_in': w_in, 'g_in': g_in, 'w_out': w_out, 'g_out': g_out}
    _L0_ffn_all = _L0_ffn_setup()
    _L0_ffn_in = {k: v for k, v in _L0_ffn_all.items() if k in ('w_in', 'g_in', 'w_out', 'g_out')}
    del _L0_ffn_all

    def _L1_attn_setup():
        import jax, jax.numpy as jnp
        import numpy as np
        DIM, HEADS = (192, 12)
        key = jax.random.key(seed)
        ks = jax.random.split(key, 9)
        B, N, C, H = (4, 256, DIM, HEADS)
        s = 0.02
        return {'x': jax.random.normal(ks[0], (B, N, C), jnp.float32), 'W_qkv': jax.random.normal(ks[1], (C, 3 * C), jnp.float32) * s, 'W_proj': jax.random.normal(ks[2], (C, C), jnp.float32) * s, 'b_proj': jax.random.normal(ks[3], (C,), jnp.float32) * s, 'W_l': jax.random.normal(ks[4], (H, H), jnp.float32) * s, 'b_l': jax.random.normal(ks[5], (H,), jnp.float32) * s, 'W_w': jax.random.normal(ks[6], (H, H), jnp.float32) * s, 'b_w': jax.random.normal(ks[7], (H,), jnp.float32) * s, 'lamb': jax.random.normal(ks[8], (H,), jnp.float32) * 0.1}
    _L1_attn_all = _L1_attn_setup()
    _L1_attn_in = {k: v for k, v in _L1_attn_all.items() if k in ('W_qkv', 'W_proj', 'b_proj', 'W_l', 'b_l', 'W_w', 'b_w', 'lamb')}
    del _L1_attn_all

    def _L1_ffn_setup():
        import jax, jax.numpy as jnp
        import numpy as np
        B, T, H, F, E = (128, 32, 192, 768, 3)
        key = jax.random.key(seed)
        ks = jax.random.split(key, 4)
        s = 0.02
        return {'x': jax.random.normal(ks[0], (B, T, H), jnp.float32), 'Wg': jax.random.normal(ks[1], (E, H), jnp.float32) * s, 'W1': jax.random.normal(ks[2], (E, H, F), jnp.float32) * s, 'b1': jnp.zeros((E, F), jnp.float32), 'W2': jax.random.normal(ks[3], (E, F, H), jnp.float32) * s, 'b2': jnp.zeros((E, H), jnp.float32)}
    _L1_ffn_all = _L1_ffn_setup()
    _L1_ffn_in = {k: v for k, v in _L1_ffn_all.items() if k in ('Wg', 'W1', 'b1', 'W2', 'b2')}
    del _L1_ffn_all
    return {'x': x, 'cls_tok': cls_tok, 'L0_tok_decode_weights': _L0_tok_in['decode_weights'], 'L0_tok_decode_biases': _L0_tok_in['decode_biases'], 'L0_tok_merge_weights': _L0_tok_in['merge_weights'], 'L0_tok_merge_biases': _L0_tok_in['merge_biases'], 'L0_tok_cls_embedding': _L0_tok_in['cls_embedding'], 'L0_tok_pos_embedding': _L0_tok_in['pos_embedding'], 'L0_attn_W_in': _L0_attn_in['W_in'], 'L0_attn_conv_w': _L0_attn_in['conv_w'], 'L0_attn_k_norm_w': _L0_attn_in['k_norm_w'], 'L0_attn_q_norm_w': _L0_attn_in['q_norm_w'], 'L0_attn_theta_raw': _L0_attn_in['theta_raw'], 'L0_attn_w_int_raw': _L0_attn_in['w_int_raw'], 'L0_attn_decay_slopes': _L0_attn_in['decay_slopes'], 'L0_attn_score_scale': _L0_attn_in['score_scale'], 'L0_attn_score_bias': _L0_attn_in['score_bias'], 'L0_attn_tanh_scale': _L0_attn_in['tanh_scale'], 'L0_attn_W_readout': _L0_attn_in['W_readout'], 'L0_attn_W_gate': _L0_attn_in['W_gate'], 'L0_attn_gnorm_w': _L0_attn_in['gnorm_w'], 'L0_attn_W_skip': _L0_attn_in['W_skip'], 'L0_attn_highway_scale': _L0_attn_in['highway_scale'], 'L0_attn_W_out': _L0_attn_in['W_out'], 'L0_ffn_w_in': _L0_ffn_in['w_in'], 'L0_ffn_g_in': _L0_ffn_in['g_in'], 'L0_ffn_w_out': _L0_ffn_in['w_out'], 'L0_ffn_g_out': _L0_ffn_in['g_out'], 'L1_attn_W_qkv': _L1_attn_in['W_qkv'], 'L1_attn_W_proj': _L1_attn_in['W_proj'], 'L1_attn_b_proj': _L1_attn_in['b_proj'], 'L1_attn_W_l': _L1_attn_in['W_l'], 'L1_attn_b_l': _L1_attn_in['b_l'], 'L1_attn_W_w': _L1_attn_in['W_w'], 'L1_attn_b_w': _L1_attn_in['b_w'], 'L1_attn_lamb': _L1_attn_in['lamb'], 'L1_ffn_Wg': _L1_ffn_in['Wg'], 'L1_ffn_W1': _L1_ffn_in['W1'], 'L1_ffn_b1': _L1_ffn_in['b1'], 'L1_ffn_W2': _L1_ffn_in['W2'], 'L1_ffn_b2': _L1_ffn_in['b2']}

def reference(x, cls_tok, L0_tok_decode_weights, L0_tok_decode_biases, L0_tok_merge_weights, L0_tok_merge_biases, L0_tok_cls_embedding, L0_tok_pos_embedding, L0_attn_W_in, L0_attn_conv_w, L0_attn_k_norm_w, L0_attn_q_norm_w, L0_attn_theta_raw, L0_attn_w_int_raw, L0_attn_decay_slopes, L0_attn_score_scale, L0_attn_score_bias, L0_attn_tanh_scale, L0_attn_W_readout, L0_attn_W_gate, L0_attn_gnorm_w, L0_attn_W_skip, L0_attn_highway_scale, L0_attn_W_out, L0_ffn_w_in, L0_ffn_g_in, L0_ffn_w_out, L0_ffn_g_out, L1_attn_W_qkv, L1_attn_W_proj, L1_attn_b_proj, L1_attn_W_l, L1_attn_b_l, L1_attn_W_w, L1_attn_b_w, L1_attn_lamb, L1_ffn_Wg, L1_ffn_W1, L1_ffn_b1, L1_ffn_W2, L1_ffn_b2):
    import jax
    import jax.numpy as jnp

    def _L0_tok_ref(pixel_values, decode_weights, decode_biases, merge_weights, merge_biases, cls_embedding, pos_embedding):
        import jax, jax.numpy as jnp
        import numpy as np
        IMG = 224
        PS = 16
        C = 3
        E = 192
        N = IMG // PS * (IMG // PS)
        PD = PS * PS
        B = pixel_values.shape[0]
        Nh = IMG // PS
        x = pixel_values.reshape(B, C, Nh, PS, Nh, PS)
        x = x.transpose(0, 1, 2, 4, 3, 5).reshape(B, C, N, PD)
        decoded = jnp.einsum('bcnp,nfp->bcnf', x, decode_weights) + decode_biases[None, None]
        merged = jnp.einsum('bcnf,nc->bnf', decoded, merge_weights) + merge_biases[None, :, None]
        cls = jnp.broadcast_to(cls_embedding[None, None, :], (B, 1, E))
        out = jnp.concatenate([cls, merged], axis=1) + pos_embedding[None]
        return out

    def _L0_attn_ref(x, W_in, conv_w, k_norm_w, q_norm_w, theta_raw, w_int_raw, decay_slopes, score_scale, score_bias, tanh_scale, W_readout, W_gate, gnorm_w, W_skip, highway_scale, W_out):
        import jax, jax.numpy as jnp
        import numpy as np
        from jax import lax
        K = 12
        K_Q = 6
        M = 1
        N_REP = K // K_Q
        D = 192
        H = D // (K * M)
        KSZ = 4
        OUT_EXPAND = 3
        DIM_MEMORY = K * H
        DIM_QUERY_TOTAL = K_Q * H * M * 2
        DIM_MEM_TOTAL = DIM_MEMORY + K
        DIM_CONV_TOTAL = DIM_MEM_TOTAL + DIM_QUERY_TOTAL
        DIM_EXPAND = H * OUT_EXPAND
        DIM_SWIGLU_HEAD = DIM_EXPAND * 2
        DIM_SWIGLU_TOTAL = K * DIM_SWIGLU_HEAD
        DIM_SKIP = D // 4
        DIM_GATE = K
        DIM_TOTAL = DIM_CONV_TOTAL + DIM_SKIP + DIM_GATE
        THETA_MIN, THETA_MAX = (0.001, 3.0)

        def _rmsnorm(v, w, eps=1e-06):
            return v * lax.rsqrt(jnp.mean(v * v, axis=-1, keepdims=True) + eps) * w
        B, L, _ = x.shape
        z_all = x @ W_in
        z_conv = z_all[..., :DIM_CONV_TOTAL]
        c_skip = z_all[..., DIM_CONV_TOTAL:DIM_CONV_TOTAL + DIM_SKIP]
        gate_logits = z_all[..., DIM_CONV_TOTAL + DIM_SKIP:]
        z_conv = lax.conv_general_dilated(z_conv, conv_w[:, None, :], (1,), [(KSZ - 1, 0)], dimension_numbers=('NWC', 'WIO', 'NWC'), feature_group_count=DIM_CONV_TOTAL)
        z_conv = jax.nn.silu(z_conv)
        z_mem = z_conv[..., :DIM_MEM_TOTAL]
        q_raw = z_conv[..., DIM_MEM_TOTAL:]
        k_val = _rmsnorm(z_mem[..., :DIM_MEMORY].reshape(B, L, K, H), k_norm_w)
        s_raw = z_mem[..., DIM_MEMORY:]
        q_raw = _rmsnorm(q_raw, q_norm_w).reshape(B, L, K_Q, 1, H, M, 2)
        q_re, q_im = (q_raw[..., 0], q_raw[..., 1])
        theta = THETA_MIN + (THETA_MAX - THETA_MIN) * jax.nn.sigmoid(theta_raw)
        w_int = jnp.exp(jnp.clip(w_int_raw, -5.0, 5.0))
        pos = jnp.arange(L, dtype=jnp.float32)
        slopes = jax.nn.softplus(decay_slopes).reshape(1, 1, K)
        dist = jnp.maximum(jnp.float32(L - 1) - pos, 0.0)
        log_time_weight = -slopes * dist[None, :, None]
        score_raw = score_scale[None, None, :] * s_raw + score_bias[None, None, :]
        p_w = jnp.clip(jax.nn.softplus(score_raw) * jax.nn.softplus(log_time_weight), 1e-06, 1000.0)
        k_f = k_val[..., None]
        phi = jnp.tanh(k_f * tanh_scale[None, None, :, None, None]) * theta
        kvw = k_f * p_w[..., None, None]
        re = kvw * jnp.cos(phi)
        im = kvw * jnp.sin(phi)
        flat = K * H * M
        stack = jnp.concatenate([p_w, re.reshape(B, L, flat), im.reshape(B, L, flat)], axis=-1)
        cs = jnp.cumsum(stack, axis=1)
        den_acc, re_f, im_f = jnp.split(cs, [K, K + flat], axis=-1)
        inv_den = (1.0 / jnp.maximum(den_acc, 0.0001))[..., None, None]
        state_re = (re_f.reshape(B, L, K, H, M) * inv_den).reshape(B, L, K_Q, N_REP, H, M)
        state_im = (im_f.reshape(B, L, K, H, M) * inv_den).reshape(B, L, K_Q, N_REP, H, M)
        match_re = state_re * q_re + state_im * q_im
        match_im = state_im * q_re - state_re * q_im
        out_re = jnp.sum(match_re * w_int, axis=-1).reshape(B, L, K, H)
        out_im = jnp.sum(match_im * w_int, axis=-1).reshape(B, L, K, H)
        out_complex = jnp.concatenate([out_re, out_im], axis=-1)
        oc_flat = out_complex.reshape(B, L, K * 2 * H)
        gate_for_norm = gate_logits @ W_gate
        g = oc_flat * jax.nn.sigmoid(gate_for_norm)
        g = g * lax.rsqrt(jnp.mean(g * g, axis=-1, keepdims=True) + 1e-06) * gnorm_w
        out_complex = g.reshape(B, L, K, 2 * H)
        y_spec = jnp.einsum('blkf,kfn->blkn', out_complex, W_readout)
        y_skip = (c_skip @ W_skip).reshape(B, L, K, DIM_SWIGLU_HEAD)
        y_spec_val, y_spec_gate = jnp.split(y_spec, 2, axis=-1)
        y_skip_val, y_skip_gate = jnp.split(y_skip, 2, axis=-1)
        hs = highway_scale[None, None, :, None]
        y_val = y_spec_val + hs * y_skip_val
        y_gate = y_spec_gate + hs * y_skip_gate
        y = y_val * jax.nn.silu(y_gate)
        return y.reshape(B, L, K * DIM_EXPAND) @ W_out

    def _L0_ffn_ref(x, w_in, g_in, w_out, g_out):
        import jax, jax.numpy as jnp
        import numpy as np
        EPS_NORM = 1e-06
        EPS_Q = 1e-05

        def rmsnorm(x, g):
            return x * jax.lax.rsqrt(jnp.mean(x * x, axis=-1, keepdims=True) + EPS_NORM) * g

        def activation_quant(x):
            scale = 127.0 / jnp.maximum(jnp.max(jnp.abs(x), axis=-1, keepdims=True), EPS_Q)
            return jnp.clip(jnp.round(x * scale), -128, 127) / scale

        def weight_quant(w):
            scale = 1.0 / jnp.maximum(jnp.mean(jnp.abs(w)), EPS_Q)
            return jnp.clip(jnp.round(w * scale), -1, 1) / scale

        def bitlinear(x, w, g):
            x_norm = rmsnorm(x, g)
            x_q = x_norm + jax.lax.stop_gradient(activation_quant(x_norm) - x_norm)
            w_q = w + jax.lax.stop_gradient(weight_quant(w) - w)
            return jnp.einsum('bsd,od->bso', x_q, w_q)
        h = bitlinear(x, w_in, g_in)
        up, gate = jnp.split(h, 2, axis=-1)
        y = jax.nn.silu(gate) * up
        return bitlinear(y, w_out, g_out)

    def _L1_attn_ref(x, W_qkv, W_proj, b_proj, W_l, b_l, W_w, b_w, lamb):
        import jax, jax.numpy as jnp
        import numpy as np
        DIM, HEADS = (192, 12)
        B, N, C = x.shape
        H = W_l.shape[0]
        d = C // H
        scale = d ** (-0.5)
        qkv = (x @ W_qkv).reshape(B, N, 3, H, d)
        q = qkv[:, :, 0].transpose(0, 2, 1, 3) * scale
        k = qkv[:, :, 1].transpose(0, 2, 1, 3)
        v = qkv[:, :, 2].transpose(0, 2, 1, 3)
        attn = jnp.einsum('bhnd,bhmd->bhnm', q, k)
        attn = jnp.einsum('bhnm,hg->bgnm', attn, W_l) + b_l[None, :, None, None]
        attn = jax.nn.softmax(attn, axis=-1)
        attn = jnp.einsum('bhnm,hg->bgnm', attn, W_w) + b_w[None, :, None, None]
        eye = jnp.eye(N, dtype=attn.dtype)
        reaction = 3.0 * jnp.einsum('bhnk,bhkm->bhnm', attn - eye, attn) + attn
        attn = attn + lamb[None, :, None, None] * reaction
        out = jnp.einsum('bhnm,bhmd->bhnd', attn, v)
        out = out.transpose(0, 2, 1, 3).reshape(B, N, C)
        return out @ W_proj + b_proj

    def _L1_ffn_ref(x, Wg, W1, b1, W2, b2):
        import jax, jax.numpy as jnp
        import numpy as np
        B, T, H, F, E = (128, 32, 192, 768, 3)
        scores = jax.nn.softmax(jnp.mean(x, axis=1) @ Wg.T, axis=-1)
        _, idx = jax.lax.top_k(scores, 1)
        sel = idx[:, 0]
        h = jax.nn.gelu(jnp.einsum('bth,ehf->betf', x, W1) + b1[None, :, None, :], approximate=False)
        y = jnp.einsum('betf,efh->beth', h, W2) + b2[None, :, None, :]
        w = scores * jax.nn.one_hot(sel, E, dtype=scores.dtype)
        out = jnp.einsum('beth,be->bth', y, w)
        return out
    h = _L0_tok_ref(x, L0_tok_decode_weights, L0_tok_decode_biases, L0_tok_merge_weights, L0_tok_merge_biases, L0_tok_cls_embedding, L0_tok_pos_embedding)
    h = jnp.concatenate([jnp.broadcast_to(cls_tok, (h.shape[0], 1, h.shape[2])), h], axis=1)
    h = h + _L0_attn_ref(_layernorm(h, axis=-1), L0_attn_W_in, L0_attn_conv_w, L0_attn_k_norm_w, L0_attn_q_norm_w, L0_attn_theta_raw, L0_attn_w_int_raw, L0_attn_decay_slopes, L0_attn_score_scale, L0_attn_score_bias, L0_attn_tanh_scale, L0_attn_W_readout, L0_attn_W_gate, L0_attn_gnorm_w, L0_attn_W_skip, L0_attn_highway_scale, L0_attn_W_out)
    h = h + _L0_ffn_ref(_layernorm(h, axis=-1), L0_ffn_w_in, L0_ffn_g_in, L0_ffn_w_out, L0_ffn_g_out)
    h = h + _L1_attn_ref(_layernorm(h, axis=-1), L1_attn_W_qkv, L1_attn_W_proj, L1_attn_b_proj, L1_attn_W_l, L1_attn_b_l, L1_attn_W_w, L1_attn_b_w, L1_attn_lamb)
    h = h + _L1_ffn_ref(_layernorm(h, axis=-1), L1_ffn_Wg, L1_ffn_W1, L1_ffn_b1, L1_ffn_W2, L1_ffn_b2)
    return h

_drawn_inputs = setup_inputs


def setup_inputs(seed=0):
    import zlib

    import numpy as np

    out = dict(_drawn_inputs(seed))
    spreads = {'L0_tok_decode_biases': (0.0, 0.1),
     'L0_tok_merge_biases': (0.0, 0.1),
     'L0_attn_k_norm_w': (1.0, 0.2),
     'L0_attn_q_norm_w': (1.0, 0.2),
     'L0_attn_w_int_raw': (0.0, 0.1),
     'L0_attn_score_scale': (1.0, 0.6),
     'L0_attn_score_bias': (0.0, 0.8),
     'L0_attn_tanh_scale': (1.0, 0.2),
     'L0_attn_gnorm_w': (1.0, 0.2),
     'L0_attn_highway_scale': (1.0, 0.6),
     'L0_ffn_g_in': (1.0, 0.6),
     'L0_ffn_g_out': (1.0, 0.6),
     'L1_ffn_b1': (0.0, 0.1),
     'L1_ffn_b2': (0.0, 0.1)}
    factors = {'L0_attn_W_gate': 8.0, 'L1_attn_W_l': 200.0, 'L1_attn_b_l': 200.0, 'L1_attn_W_w': 8.0}
    for name, (base, spread) in spreads.items():
        noise = np.random.default_rng([zlib.crc32(name.encode()), seed]).standard_normal(out[name].shape)
        drawn = base * np.exp(spread * noise) if base else spread * noise
        out[name] = jnp.asarray(drawn.astype(out[name].dtype))
    for name, factor in factors.items():
        out[name] = (out[name] * factor).astype(out[name].dtype)
    return out
```

```python
import concourse.bass as bass
from concourse import mybir
from contextlib import ExitStack

B, C, IMG, PS = 64, 3, 224, 16
NH = IMG // PS
NP_ = NH * NH
L = NP_ + 2
D = 192
T = L // 2
HW = 96
KH, HD = 12, 16
NQ = 6
TAPS = 4
CONV = KH * HD + KH + NQ * HD * 2
SKIP = D // 4
FS = 48
FH = 512
FM = 768
NE = 3
PP = 7
NG = NP_ // PP
PD = PS * PS
NB = 10
NT = 20
NPAD = NB * NT
SR = KH * NB
EPS_LN = 1e-5
EPS_RMS = 1e-6
EPS_Q = 1e-5
MAGIC = 12582912.0
THETA_MIN, THETA_MAX = 0.001, 3.0
LOG1P_TERMS = 7


def vit_program(nc, a, out, images=B):
    f32, bf16, i32 = mybir.dt.float32, mybir.dt.bfloat16, mybir.dt.int32
    ALU, ACT, AX = mybir.AluOpType, mybir.ActivationFunctionType, mybir.AxisListType

    h_dram = nc.dram_tensor("h_tokens", (B, L, D), f32, kind="Internal").ap()

    ctx = ExitStack()
    with ctx:
        def sb(name, shape, dt=f32):
            return ctx.enter_context(nc.sbuf_tensor(name, list(shape), dt))

        def sems(names):
            return [ctx.enter_context(nc.semaphore(n)) for n in names.split()]

        ident = sb("ident", (128, 128))
        ident_b = sb("ident_b", (128, 128), bf16)
        upper = sb("upper", (T, T))
        ones = sb("ones", (128, 128))
        half_pi = sb("half_pi", (128, 1))
        neg_half = sb("neg_half", (128, 32))
        w_in = sb("w_in", (HW, 2, CONV + SKIP + KH))
        conv_w = sb("conv_w", (HW, 4, TAPS))
        conv_ws = sb("conv_ws", (KH, TAPS))
        k_norm = sb("k_norm", (T, 2 * D))
        tanh_scale = sb("tanh_scale", (T, 2 * D))
        theta = sb("theta", (T, 2 * D))
        q_w = sb("q_w", (T, 2, 2 * D))
        score_w = sb("score_w", (T, 2 * KH))
        score_b = sb("score_b", (T, 2 * KH))
        time_w = sb("time_w", (T, 2 * KH))
        dist = sb("dist", (T, 2 * KH))
        w_gate = sb("w_gate", (KH, 2 * D))
        w_read = sb("w_read", (112, 6, 2 * HW))
        w_out = sb("w_out", (HW, 6, D))
        fq1 = sb("fq1", (HW, 2, 2 * FH), bf16)
        fq2 = sb("fq2", (128, 4, D), bf16)
        g_in = sb("g_in", (T, 2 * D))
        g_out = sb("g_out", (T, FH))
        w_mean = sb("w_mean", (128, 2))
        w_abs = sb("w_abs", (128, 2))
        w_qkv = sb("w_qkv", (HW, 2, 3 * D))
        mix_l = sb("mix_l", (HW, 2, KH))
        mix_w = sb("mix_w", (SR + 1, SR))
        lam = sb("lam", (128, 3))
        lam_1 = sb("lam_1", (128, 3))
        lam_2 = sb("lam_2", (128, 3))
        w_proj = sb("w_proj", (128, 3, D))
        b_proj = sb("b_proj", (T, 2 * D))
        w_route = sb("w_route", (HW, 2, NE))

        psum_a = ctx.enter_context(nc.psum_tensor("psum_a", [128, 4, 512], f32))
        psum_c = ctx.enter_context(nc.psum_tensor("psum_c", [128, 4, 512], f32))

        (const_loaded, const_memset, ident_ready, setup_v, setup_a, setup_pe, setup_done_v,
         setup_done_a) = sems("const_loaded const_memset ident_ready setup_v setup_a setup_pe setup_done_v setup_done_a")

        with ExitStack() as tmp:
            def sbt(name, shape, dt=f32):
                return tmp.enter_context(nc.sbuf_tensor("init_" + name, list(shape), dt))
            w_read_f = sbt("w_read_f", (112, 6, 2 * HW))
            wf1 = sbt("wf1", (HW, 2, 2 * FH))
            wf2 = sbt("wf2", (128, 4, D))
            q_int = sbt("q_int", (T, 2, 2 * D))
            decay = sbt("decay", (T, 2 * KH))
            sp_u = sbt("sp_u", (T, 2 * KH))
            sp_z = sbt("sp_z", (T, 2 * KH))
            sp_z2 = sbt("sp_z2", (T, 2 * KH))
            sp_p = sbt("sp_p", (T, 2 * KH))
            scratch = sbt("scratch", (128, 2 * 2 * FH))
            rscale = sbt("rscale", (128, 2))
            cls = sbt("cls", (B, 3, D))

            loads = [(w_in, "W_in"), (conv_w, "conv_w"), (conv_ws, "conv_ws"), (k_norm, "k_norm"),
                     (tanh_scale, "tanh_scale"), (theta, "theta"), (q_w, "q_norm"), (q_int, "w_int"),
                     (score_w, "score_w"), (score_b, "score_b"), (dist, "dist"), (decay, "decay"),
                     (w_gate, "W_gate"), (w_read, "W_read"), (w_read_f, "W_read_f"), (w_out, "W_out"),
                     (wf1, "ffn_w1"), (wf2, "ffn_w2"), (g_in, "g_in"), (g_out, "g_out"),
                     (w_qkv, "W_qkv"), (mix_l, "mix_l"), (mix_w, "mix_w"), (lam, "lam"),
                     (w_proj, "W_proj"), (b_proj, "b_proj"), (w_route, "W_route"), (cls, "cls"),
                     (upper, "upper"), (ident, "ident")]
            LOADED = 16 * len(loads)
            cls_added, cls_stored = sems("cls_added cls_stored")
            block = tmp.enter_context(nc.Block())

            @block.sync
            def _(sp):
                for tile, name in loads:
                    full = tuple(slice(None) for _ in tile.shape)
                    sp.dma_start(tile[full], a[name]).then_inc(const_loaded, 16)
                sp.wait_ge(cls_added, 1)
                sp.dma_start(h_dram[:, 0:2, :], cls[:, 0:2, :]).then_inc(cls_stored, 16)
                sp.wait_ge(cls_stored, 16)

            @block.gpsimd
            def _(pool):
                nc.gpsimd.memset(ones[:, :], 1.0)
                nc.gpsimd.memset(half_pi[:, :], 1.5707963267948966)
                nc.gpsimd.memset(neg_half[:, :], -0.5).then_inc(const_memset, 1)

            @block.tensor
            def _(pe):
                pe.wait_ge(const_memset, 1)
                pe.wait_ge(setup_a, 5)
                nc.tensor.matmul(psum_a[:, 0, 0:1], ones[0:HW, :], w_abs[0:HW, 0:1], start=True, stop=True)
                nc.tensor.matmul(psum_a[:, 0, 1:2], ones[:, :], w_abs[:, 1:2], start=True,
                                 stop=True).then_inc(setup_pe, 1)

            @block.scalar
            def _(act):
                act.wait_ge(const_loaded, LOADED)
                nc.scalar.activation(sp_u[:, :], decay[:, :], ACT.Abs).then_inc(setup_a, 1)
                act.wait_ge(setup_a, 1)
                nc.scalar.activation(sp_u[:, :], sp_u[:, :], ACT.Exp, scale=-1.0).then_inc(setup_a, 1)
                nc.scalar.activation(theta[:, :], theta[:, :], ACT.Tanh, scale=0.5).then_inc(setup_a, 1)
                act.wait_ge(setup_a, 3)
                nc.scalar.activation(scratch[0:HW, :], wf1[:, :, :].rearrange("p k n -> p (k n)"), ACT.Abs,
                                     accum_out=w_abs[0:HW, 0:1]).then_inc(setup_a, 1)
                act.wait_ge(setup_a, 4)
                nc.scalar.activation(scratch[:, 0:4 * D], wf2[:, :, :].rearrange("p k n -> p (k n)"), ACT.Abs,
                                     accum_out=w_abs[:, 1:2]).then_inc(setup_a, 1)
                act.wait_ge(setup_v, 1)
                nc.scalar.activation(q_int[:, :, :], q_int[:, :, :], ACT.Exp).then_inc(setup_a, 1)
                act.wait_ge(setup_done_a, 1)
                nc.scalar.activation(sp_u[:, :], time_w[:, :], ACT.Exp).then_inc(setup_a, 1)

            @block.vector
            def _(dve):
                count = [0]

                def link(ins):
                    count[0] += 1
                    ins.then_inc(setup_v, 1)
                    dve.wait_ge(setup_v, count[0])

                dve.wait_ge(const_loaded, LOADED)
                link(nc.vector.tensor_scalar(q_int[:, :, :], q_int[:, :, :], -5.0, 5.0, ALU.max, ALU.min))
                nc.vector.tensor_tensor(cls[:, 1, :], cls[:, 1, :], cls[:, 2, :], ALU.add).then_inc(cls_added, 1)
                nc.vector.tensor_copy(ident_b[:, :], ident[:, :])
                nc.vector.tensor_tensor(w_read[:, :, :], w_read[:, :, :], w_read_f[:, :, :], ALU.mult)
                nc.vector.tensor_scalar(lam_1[:, :], lam[:, :], -2.0, 1.0, ALU.mult, ALU.add)
                link(nc.vector.tensor_scalar(lam_2[:, :], lam[:, :], 3.0, None, ALU.mult))
                dve.wait_ge(setup_a, 3)
                link(nc.vector.tensor_scalar(theta[:, :], theta[:, :], 0.5, 0.5, ALU.mult, ALU.add))
                link(nc.vector.tensor_scalar(theta[:, :], theta[:, :], THETA_MAX - THETA_MIN, THETA_MIN,
                                             ALU.mult, ALU.add))

                def log1p_u():
                    link(nc.vector.tensor_scalar(sp_p[:, :], sp_u[:, :], 2.0, None, ALU.add))
                    link(nc.vector.reciprocal(sp_p[:, :], sp_p[:, :]))
                    link(nc.vector.tensor_tensor(sp_z[:, :], sp_u[:, :], sp_p[:, :], ALU.mult))
                    link(nc.vector.tensor_tensor(sp_z2[:, :], sp_z[:, :], sp_z[:, :], ALU.mult))
                    link(nc.vector.tensor_scalar(sp_p[:, :], sp_z2[:, :], 2.0 / (2 * LOG1P_TERMS - 1), None, ALU.mult))
                    for k in range(LOG1P_TERMS - 2, 0, -1):
                        link(nc.vector.scalar_tensor_tensor(out=sp_p[:, :], in0=sp_p[:, :], scalar=2.0 / (2 * k + 1),
                                                            in1=sp_z2[:, :], op0=ALU.add, op1=ALU.mult))
                    link(nc.vector.scalar_tensor_tensor(out=sp_p[:, :], in0=sp_p[:, :], scalar=2.0,
                                                        in1=sp_z[:, :], op0=ALU.add, op1=ALU.mult))

                log1p_u()
                link(nc.vector.scalar_tensor_tensor(out=sp_p[:, :], in0=decay[:, :], scalar=0.0, in1=sp_p[:, :],
                                                    op0=ALU.max, op1=ALU.add))
                nc.vector.scalar_tensor_tensor(out=time_w[:, :], in0=sp_p[:, :], scalar=-1.0, in1=dist[:, :],
                                               op0=ALU.mult, op1=ALU.mult).then_inc(setup_done_a, 1)
                dve.wait_ge(setup_a, 6)
                link(nc.vector.tensor_tensor(q_w[:, :, :], q_w[:, :, :], q_int[:, :, :], ALU.mult))
                dve.wait_ge(setup_a, 7)
                log1p_u()
                link(nc.vector.tensor_copy(time_w[:, :], sp_p[:, :]))
                dve.wait_ge(setup_pe, 1)
                nc.vector.tensor_scalar(w_mean[:, 0:1], psum_a[:, 0, 0:1], 1.0 / (2 * FH * D), EPS_Q, ALU.mult, ALU.max)
                link(nc.vector.tensor_scalar(w_mean[:, 1:2], psum_a[:, 0, 1:2], 1.0 / (FH * D), EPS_Q, ALU.mult, ALU.max))
                link(nc.vector.reciprocal(rscale[:, :], w_mean[:, :]))
                for wf, wq, rows, n in ((wf1, fq1, HW, 0), (wf2, fq2, 128, 1)):
                    link(nc.vector.tensor_scalar(wf[:, :, :], wf[:, :, :], rscale[0:rows, n:n + 1], MAGIC,
                                                 ALU.mult, ALU.add))
                    link(nc.vector.tensor_scalar(wf[:, :, :], wf[:, :, :], MAGIC, 1.0, ALU.subtract, ALU.min))
                    link(nc.vector.tensor_scalar(wq[:, :, :], wf[:, :, :], -1.0, None, ALU.max))

        with ExitStack() as tmp:
            def sbt(name, shape, dt=f32):
                return tmp.enter_context(nc.sbuf_tensor("tok_" + name, list(shape), dt))
            XG = PP * C * 2 * B
            xg = [sbt(f"xg{k}", (128, XG + PP * C)) for k in range(2)]
            wg = [sbt(f"wg{k}", (128, PP, 2, D)) for k in range(2)]
            bs = [sbt(f"bs{k}", (5, PP, B)) for k in range(2)]
            bm = [sbt(f"bm{k}", (5, PP, D)) for k in range(2)]
            xm = [sbt(f"xm{k}", (128, PP, 2 * B)) for k in range(2)]
            hg = [sbt(f"hg{k}", (B, PP, D)) for k in range(2)]
            tok_loaded, tok_merged, tok_product, tok_ready = [], [], [], []
            for k in range(2):
                s = sems(f"tok_loaded{k} tok_merged{k} tok_product{k} tok_evac{k}")
                tok_loaded.append(s[0])
                tok_merged.append(s[1])
                tok_product.append(s[2])
                tok_ready.append(s[3])
            tok_stored, tok_step = [sems(f"tok_stored{k}")[0] for k in range(2)], sems("tok_step")[0]
            block = tmp.enter_context(nc.Block())
            PAIRS = NG // 2

            @block.sync
            def _(sp):
                def load(g, k):
                    sp.dma_start(xg[k][:, :], a["pixels"][bass.ds(g, 1)].rearrange("o p n -> (o p) n")).then_inc(tok_loaded[k], 16)
                    sp.dma_start(wg[k][:, :, :].rearrange("p a b c -> p (a b c)"),
                                 a["dec_w"][bass.ds(g, 1)].rearrange("o p n -> (o p) n")).then_inc(tok_loaded[k], 16)
                    sp.dma_start(bs[k][:, :, :].rearrange("p a b -> p (a b)"),
                                 a["bias_s"][bass.ds(g, 1)].rearrange("o p n -> (o p) n")).then_inc(tok_loaded[k], 16)
                    sp.dma_start(bm[k][:, :, :].rearrange("p a b -> p (a b)"),
                                 a["bias_m"][bass.ds(g, 1)].rearrange("o p n -> (o p) n")).then_inc(tok_loaded[k], 16)

                for k in range(2):
                    load(k, k)
                with sp.Fori(1, PAIRS) as i:
                    for k in range(2):
                        sp.wait_ge(tok_product[k], i)
                        load(i * 2 + k, k)

            @block.vector
            def _(dve):
                def merge(i, k):
                    dve.wait_ge(tok_loaded[k], i * 64 + 64)
                    px = xg[k][:, 0:XG].rearrange("p (n c m) -> p n c m", n=PP, c=C)
                    mw = xg[k][:, XG:XG + PP * C].unsqueeze(2).broadcast_to([128, PP * C, 2 * B])
                    flat = xg[k][:, 0:XG].rearrange("p (n m) -> p n m", m=2 * B)
                    nc.vector.tensor_tensor(flat, flat, mw, ALU.mult).then_inc(tok_step, 1)
                    dve.wait_ge(tok_step, i * 4 + (2 * k + 1))
                    nc.vector.tensor_tensor(xm[k][:, :, :], px[:, :, 0, :], px[:, :, 1, :], ALU.add).then_inc(tok_step, 1)
                    dve.wait_ge(tok_step, i * 4 + (2 * k + 2))
                    nc.vector.tensor_tensor(xm[k][:, :, :], xm[k][:, :, :], px[:, :, 2, :],
                                            ALU.add).then_inc(tok_merged[k], 1)

                for k in range(2):
                    merge(0, k)
                with dve.Fori(1, PAIRS) as i:
                    for k in range(2):
                        dve.wait_ge(tok_product[k], i)
                        merge(i, k)

            @block.tensor
            def _(pe):
                def products(i, k):
                    pe.wait_ge(tok_merged[k], i + 1)
                    bank = psum_a if k == 0 else psum_c
                    for n in range(PP):
                        o = bank[0:B, n // 2, (n % 2) * D:(n % 2 + 1) * D]
                        for c in range(2):
                            nc.tensor.matmul(o, xm[k][:, n, c * B:(c + 1) * B], wg[k][:, n, c, :],
                                             start=(c == 0), stop=False)
                        last = nc.tensor.matmul(o, bs[k][:, n, :], bm[k][:, n, :], start=False, stop=True)
                    last.then_inc(tok_product[k], 1)

                for k in range(2):
                    products(0, k)
                with pe.Fori(1, PAIRS) as i:
                    for k in range(2):
                        pe.wait_ge(tok_ready[k], i)
                        products(i, k)

            @block.scalar
            def _(act):
                def evacuate(i, k):
                    act.wait_ge(tok_product[k], i + 1)
                    bank = psum_a if k == 0 else psum_c
                    nc.scalar.activation(hg[k][:, 0:6, :].rearrange("p (a b) n -> p a (b n)", b=2),
                                         bank[0:B, 0:3, 0:2 * D], ACT.Copy)
                    nc.scalar.activation(hg[k][:, 6, :], bank[0:B, 3, 0:D], ACT.Copy).then_inc(tok_ready[k], 1)
                    act.wait_ge(tok_ready[k], i + 1)
                    act.dma_start(h_dram[:, bass.ds((i * 2 + k) * PP + 2, PP), :], hg[k][:, :, :]).then_inc(tok_stored[k], 16)

                for k in range(2):
                    evacuate(0, k)
                with act.Fori(1, PAIRS) as i:
                    for k in range(2):
                        act.wait_ge(tok_stored[k], i * 16)
                        evacuate(i, k)
                for k in range(2):
                    act.wait_ge(tok_stored[k], 16 * PAIRS)



        x = sb("x", (T, 2, D))
        xn = sb("xn", (T, 2, D))
        xT = sb("xT", (HW, 2, L))
        zc = sb("zc", (HW, 4, L))
        zs = sb("zs", (KH, L))
        gT = sb("gT", (KH, L))
        gs = sb("gs", (T, 2, 6, 112))
        zk = sb("zk", (T, 2, D + KH))
        zq = sb("zq", (T, 2, D))
        sq = sb("sq", (T, 2, D))
        var = sb("var", (T, 2 * KH + 2))
        rs = sb("rs", (T, 2 * KH + 2))
        score = sb("score", (T, 2, KH))
        sp_u = sb("sp_u", (T, 2 * KH))
        sp_z = sb("sp_z", (T, 2 * KH))
        sp_z2 = sb("sp_z2", (T, 2 * KH))
        sp_p = sb("sp_p", (T, 2 * KH))
        kv = sb("kv", (T, 2, D))
        kvw = sb("kvw", (T, 2, D))
        phi = sb("phi", (T, 2 * D))
        phi_abs = sb("phi_abs", (T, 2 * D))
        sin_p = sb("sin_p", (T, 2, D))
        cos_p = sb("cos_p", (T, 2, D))
        stack = sb("stack", (T, 2, 2 * D + KH))
        den = sb("den", (T, 2, KH))
        s_re = sb("s_re", (T, 2 * D))
        s_im = sb("s_im", (T, 2 * D))
        qx_re = sb("qx_re", (T, 2 * D))
        qx_im = sb("qx_im", (T, 2 * D))
        m_a = sb("m_a", (T, 2 * D))
        m_b = sb("m_b", (T, 2 * D))
        oc = sb("oc", (T, 2, 2 * D))
        gate_t = sb("gate_t", (T, 2, 2 * D))
        sum_g = sb("sum_g", (T, 2))
        rs_g = sb("rs_g", (T, 2))
        gsT = sb("gsT", (112, 6, L))
        y_silu_t = sb("y_silu_t", (HW, 2, 2, L))
        yT = sb("yT", (HW, 6, L))
        h1 = sb("h1", (T, 2, D))
        stats = sb("stats", (T, 2, 6))
        mv = sb("mv", (T, 2, 2))
        rstd = sb("rstd", (T, 2))
        n2_a = sb("n2_a", (T, 2))
        n2_b = sb("n2_b", (T, 2))
        amax = sb("amax", (T, 2))
        qscale = sb("qscale", (T, 2))
        deq1 = sb("deq1", (T, 2))
        deq2 = sb("deq2", (T, 2))
        xqb = sb("xqb", (T, 2, D), bf16)
        xqT = sb("xqT", (HW, 4, 100), bf16)
        sg_f = sb("sg_f", (T, 2, FH))
        y_f = sb("y_f", (T, 2, FH))
        y_junk = sb("y_junk", (T, FH))
        sum_f = sb("sum_f", (T, 2))
        f_a = sb("f_a", (T, 2))
        f_b = sb("f_b", (T, 2))
        f_c = sb("f_c", (T, 2))
        yqb = sb("yqb", (T, 2, FH), bf16)
        yqT = sb("yqT", (128, 8, 100), bf16)
        h2 = sb("h2", (T, 2, D))
        h3 = sb("h3", (T, 2, D))
        h4 = sb("h4", (T, 2, D))
        stats_c = sb("stats_c", (T, 2, 6))
        mv_c = sb("mv_c", (T, 2, 2))
        rstd_c = sb("rstd_c", (T, 2))
        xn_c = sb("xn_c", (T, 2, D))
        xT_c = sb("xT_c", (HW, 2, L))
        qT = sb("qT", (HW, 2, NPAD))
        kT = sb("kT", (HW + 1, 2, L))
        vp = sb("vp", (T, 2, KH, 32))
        qm = sb("qm", (HW + 1, 2, NT, SR))
        nmax = sb("nmax", (SR, 2, NT // 2))
        expo = [sb(f"expo{k}", (SR + 1, 2, L)) for k in range(2)]
        zsum = sb("zsum", (SR, NT // 2, 2))
        rz = sb("rz", (SR, NT // 2, 2))
        wz = [sb(f"wz{k}", (SR + 1, 2, SR)) for k in range(2)]
        at = sb("at", (T, NT, 2, SR))
        wT = sb("wT", (128, 3, NPAD))
        wp = sb("wp", (T, 2, 3 * 128))
        o2 = sb("o2", (128, 3, NPAD))
        xsum = sb("xsum", (HW, 2))
        lmax = sb("lmax", (T, 2))
        lexp = sb("lexp", (T, NE))
        lsum = sb("lsum", (T, 1))
        route_w = sb("route_w", (T, 1))
        sel_f = sb("sel_f", (1, 4))
        sel = sb("sel", (1, 1), i32)
        e_w1 = sb("e_w1", (HW, 2, FM))
        e_w2 = sb("e_w2", (128, 6, D))
        e_b1 = sb("e_b1", (128, 6))
        e_b2 = sb("e_b2", (T, 2 * D))
        hT = sb("hT", (128, 6, L))
        o = sb("o", (T, 2, D))

        (x_loaded, stat1, rstd1, xn1, xT1_ps, xT1, z_ps, z_tap, conv_done, zT_ps, silu_done, kq_var, kq_rs,
         exp_u, tanh_in, tanh_out, phi_ready, trig, stack_ready, gate_ps, cum_ps, gate_done, g_ready, g_sum,
         g_rs, gs_ready, gsT_ps, gsT_ready, y_ps, y_silu, y_ready, out1_ps, h1_ready) = sems(
            "x_loaded stat1 rstd1 xn1 xT1_ps xT1 z_ps z_tap conv_done zT_ps silu_done kq_var kq_rs "
            "exp_u tanh_in tanh_out phi_ready trig stack_ready gate_ps cum_ps gate_done g_ready g_sum "
            "g_rs gs_ready gsT_ps gsT_ready y_ps y_silu y_ready out1_ps h1_ready")
        (stat2, norm2_s, xq_ready, xqT_ps, xqT_ready, h_ps, sg_ready, yf_ready, yf_sum, yf_s, yq_ready,
         yqT_ps, yqT_ready, out2_ps, h2_ready) = sems(
            "stat2 norm2_s xq_ready xqT_ps xqT_ready h_ps sg_ready yf_ready yf_sum yf_s yq_ready "
            "yqT_ps yqT_ready out2_ps h2_ready")
        (stat3, rstd3, xn3, xT3_ps, xT3, qkv_ps, q_ready, k_ready, v_ready, qm_ready, s_ps, s_max, exp_done,
         rz_ready, wz_ready, at_ps, at_ready, w_ps, w_ready, wT_ps, wp_ready, w2_ps, o2_ready, proj_ps,
         stat4, rstd4, xn4, xT4_ps, xT4, xsum_ready, logit_ps, lmax_ready, lexp_ready, sel_ready,
         expert_loaded, hid_ps, hid_ready, ffn_ps, o_ready, o_stored) = sems(
            "stat3 rstd3 xn3 xT3_ps xT3 qkv_ps q_ready k_ready v_ready qm_ready s_ps s_max exp_done "
            "rz_ready wz_ready at_ps at_ready w_ps w_ready wT_ps wp_ready w2_ps o2_ready proj_ps "
            "stat4 rstd4 xn4 xT4_ps xT4 xsum_ready logit_ps lmax_ready lexp_ready sel_ready "
            "expert_loaded hid_ps hid_ready ffn_ps o_ready o_stored")
        v_first, v_second, a_first, a_second, p_first, p_second, pad_set, pad_loaded = sems(
            "v_first v_second a_first a_second p_first p_second pad_set pad_loaded")
        V1, V2, A1, A2, P1, P2 = 45, 11, 3, 1, 14, 2

        block = ctx.enter_context(nc.Block())
        SU = NT // 2

        def run(eng, phases):
            def both(n, m):
                for stream, phase in ORDER:
                    if phase in phases:
                        phases[phase](n if stream == 1 else m)

            def one(which, n):
                for stream, phase in ORDER:
                    if stream == which and phase in phases:
                        phases[phase](n)

            one(1, 1)
            both(2, 1)
            with eng.Fori(3, images) as n:
                both(n, n - 1)
            both(images, images - 1)
            one(2, images)

        def linked(eng, sem, steps):
            count = [0]

            def link(ins, n):
                count[0] += 1
                ins.then_inc(sem, 1)
                eng.wait_ge(sem, n * steps + ((count[0] - 1) % steps + 1 - steps))
            return link, count

        def own_wait(eng):
            eng.nop(nofuse=True)

        def signal(eng, ins, sem, n, each=1, at=0):
            ins.then_inc(sem, 1)
            eng.wait_ge(sem, n if each == 1 else n * each + (at + 1 - each))

        @block.sync
        def _(sp):
            sp.wait_ge(pad_set, 3)
            for k in range(2):
                for t in range(2):
                    sp.dma_start(wz[k][:, t, :], mix_w[:, :]).then_inc(pad_loaded, 16)
            sp.dma_start(qm[HW:HW + 1, 1, :, :].rearrange("p t r -> p (t r)"), a["b_l"]).then_inc(pad_loaded, 16)

            def load(n):
                for j in range(2):
                    sp.dma_start(x[:, j, :], h_dram[bass.ds(n - 1, 1), j * T:(j + 1) * T, :]
                                 .rearrange("o p d -> (o p) d")).then_inc(x_loaded, 16)

            def load_next(n):
                sp.wait_ge(h1_ready, n)
                if not (isinstance(n, int) and n >= images):
                    load(n + 1)

            def experts(n):
                sp.wait_ge(sel_ready, n)
                own_wait(sp)
                e = sp.value_load(sel[0:1, 0:1], min_val=0, max_val=NE - 1)
                sp.dma_start(e_w1[:, :, :].rearrange("p a b -> p (a b)"),
                             a["W1"][bass.ds(e, 1)].rearrange("o p n -> (o p) n")).then_inc(expert_loaded, 16)
                sp.dma_start(e_w2[:, :, :].rearrange("p a b -> p (a b)"),
                             a["W2"][bass.ds(e, 1)].rearrange("o p n -> (o p) n")).then_inc(expert_loaded, 16)
                sp.dma_start(e_b1[:, :], a["b1"][bass.ds(e, 1)].rearrange("o p n -> (o p) n")).then_inc(expert_loaded, 16)
                sp.dma_start(e_b2[:, :], a["b2"][bass.ds(e, 1)].rearrange("o p n -> (o p) n")).then_inc(expert_loaded, 16)

            def store(n):
                sp.wait_ge(o_ready, n)
                for j in range(2):
                    sp.dma_start(out[bass.ds(n - 1, 1), j * T:(j + 1) * T, :].rearrange("o p d -> (o p) d"),
                                 o[:, j, :]).then_inc(o_stored, 16)

            load(1)
            sp_phases = {"h1": load_next, "route": experts, "ffn_out": store}
            run(sp, sp_phases)
            sp.wait_ge(o_stored, 32 * images)

        @block.gpsimd
        def _(pool):
            nc.gpsimd.memset(kT[:, :, :], 1.0)
            nc.gpsimd.memset(vp[:, :, :, :], 0.0)
            nc.gpsimd.memset(qm[:, :, :, :], 0.0)
            nc.gpsimd.memset(qT[:, :, :], 0.0).then_inc(pad_set, 1)
            for k in range(2):
                nc.gpsimd.memset(expo[k][:, :, :], 1.0).then_inc(pad_set, 1)
            pool.wait_ge(pad_set, 3)
            link1, c1 = linked(pool, p_first, P1)
            link2, c2 = linked(pool, p_second, P2)

            def power(out_, in_, w):
                return nc.gpsimd.tensor_tensor(out_, in_, neg_half[0:T, 0:w], ALU.pow)

            def norm1(n):
                pool.wait_ge(stat1, n)
                own_wait(pool)
                link1(nc.gpsimd.tensor_scalar(rstd[:, :], mv[:, :, 1], EPS_LN, 1.0, ALU.add, ALU.mult), n)
                signal(pool, power(rstd[:, :], rstd[:, :], 2), rstd1, n)

            def kq(n):
                pool.wait_ge(kq_var, n)
                own_wait(pool)
                nc.gpsimd.tensor_scalar(rs[:, 0:2 * KH], var[:, 0:2 * KH], 1.0 / HD, EPS_RMS, ALU.mult, ALU.add)
                link1(nc.gpsimd.tensor_scalar(rs[:, 2 * KH:], var[:, 2 * KH:], 1.0 / D, EPS_RMS, ALU.mult, ALU.add), n)
                signal(pool, power(rs[:, :], rs[:, :], 2 * KH + 2), kq_rs, n)

            def gated(n):
                pool.wait_ge(g_sum, n)
                own_wait(pool)
                link1(nc.gpsimd.tensor_scalar(rs_g[:, :], sum_g[:, :], 0.25 / (2 * D), EPS_RMS, ALU.mult, ALU.add), n)
                link1(power(rs_g[:, :], rs_g[:, :], 2), n)
                own_wait(pool)
                signal(pool, nc.gpsimd.tensor_scalar(rs_g[:, :], rs_g[:, :], 0.5, 0.0, ALU.mult, ALU.add), g_rs, n)

            def norm2(n):
                pool.wait_ge(stat2, n)
                own_wait(pool)
                link1(nc.gpsimd.tensor_scalar(n2_a[:, :], mv[:, :, 1], EPS_LN, 1.0, ALU.add, ALU.mult), n)
                link1(power(rstd[:, :], n2_a[:, :], 2), n)
                link1(nc.gpsimd.tensor_tensor(n2_a[:, :], rstd[:, :], rstd[:, :], ALU.mult), n)
                link1(nc.gpsimd.tensor_tensor(n2_a[:, :], n2_a[:, :], mv[:, :, 1], ALU.mult), n)
                own_wait(pool)
                link1(nc.gpsimd.tensor_scalar(n2_a[:, :], n2_a[:, :], EPS_RMS, 1.0, ALU.add, ALU.mult), n)
                link1(power(n2_b[:, :], n2_a[:, :], 2), n)
                signal(pool, nc.gpsimd.tensor_tensor(rstd[:, :], rstd[:, :], n2_b[:, :], ALU.mult), norm2_s, n)

            def ffn_norm(n):
                pool.wait_ge(yf_sum, n)
                link1(nc.gpsimd.tensor_tensor(f_a[:, :], sum_f[:, :], deq1[:, :], ALU.mult), n)
                link1(nc.gpsimd.tensor_tensor(f_a[:, :], f_a[:, :], deq1[:, :], ALU.mult), n)
                own_wait(pool)
                link1(nc.gpsimd.tensor_scalar(f_a[:, :], f_a[:, :], 1.0 / FH, EPS_RMS, ALU.mult, ALU.add), n)
                link1(power(f_b[:, :], f_a[:, :], 2), n)
                signal(pool, nc.gpsimd.tensor_tensor(f_b[:, :], f_b[:, :], deq1[:, :], ALU.mult), yf_s, n)

            def norm3(n):
                pool.wait_ge(stat3, n)
                own_wait(pool)
                link2(nc.gpsimd.tensor_scalar(rstd_c[:, :], mv_c[:, :, 1], EPS_LN, 1.0, ALU.add, ALU.mult), n)
                signal(pool, power(rstd_c[:, :], rstd_c[:, :], 2), rstd3, n)

            def mix_queries(n):
                pool.wait_ge(q_ready, n)
                for c in range(2):
                    last = nc.gpsimd.tensor_tensor(
                        qm[0:HW, c, :, :].rearrange("p t (g n) -> p t g n", n=NB),
                        qT[:, c, :].rearrange("p (t n) -> p t n", n=NB).unsqueeze(2).broadcast_to([HW, NT, KH, NB]),
                        mix_l[:, c, :].unsqueeze(1).unsqueeze(3).broadcast_to([HW, NT, KH, NB]), ALU.mult)
                signal(pool, last, qm_ready, n)

            def mix_weights(u):
                def step(n):
                    pool.wait_ge(rz_ready, n * SU + (u + 1 - SU))
                    if u >= 2:
                        pool.wait_ge(at_ps, n * SU + (u - 1 - SU))
                    own_wait(pool)
                    for t in range(2):
                        last = nc.gpsimd.tensor_scalar(wz[u % 2][0:SR, t, :], mix_w[0:SR, :], rz[:, u, t:t + 1], 0.0,
                                                       ALU.mult, ALU.add)
                    signal(pool, last, wz_ready, n, SU, u)
                return step

            def norm4(n):
                pool.wait_ge(stat4, n)
                own_wait(pool)
                link2(nc.gpsimd.tensor_scalar(rstd_c[:, :], mv_c[:, :, 1], EPS_LN, 1.0, ALU.add, ALU.mult), n)
                signal(pool, power(rstd_c[:, :], rstd_c[:, :], 2), rstd4, n)

            phases = {"norm1": norm1, "kq": kq, "gated": gated, "norm2": norm2, "ffn_norm": ffn_norm,
                      "norm3": norm3, "qkv": mix_queries, "norm4": norm4}
            for u in range(SU):
                phases[f"exp{u}"] = mix_weights(u)
            run(pool, phases)
            assert c1[0] == 4 * P1, ("P1", c1[0] / 4)
            assert c2[0] == 4 * P2, ("P2", c2[0] / 4)

        @block.scalar
        def _(act):
            link1, c1 = linked(act, a_first, A1)
            link2, c2 = linked(act, a_second, A2)
            activation = nc.scalar.activation

            def xT1_(n):
                act.wait_ge(xT1_ps, n)
                signal(act, activation(xT[:, :, :].rearrange("p a b -> p (a b)"), psum_a[0:HW, 0, 0:2 * L], ACT.Copy), xT1, n)

            def z(n):
                act.wait_ge(z_ps, n)
                for g in range(4):
                    activation(zc[:, g, :], psum_a[0:HW, 1 + g // 2, (g % 2) * L:(g % 2 + 1) * L], ACT.Identity,
                               bias=0.0, scale=conv_w[:, g, TAPS - 1:TAPS])
                activation(zs[:, :], psum_a[0:KH, 3, 0:L], ACT.Identity, bias=0.0, scale=conv_ws[:, TAPS - 1:TAPS])
                activation(gT[:, :], psum_a[0:KH, 3, L:2 * L], ACT.Copy)
                for j in range(2):
                    last = activation(gs[:, j, :, 64:112],
                                      psum_a[0:T, 0, j * SKIP:(j + 1) * SKIP].unsqueeze(1).broadcast_to([T, 6, SKIP]), ACT.Copy)
                signal(act, last, z_tap, n)

            def silu(n):
                act.wait_ge(zT_ps, n)
                activation(zk[:, :, :], psum_a[0:T, 1:3, 0:D + KH], ACT.Silu)
                signal(act, activation(zq[:, :, :], psum_a[0:T, 1:3, D + KH:CONV], ACT.Silu), silu_done, n)

            def kq(n):
                act.wait_ge(kq_var, n)
                link1(activation(sp_u[:, :], score[:, :, :].rearrange("p a b -> p (a b)"), ACT.Abs), n)
                signal(act, activation(sp_u[:, :], sp_u[:, :], ACT.Exp, scale=-1.0), exp_u, n)
                act.wait_ge(tanh_in, n)
                signal(act, activation(phi[:, :], phi[:, :], ACT.Tanh), tanh_out, n)
                act.wait_ge(gate_ps, n)
                activation(gate_t[:, 0, :], psum_a[0:T, 3, 0:2 * D], ACT.Tanh, scale=0.5)
                signal(act, activation(gate_t[:, 1, :], psum_a[0:T, 0, 0:2 * D], ACT.Tanh, scale=0.5), gate_done, n)

            def trig_(n):
                act.wait_ge(phi_ready, n)
                activation(sin_p[:, :, :].rearrange("p a b -> p (a b)"), phi[:, :], ACT.Sin)
                link1(activation(phi_abs[:, :], phi[:, :], ACT.Abs), n)
                signal(act, activation(cos_p[:, :, :].rearrange("p a b -> p (a b)"), phi_abs[:, :], ACT.Sin,
                                       bias=half_pi[0:T, :], scale=-1.0), trig, n)

            def gated(n):
                act.wait_ge(g_ready, n)
                activation(gate_t[:, 0, :], oc[:, 0, :], ACT.Square, accum_out=sum_g[:, 0:1])
                signal(act, activation(gate_t[:, 1, :], oc[:, 1, :], ACT.Square, accum_out=sum_g[:, 1:2]), g_sum, n)

            def gsT_(n):
                act.wait_ge(gsT_ps, n)
                signal(act, activation(gsT[:, :, :].rearrange("p (a b) n -> p a (b n)", b=2),
                                       psum_a[0:112, 0:3, 0:2 * L], ACT.Copy), gsT_ready, n)

            def y_silu_(n):
                for r in range(3):
                    act.wait_ge(y_ps, n * 3 + (r - 2))
                    if r == 2:
                        act.wait_ge(y_ready, n * 3 - 2)
                    k = 2 * (r % 2)
                    signal(act, activation(y_silu_t[:, r % 2, :, :], psum_a[0:HW, k:k + 2, L:2 * L], ACT.Silu),
                           y_silu, n, 3, r)

            def xqT_(n):
                act.wait_ge(xqT_ps, n)
                signal(act, activation(xqT[:, :, 0:T], psum_a[0:HW, 0, 0:200].bitcast(bf16)
                                       .rearrange("p (k t) -> p k t", k=4)[:, :, 0:T], ACT.Copy), xqT_ready, n)

            def f_silu(n):
                act.wait_ge(h_ps, n)
                activation(sg_f[:, 0, :], psum_a[0:T, 1, :], ACT.Silu, scale=deq1[:, 0:1])
                signal(act, activation(sg_f[:, 1, :], psum_a[0:T, 3, :], ACT.Silu, scale=deq1[:, 1:2]), sg_ready, n)

            def ffn_norm(n):
                act.wait_ge(yf_ready, n)
                link1(activation(y_junk[:, :], y_f[:, 0, :], ACT.Square, accum_out=sum_f[:, 0:1]), n)
                signal(act, activation(y_junk[:, :], y_f[:, 1, :], ACT.Square, accum_out=sum_f[:, 1:2]), yf_sum, n)

            def yqT_(n):
                act.wait_ge(yqT_ps, n)
                signal(act, activation(yqT[:, :, 0:T], psum_a[:, 0, 0:400].bitcast(bf16)
                                       .rearrange("p (k t) -> p k t", k=8)[:, :, 0:T], ACT.Copy), yqT_ready, n)

            def xT3_(n):
                act.wait_ge(xT3_ps, n)
                signal(act, activation(xT_c[:, :, :].rearrange("p a b -> p (a b)"), psum_c[0:HW, 0, 0:2 * L], ACT.Copy), xT3, n)

            def qkv(n):
                act.wait_ge(qkv_ps, n)
                signal(act, activation(qT[:, :, 0:L], psum_c[0:HW, 1, 0:2 * L].rearrange("p (a b) -> p a b", a=2),
                                       ACT.Copy, scale=HD ** -0.5), q_ready, n)
                signal(act, activation(kT[0:HW, :, :].rearrange("p a b -> p (a b)"), psum_c[0:HW, 2, 0:2 * L], ACT.Copy), k_ready, n)
                signal(act, activation(vp[:, :, :, 0:HD].rearrange("p a g d -> p (a g) d"),
                                       psum_c[0:T, 3, 0:2 * D].rearrange("p (h d) -> p h d", d=HD), ACT.Copy), v_ready, n)

            def exps(u):
                def step(n):
                    act.wait_ge(s_max, n * SU + (u + 1 - SU))
                    if u >= 2:
                        act.wait_ge(at_ps, n * SU + (u - 1 - SU))
                    for t in range(2):
                        last = activation(expo[u % 2][0:SR, t, :], psum_c[0:SR, u % 2, t * L:(t + 1) * L], ACT.Exp,
                                          bias=nmax[:, t, u:u + 1], accum_out=zsum[:, u, t:t + 1])
                    signal(act, last, exp_done, n, SU, u)
                return step

            def w_(n):
                act.wait_ge(w_ps, n)
                activation(wT[:, 0:2, :].rearrange("p a b -> p (a b)"), psum_c[:, 0, 0:2 * NPAD], ACT.Copy)
                signal(act, activation(wT[:, 2, :], psum_c[:, 1, 0:NPAD], ACT.Copy), w_ready, n)

            def wp_(n):
                act.wait_ge(wT_ps, n)
                signal(act, activation(wp[:, :, :], psum_c[0:T, 2:4, 0:384], ACT.Copy), wp_ready, n)

            def xT4_(n):
                act.wait_ge(xT4_ps, n)
                signal(act, activation(xT_c[:, :, :].rearrange("p a b -> p (a b)"), psum_c[0:HW, 0, 0:2 * L], ACT.Copy), xT4, n)

            def route(n):
                act.wait_ge(lmax_ready, n)
                signal(act, activation(lexp[:, :], psum_c[0:T, 1, 0:NE], ACT.Exp, bias=lmax[:, 1:2], scale=1.0 / L,
                                       accum_out=lsum[:, :]), lexp_ready, n)

            def hidden(n):
                act.wait_ge(expert_loaded, n * 64)
                for r in range(3):
                    act.wait_ge(hid_ps, n * 3 + (r - 2))
                    for k in range(2):
                        last = activation(hT[:, 2 * r + k, :], psum_c[:, r, k * L:(k + 1) * L], ACT.Gelu,
                                          bias=e_b1[:, 2 * r + k:2 * r + k + 1])
                signal(act, last, hid_ready, n)

            phases = {"xT1": xT1_, "z": z, "zT": silu, "kq": kq, "trig": trig_, "gated": gated, "gsT": gsT_,
                      "y": y_silu_, "xqT": xqT_, "hid1": f_silu, "ffn_norm": ffn_norm, "yqT": yqT_,
                      "xT3": xT3_, "qkv": qkv, "w": w_, "wp": wp_, "xT4": xT4_, "route": route, "hidden": hidden}
            for u in range(SU):
                phases[f"exp{u}"] = exps(u)
            run(act, phases)
            assert c1[0] == 4 * A1, ("A1", c1[0] / 4)

        @block.tensor
        def _(pe):
            matmul, transpose = nc.tensor.matmul, nc.tensor.transpose

            def halves_T(src, bank):
                for c in range(2):
                    for j in range(2):
                        last = transpose(bank[0:HW, c * L + j * T:c * L + (j + 1) * T],
                                         src[:, j, c * HW:(c + 1) * HW], ident[0:T, 0:T])
                return last

            def xT1_(n):
                pe.wait_ge(xn1, n)
                halves_T(xn, psum_a[:, 0, :]).then_inc(xT1_ps, 1)

            def z(n):
                pe.wait_ge(xT1, n)

                def channels(o_, c0, width):
                    for c in range(2):
                        matmul(o_, w_in[:, c, c0:c0 + width], xT[:, c, :], start=(c == 0), stop=(c == 1))
                for g, c0 in enumerate((0, HW, D + KH, D + KH + HW)):
                    channels(psum_a[0:HW, 1 + g // 2, (g % 2) * L:(g % 2 + 1) * L], c0, HW)
                channels(psum_a[0:KH, 3, 0:L], D, KH)
                channels(psum_a[0:KH, 3, L:2 * L], CONV + SKIP, KH)
                for j in range(2):
                    for c in range(2):
                        last = matmul(psum_a[0:T, 0, j * SKIP:(j + 1) * SKIP], xT[:, c, j * T:(j + 1) * T],
                                      w_in[:, c, CONV:CONV + SKIP], start=(c == 0), stop=(c == 1))
                last.then_inc(z_ps, 1)

            def zT(n):
                pe.wait_ge(conv_done, n)
                for j in range(2):
                    t = slice(j * T, (j + 1) * T)
                    for src, rows, c0 in ((zc[:, 0, t], HW, 0), (zc[:, 1, t], HW, HW), (zs[:, t], KH, D),
                                          (zc[:, 2, t], HW, D + KH), (zc[:, 3, t], HW, D + KH + HW)):
                        last = transpose(psum_a[0:T, 1 + j, c0:c0 + rows], src, ident[0:rows, 0:rows])
                last.then_inc(zT_ps, 1)
                for j in range(2):
                    last = matmul(psum_a[0:T, 3 * (1 - j), 0:2 * D], gT[:, j * T:(j + 1) * T], w_gate[:, :],
                                  start=True, stop=True)
                last.then_inc(gate_ps, 1)

            def cum(n):
                pe.wait_ge(stack_ready, n)
                matmul(psum_a[0:T, 1, 0:CONV], upper[:, :], stack[:, 0, :], start=True, stop=True)
                matmul(psum_a[0:T, 2, 0:CONV], ones[0:T, 0:T], stack[:, 0, :], start=True, stop=False)
                matmul(psum_a[0:T, 2, 0:CONV], upper[:, :], stack[:, 1, :], start=False, stop=True).then_inc(cum_ps, 1)

            def gsT_(n):
                pe.wait_ge(gs_ready, n)
                for p in range(6):
                    for j in range(2):
                        c0 = (p % 2) * L + j * T
                        last = transpose(psum_a[0:112, p // 2, c0:c0 + T], gs[:, j, p, :], ident[0:T, 0:T])
                last.then_inc(gsT_ps, 1)

            def y(n):
                pe.wait_ge(gsT_ready, n)
                for r in range(3):
                    if r == 2:
                        pe.wait_ge(y_ready, n * 3 - 2)
                    for k in range(2):
                        p = 2 * r + k
                        for half in range(2):
                            last = matmul(psum_a[0:HW, 2 * (r % 2) + k, half * L:(half + 1) * L],
                                          w_read[:, p, half * HW:(half + 1) * HW], gsT[:, p, :], start=True, stop=True)
                    last.then_inc(y_ps, 1)
                pe.wait_ge(y_ready, n * 3)
                for j in range(2):
                    for p in range(6):
                        last = matmul(psum_a[0:T, 2, j * D:(j + 1) * D], yT[:, p, j * T:(j + 1) * T], w_out[:, p, :],
                                      start=(p == 0), stop=(p == 5))
                last.then_inc(out1_ps, 1)

            def xqT_(n):
                pe.wait_ge(xq_ready, n)
                bank = psum_a[0:HW, 0, 0:200].bitcast(bf16)
                for c in range(2):
                    for j in range(2):
                        c0 = (2 * c + j) * 100
                        last = transpose(bank[:, c0:c0 + T], xqb[:, j, c * HW:(c + 1) * HW], ident_b[0:T, 0:T])
                last.then_inc(xqT_ps, 1)

            def hid1(n):
                pe.wait_ge(xqT_ready, n)
                for j, part, bank in ((0, 1, 1), (0, 0, 2), (1, 1, 3), (1, 0, 0)):
                    for c in range(2):
                        last = matmul(psum_a[0:T, bank, :], xqT[:, 2 * c + j, 0:T], fq1[:, c, part * FH:(part + 1) * FH],
                                      start=(c == 0), stop=(c == 1))
                last.then_inc(h_ps, 1)

            def yqT_(n):
                pe.wait_ge(yq_ready, n)
                bank = psum_a[:, 0, 0:400].bitcast(bf16)
                for c in range(4):
                    for j in range(2):
                        c0 = (2 * c + j) * 100
                        last = transpose(bank[:, c0:c0 + T], yqb[:, j, c * 128:(c + 1) * 128], ident_b[0:T, 0:T])
                last.then_inc(yqT_ps, 1)

            def out2(n):
                pe.wait_ge(yqT_ready, n)
                for j in range(2):
                    for c in range(4):
                        last = matmul(psum_a[0:T, 1, j * D:(j + 1) * D], yqT[:, 2 * c + j, 0:T], fq2[:, c, :],
                                      start=(c == 0), stop=(c == 3))
                last.then_inc(out2_ps, 1)

            def xT3_(n):
                pe.wait_ge(xn3, n)
                halves_T(xn_c, psum_c[:, 0, :]).then_inc(xT3_ps, 1)

            def qkv(n):
                pe.wait_ge(xT3, n)
                for bank, c0 in ((1, 0), (2, D)):
                    for half in range(2):
                        for c in range(2):
                            matmul(psum_c[0:HW, bank, half * L:(half + 1) * L],
                                   w_qkv[:, c, c0 + half * HW:c0 + (half + 1) * HW], xT_c[:, c, :],
                                   start=(c == 0), stop=(c == 1))
                for j in range(2):
                    for c in range(2):
                        last = matmul(psum_c[0:T, 3, j * D:(j + 1) * D], xT_c[:, c, j * T:(j + 1) * T],
                                      w_qkv[:, c, 2 * D:3 * D], start=(c == 0), stop=(c == 1))
                last.then_inc(qkv_ps, 1)

            def scores(u):
                def step(n):
                    if u == 0:
                        pe.wait_ge(pad_loaded, 80)
                        pe.wait_ge(k_ready, n)
                        pe.wait_ge(qm_ready, n)
                    if u >= 2:
                        pe.wait_ge(exp_done, n * SU + (u - 1 - SU))
                    for t in range(2):
                        o_ = psum_c[0:SR, u % 2, t * L:(t + 1) * L]
                        matmul(o_, qm[0:HW, 0, 2 * u + t, :], kT[0:HW, 0, :], start=True, stop=False)
                        last = matmul(o_, qm[:, 1, 2 * u + t, :], kT[:, 1, :], start=False, stop=True)
                    last.then_inc(s_ps, 1)
                return step

            def mixed(u):
                def step(n):
                    pe.wait_ge(exp_done, n * SU + (u + 1 - SU))
                    pe.wait_ge(wz_ready, n * SU + (u + 1 - SU))
                    if u >= 2:
                        pe.wait_ge(at_ready, n * SU + (u - 1 - SU))
                    for t in range(2):
                        for half in range(2):
                            c0 = (2 * t + half) * SR
                            last = matmul(psum_c[0:T, 2 + u % 2, c0:c0 + SR], expo[u % 2][:, t, half * T:(half + 1) * T],
                                          wz[u % 2][:, t, :], start=True, stop=True)
                    last.then_inc(at_ps, 1)
                return step

            def apply_attention(values):
                for g in range(KH):
                    r, q = g // 4, g % 4
                    for half in range(2):
                        last = matmul(psum_c[32 * q:32 * q + 32, r // 2, (r % 2) * NPAD:(r % 2 + 1) * NPAD],
                                      values[:, half, g, :], at[:, :, half, g * NB:(g + 1) * NB],
                                      start=(half == 0), stop=(half == 1))
                return last

            def w_(n):
                pe.wait_ge(at_ready, n * SU)
                pe.wait_ge(v_ready, n)
                apply_attention(vp).then_inc(w_ps, 1)

            def wp_(n):
                pe.wait_ge(w_ready, n)
                for j in range(2):
                    for r in range(3):
                        last = transpose(psum_c[0:T, 2 + j, r * 128:(r + 1) * 128], wT[:, r, j * T:(j + 1) * T], ident[:, :])
                last.then_inc(wT_ps, 1)

            def w2(n):
                pe.wait_ge(wp_ready, n)
                apply_attention(wp[:, :, :].rearrange("p a (g d) -> p a g d", d=32)).then_inc(w2_ps, 1)

            def proj(n):
                pe.wait_ge(o2_ready, n)
                for j in range(2):
                    for r in range(3):
                        last = matmul(psum_c[0:T, 2, j * D:(j + 1) * D], o2[:, r, j * T:(j + 1) * T], w_proj[:, r, :],
                                      start=(r == 0), stop=(r == 2))
                last.then_inc(proj_ps, 1)

            def xT4_(n):
                pe.wait_ge(xn4, n)
                halves_T(xn_c, psum_c[:, 0, :]).then_inc(xT4_ps, 1)

            def route(n):
                pe.wait_ge(xsum_ready, n)
                for c in range(2):
                    last = matmul(psum_c[0:T, 1, 0:NE], xsum[:, c:c + 1].broadcast_to([HW, T]), w_route[:, c, :],
                                  start=(c == 0), stop=(c == 1))
                last.then_inc(logit_ps, 1)

            def hidden(n):
                pe.wait_ge(expert_loaded, n * 64)
                pe.wait_ge(lexp_ready, n)
                for r in range(3):
                    for k in range(2):
                        f = 2 * r + k
                        for c in range(2):
                            last = matmul(psum_c[:, r, k * L:(k + 1) * L], e_w1[:, c, f * 128:(f + 1) * 128], xT_c[:, c, :],
                                          start=(c == 0), stop=(c == 1))
                    last.then_inc(hid_ps, 1)

            def ffn_out(n):
                pe.wait_ge(hid_ready, n)
                for j in range(2):
                    for f in range(6):
                        last = matmul(psum_c[0:T, 3, j * D:(j + 1) * D], hT[:, f, j * T:(j + 1) * T], e_w2[:, f, :],
                                      start=(f == 0), stop=(f == 5))
                last.then_inc(ffn_ps, 1)

            phases = {"xT1": xT1_, "z": z, "zT": zT, "cum": cum, "gsT": gsT_, "y": y, "xqT": xqT_, "hid1": hid1,
                      "yqT": yqT_, "out2": out2, "xT3": xT3_, "qkv": qkv, "w": w_, "wp": wp_, "w2": w2,
                      "proj": proj, "xT4": xT4_, "route": route, "hidden": hidden, "ffn_out": ffn_out}
            for u in range(SU):
                phases[f"score{u}"] = scores(u)
                phases[f"mixed{u}"] = mixed(u)
            run(pe, phases)

        @block.vector
        def _(dve):
            link1, c1 = linked(dve, v_first, V1)
            link2, c2 = linked(dve, v_second, V2)
            tt, ts, stt = nc.vector.tensor_tensor, nc.vector.tensor_scalar, nc.vector.scalar_tensor_tensor

            def heads(ap, width=HD):
                return ap.rearrange("p (h d) -> p h d", d=width)

            def flat(t):
                return t[:, :, :].rearrange("p a b -> p (a b)")

            def row_stats(h, stats_, mv_, link, n, ready):
                for j in range(2):
                    last = nc.vector.bn_stats(stats_[:, j, :], h[:, j, :])
                link(last, n)
                own_wait(dve)
                nc.vector.bn_aggr(mv_[:, 0, :], stats_[:, 0, :])
                signal(dve, nc.vector.bn_aggr(mv_[:, 1, :], stats_[:, 1, :]), ready, n)

            def normalise(out_, h, mv_, rstd_):
                for j in range(2):
                    last = ts(out_[:, j, :], h[:, j, :], mv_[:, j, 0:1], rstd_[:, j:j + 1], ALU.subtract, ALU.mult)
                return last

            def norm1(n):
                dve.wait_ge(x_loaded, n * 32)
                row_stats(x, stats, mv, link1, n, stat1)
                dve.wait_ge(rstd1, n)
                signal(dve, normalise(xn, x, mv, rstd), xn1, n)

            def conv(n):
                dve.wait_ge(z_tap, n)
                for s in range(1, TAPS):
                    w = TAPS - 1 - s
                    for g in range(4):
                        c0 = (g % 2) * L
                        stt(out=zc[:, g, s:L], in0=psum_a[0:HW, 1 + g // 2, c0:c0 + L - s], scalar=conv_w[:, g, w:w + 1],
                            in1=zc[:, g, s:L], op0=ALU.mult, op1=ALU.add)
                    last = stt(out=zs[:, s:L], in0=psum_a[0:KH, 3, 0:L - s], scalar=conv_ws[:, w:w + 1], in1=zs[:, s:L],
                               op0=ALU.mult, op1=ALU.add)
                    if s < TAPS - 1:
                        link1(last, n)
                signal(dve, last, conv_done, n)

            def kq(n):
                dve.wait_ge(silu_done, n)
                tt(score[:, :, :], zk[:, :, D:D + KH], score_w[:, :].rearrange("p (a b) -> p a b", a=2), ALU.mult)
                link1(tt(sq[:, :, :], zk[:, :, 0:D], zk[:, :, 0:D], ALU.mult), n)
                tt(score[:, :, :], score[:, :, :], score_b[:, :].rearrange("p (a b) -> p a b", a=2), ALU.add)
                link1(nc.vector.reduce_sum(var[:, 0:2 * KH], heads(flat(sq)), axis=AX.X), n)
                link1(tt(sq[:, :, :], zq[:, :, :], zq[:, :, :], ALU.mult), n)
                signal(dve, nc.vector.reduce_sum(var[:, 2 * KH:], sq[:, :, :], axis=AX.X), kq_var, n)
                for c, q in ((0, qx_re), (1, qx_im)):
                    src = flat(zq).rearrange("p (q h c) -> p q h c", h=HD, c=2)[:, :, :, c]
                    tt(q[:, :].rearrange("p (q r h) -> p q r h", r=2, h=HD),
                       src.unsqueeze(2).broadcast_to([T, 2 * NQ, 2, HD]),
                       q_w[:, c, :].rearrange("p (q r h) -> p q r h", r=2, h=HD), ALU.mult)
                dve.wait_ge(kq_rs, n)
                link1(tt(kv[:, :, :].rearrange("p a (k h) -> p a k h", h=HD),
                         zk[:, :, 0:D].rearrange("p a (k h) -> p a k h", h=HD),
                         rs[:, 0:2 * KH].rearrange("p (a k) -> p a k", a=2).unsqueeze(3).broadcast_to([T, 2, KH, HD]),
                         ALU.mult), n)
                link1(tt(flat(kv), flat(kv), k_norm[:, :], ALU.mult), n)
                signal(dve, tt(phi[:, :], flat(kv), tanh_scale[:, :], ALU.mult), tanh_in, n)
                dve.wait_ge(exp_u, n)
                link1(ts(sp_p[:, :], sp_u[:, :], 2.0, None, ALU.add), n)
                link1(nc.vector.reciprocal(sp_p[:, :], sp_p[:, :]), n)
                link1(tt(sp_z[:, :], sp_u[:, :], sp_p[:, :], ALU.mult), n)
                link1(tt(sp_z2[:, :], sp_z[:, :], sp_z[:, :], ALU.mult), n)
                link1(ts(sp_p[:, :], sp_z2[:, :], 2.0 / (2 * LOG1P_TERMS - 1), None, ALU.mult), n)
                dve.wait_ge(tanh_out, n)
                signal(dve, tt(phi[:, :], phi[:, :], theta[:, :], ALU.mult), phi_ready, n)
                for k in range(LOG1P_TERMS - 2, 0, -1):
                    link1(stt(out=sp_p[:, :], in0=sp_p[:, :], scalar=2.0 / (2 * k + 1), in1=sp_z2[:, :],
                              op0=ALU.add, op1=ALU.mult), n)
                link1(stt(out=sp_p[:, :], in0=sp_p[:, :], scalar=2.0, in1=sp_z[:, :], op0=ALU.add, op1=ALU.mult), n)
                link1(stt(out=sp_p[:, :], in0=flat(score), scalar=0.0, in1=sp_p[:, :], op0=ALU.max, op1=ALU.add), n)
                link1(tt(sp_p[:, :], sp_p[:, :], time_w[:, :], ALU.mult), n)
                p_w = stack[:, :, 2 * D:2 * D + KH]
                link1(ts(p_w, sp_p[:, :].rearrange("p (a k) -> p a k", a=2), 1e-6, 1000.0, ALU.max, ALU.min), n)
                link1(tt(kvw[:, :, :].rearrange("p a (k h) -> p a k h", h=HD),
                         kv[:, :, :].rearrange("p a (k h) -> p a k h", h=HD),
                         p_w.unsqueeze(3).broadcast_to([T, 2, KH, HD]), ALU.mult), n)

            def trig_(n):
                dve.wait_ge(trig, n)
                tt(stack[:, :, 0:D], kvw[:, :, :], cos_p[:, :, :], ALU.mult)
                signal(dve, tt(stack[:, :, D:2 * D], kvw[:, :, :], sin_p[:, :, :], ALU.mult), stack_ready, n)

            def match(n):
                dve.wait_ge(cum_ps, n)
                link1(ts(den[:, :, :], psum_a[0:T, 1:3, 2 * D:2 * D + KH], 1e-4, None, ALU.max), n)
                link1(nc.vector.reciprocal(den[:, :, :], den[:, :, :]), n)
                link1(tt(den[:, :, :], den[:, :, :],
                         rs[:, 2 * KH:].unsqueeze(2).broadcast_to([T, 2, KH]), ALU.mult), n)
                for c, s in ((0, s_re), (1, s_im)):
                    last = tt(s[:, :].rearrange("p (a k h) -> p a k h", a=2, h=HD),
                              psum_a[0:T, 1:3, c * D:(c + 1) * D].rearrange("p a (k h) -> p a k h", h=HD),
                              den[:, :, :].unsqueeze(3).broadcast_to([T, 2, KH, HD]), ALU.mult)
                link1(last, n)
                oc_h = flat(oc).rearrange("p (k c h) -> p k c h", c=2, h=HD)
                tt(m_a[:, :], s_re[:, :], qx_re[:, :], ALU.mult)
                link1(tt(m_b[:, :], s_im[:, :], qx_im[:, :], ALU.mult), n)
                link1(tt(oc_h[:, :, 0, :], heads(m_a[:, :]), heads(m_b[:, :]), ALU.add), n)
                tt(m_a[:, :], s_im[:, :], qx_re[:, :], ALU.mult)
                link1(tt(m_b[:, :], s_re[:, :], qx_im[:, :], ALU.mult), n)
                link1(tt(oc_h[:, :, 1, :], heads(m_a[:, :]), heads(m_b[:, :]), ALU.subtract), n)
                dve.wait_ge(gate_done, n)
                signal(dve, stt(out=flat(oc), in0=flat(gate_t), scalar=1.0, in1=flat(oc), op0=ALU.add, op1=ALU.mult),
                       g_ready, n)

            def gated(n):
                dve.wait_ge(g_rs, n)
                for j in range(2):
                    last = ts(gs[:, j, :, 0:64], oc[:, j, :].rearrange("p (q c) -> p q c", c=64), rs_g[:, j:j + 1], None,
                              ALU.mult)
                signal(dve, last, gs_ready, n)

            def y(n):
                for r in range(3):
                    dve.wait_ge(y_silu, n * 3 + (r - 2))
                    k = 2 * (r % 2)
                    signal(dve, tt(yT[:, 2 * r:2 * r + 2, :], psum_a[0:HW, k:k + 2, 0:L], y_silu_t[:, r % 2, :, :], ALU.mult),
                           y_ready, n, 3, r)

            def h1_(n):
                dve.wait_ge(out1_ps, n)
                signal(dve, tt(flat(h1), psum_a[0:T, 2, 0:2 * D], flat(x), ALU.add), h1_ready, n)

            def quantise(src, out_, w, deq, n):
                link1(nc.vector.tensor_reduce(amax[:, :], src, axis=AX.X, op=ALU.max, apply_absolute_value=True), n)
                link1(ts(amax[:, :], amax[:, :], EPS_Q, None, ALU.max), n)
                ts(deq[:, :], amax[:, :], 1.0 / 127.0, w_mean[0:T, w:w + 1], ALU.mult, ALU.mult)
                link1(nc.vector.reciprocal(qscale[:, :], amax[:, :]), n)
                link1(ts(qscale[:, :], qscale[:, :], 127.0, None, ALU.mult), n)
                for j in range(2):
                    last = ts(src[:, j, :], src[:, j, :], qscale[:, j:j + 1], MAGIC, ALU.mult, ALU.add)
                link1(last, n)
                return ts(out_, src, MAGIC, None, ALU.subtract)

            def norm2(n):
                row_stats(h1, stats, mv, link1, n, stat2)
                dve.wait_ge(norm2_s, n)
                link1(normalise(xn, h1, mv, rstd), n)
                link1(tt(flat(xn), flat(xn), g_in[:, :], ALU.mult), n)
                signal(dve, quantise(xn[:, :, :], xqb[:, :, :], 0, deq1, n), xq_ready, n)

            def hid1(n):
                dve.wait_ge(sg_ready, n)
                tt(y_f[:, 0, :], psum_a[0:T, 2, :], sg_f[:, 0, :], ALU.mult)
                signal(dve, tt(y_f[:, 1, :], psum_a[0:T, 0, :], sg_f[:, 1, :], ALU.mult), yf_ready, n)

            def ffn_norm(n):
                dve.wait_ge(yf_s, n)
                for j in range(2):
                    last = stt(out=y_f[:, j, :], in0=y_f[:, j, :], scalar=f_b[:, j:j + 1], in1=g_out[:, :],
                               op0=ALU.mult, op1=ALU.mult)
                link1(last, n)
                signal(dve, quantise(y_f[:, :, :], yqb[:, :, :], 1, deq2, n), yq_ready, n)

            def out2(n):
                dve.wait_ge(out2_ps, n)
                for j in range(2):
                    last = stt(out=h2[:, j, :], in0=psum_a[0:T, 1, j * D:(j + 1) * D], scalar=deq2[:, j:j + 1],
                               in1=h1[:, j, :], op0=ALU.mult, op1=ALU.add)
                signal(dve, last, h2_ready, n)

            def norm3(n):
                dve.wait_ge(h2_ready, n)
                link2(nc.vector.tensor_copy(flat(h3), flat(h2)), n)
                row_stats(h3, stats_c, mv_c, link2, n, stat3)
                dve.wait_ge(rstd3, n)
                signal(dve, normalise(xn_c, h3, mv_c, rstd_c), xn3, n)

            def score_max(u):
                def step(n):
                    dve.wait_ge(s_ps, n * SU + (u + 1 - SU))
                    signal(dve, nc.vector.tensor_reduce(nmax[:, :, u], psum_c[0:SR, u % 2, 0:2 * L]
                                                        .rearrange("p (t m) -> p t m", t=2),
                                                        axis=AX.X, op=ALU.max, negate=True), s_max, n, SU, u)
                return step

            def denominators(u):
                def step(n):
                    dve.wait_ge(exp_done, n * SU + (u + 1 - SU))
                    signal(dve, nc.vector.reciprocal(rz[:, u, :], zsum[:, u, :]), rz_ready, n, SU, u)
                return step

            def keep_mixed(u):
                def step(n):
                    dve.wait_ge(at_ps, n * SU + (u + 1 - SU))
                    signal(dve, nc.vector.tensor_copy(at[:, 2 * u:2 * u + 2, :, :].rearrange("p t a n -> p (t a n)"),
                                                      psum_c[0:T, 2 + u % 2, 0:4 * SR]), at_ready, n, SU, u)
                return step

            def w2(n):
                dve.wait_ge(w_ready, n)
                for r in range(3):
                    last = ts(o2[:, r, :], wT[:, r, :], lam_1[:, r:r + 1], None, ALU.mult)
                link2(last, n)
                dve.wait_ge(w2_ps, n)
                for r in range(3):
                    last = stt(out=o2[:, r, :], in0=psum_c[:, r // 2, (r % 2) * NPAD:(r % 2 + 1) * NPAD],
                               scalar=lam_2[:, r:r + 1], in1=o2[:, r, :], op0=ALU.mult, op1=ALU.add)
                signal(dve, last, o2_ready, n)

            def norm4(n):
                dve.wait_ge(proj_ps, n)
                link2(tt(flat(h4), psum_c[0:T, 2, 0:2 * D], flat(h3), ALU.add), n)
                link2(tt(flat(h4), flat(h4), b_proj[:, :], ALU.add), n)
                row_stats(h4, stats_c, mv_c, link2, n, stat4)
                dve.wait_ge(rstd4, n)
                signal(dve, normalise(xn_c, h4, mv_c, rstd_c), xn4, n)

            def route(n):
                dve.wait_ge(xT4, n)
                signal(dve, nc.vector.reduce_sum(xsum[:, :], xT_c[:, :, :], axis=AX.X), xsum_ready, n)
                dve.wait_ge(logit_ps, n)
                link2(nc.vector.reduce_max(lmax[:, 0:1], psum_c[0:T, 1, 0:NE], axis=AX.X), n)
                link2(ts(sel_f[:, 0:2], psum_c[0:1, 1, 0:2], lmax[0:1, 0:1], None, ALU.is_ge), n)
                signal(dve, ts(lmax[:, 1:2], lmax[:, 0:1], -1.0 / L, None, ALU.mult), lmax_ready, n)
                ts(sel_f[:, 2:3], sel_f[:, 0:1], -1.0, 1.0, ALU.mult, ALU.add)
                link2(ts(sel_f[:, 3:4], sel_f[:, 1:2], -1.0, 2.0, ALU.mult, ALU.add), n)
                signal(dve, tt(sel[:, :], sel_f[:, 2:3], sel_f[:, 3:4], ALU.mult), sel_ready, n)
                dve.wait_ge(lexp_ready, n)
                link2(nc.vector.reciprocal(route_w[:, :], lsum[:, :]), n)

            def ffn_out(n):
                dve.wait_ge(ffn_ps, n)
                dve.wait_ge(expert_loaded, n * 64)
                if not (isinstance(n, int) and n == 1):
                    dve.wait_ge(o_stored, n * 32 - 32)
                link2(tt(flat(o), psum_c[0:T, 3, 0:2 * D], e_b2[:, :], ALU.add), n)
                signal(dve, stt(out=flat(o), in0=flat(o), scalar=route_w[:, :], in1=flat(h4), op0=ALU.mult, op1=ALU.add),
                       o_ready, n)

            phases = {"norm1": norm1, "conv": conv, "kq": kq, "trig": trig_, "match": match, "gated": gated, "y": y,
                      "h1": h1_, "norm2": norm2, "hid1": hid1, "ffn_norm": ffn_norm, "out2": out2, "norm3": norm3,
                      "w2": w2, "norm4": norm4, "route": route, "ffn_out": ffn_out}
            for u in range(SU):
                phases[f"score{u}"] = score_max(u)
                phases[f"exp{u}"] = denominators(u)
                phases[f"mixed{u}"] = keep_mixed(u)
            run(dve, phases)
            assert c1[0] == 4 * V1, ("V1", c1[0] / 4)
            assert c2[0] == 4 * V2, ("V2", c2[0] / 4)


FIRST = ["norm1", "xT1", "z", "conv", "zT", "kq", "trig", "cum", "match", "gated", "gsT", "y", "h1",
         "norm2", "xqT", "hid1", "ffn_norm", "yqT", "out2"]
SECOND = (["norm3", "xT3", "qkv", "score0"]
          + [p for u in range(1, NT // 2) for p in (f"score{u}", f"exp{u - 1}", f"mixed{u - 1}")]
          + [f"exp{NT // 2 - 1}", f"mixed{NT // 2 - 1}", "w", "wp", "w2", "proj", "norm4", "xT4", "route",
             "hidden", "ffn_out"])
ORDER = [(2, p) for p in SECOND] + [(1, p) for p in FIRST]


def layout(x):
    import numpy as np

    def arr(name):
        return np.asarray(x[name])

    def rows(v, n=T):
        return np.broadcast_to(v.reshape(1, -1), (n, v.size))

    def twice(v):
        return rows(np.concatenate([v.reshape(-1)] * 2))

    def part(w, p):
        return w.reshape(w.shape[0] // p, p, w.shape[1]).transpose(1, 0, 2)

    d = {}
    px = arr("x").reshape(B, C, NH, PS, NH, PS).transpose(2, 4, 3, 5, 1, 0)
    px = px.reshape(NG, PP, 2, 128, C, B).transpose(0, 3, 1, 4, 2, 5).reshape(NG, 128, PP * C * 2 * B)
    mw = arr("L0_tok_merge_weights")
    mws = np.broadcast_to(mw.reshape(NG, 1, PP * C), (NG, 128, PP * C))
    d["pixels"] = np.concatenate([px, mws], axis=2)
    dw = arr("L0_tok_decode_weights").reshape(NG, PP, D, 2, 128)
    d["dec_w"] = dw.transpose(0, 4, 1, 3, 2).reshape(NG, 128, PP * 2 * D)
    one = np.ones((1, NP_), np.float32)
    stat = np.concatenate([mw.T, arr("L0_tok_merge_biases").reshape(1, NP_), one])
    stat = np.broadcast_to(stat[:, :, None], (5, NP_, B)).reshape(5, NG, PP * B)
    d["bias_s"] = stat.transpose(1, 0, 2)
    db = arr("L0_tok_decode_biases")
    mov = np.stack([db, db, db, np.ones((NP_, D), np.float32), arr("L0_tok_pos_embedding")[1:]])
    d["bias_m"] = mov.reshape(5, NG, PP * D).transpose(1, 0, 2)
    cls = np.stack([arr("cls_tok").reshape(D), arr("L0_tok_cls_embedding"), arr("L0_tok_pos_embedding")[0]])
    d["cls"] = np.broadcast_to(cls[None], (B, 3, D))
    d["W_in"] = part(arr("L0_attn_W_in"), HW)
    cw = arr("L0_attn_conv_w").T
    q0 = KH * HD + KH
    d["conv_w"] = np.stack([cw[0:HW], cw[HW:2 * HW], cw[q0:q0 + HW], cw[q0 + HW:q0 + 2 * HW]], axis=1)
    d["conv_ws"] = cw[KH * HD:q0]
    d["k_norm"] = twice(np.broadcast_to(arr("L0_attn_k_norm_w"), (KH, HD)))
    d["tanh_scale"] = twice(np.broadcast_to(arr("L0_attn_tanh_scale")[:, None], (KH, HD)))
    d["theta"] = twice(arr("L0_attn_theta_raw"))
    qn = arr("L0_attn_q_norm_w").reshape(NQ, 1, HD, 2)
    qn = np.broadcast_to(qn, (NQ, 2, HD, 2)).transpose(3, 0, 1, 2)
    wi = np.broadcast_to(arr("L0_attn_w_int_raw").reshape(1, D), (2, D))
    d["q_norm"] = rows(np.concatenate([qn[0].reshape(-1)] * 2 + [qn[1].reshape(-1)] * 2)).reshape(T, 2, 2 * D)
    d["w_int"] = rows(np.concatenate([wi[0]] * 4)).reshape(T, 2, 2 * D)
    d["score_w"] = twice(arr("L0_attn_score_scale"))
    d["score_b"] = twice(arr("L0_attn_score_bias"))
    d["decay"] = twice(arr("L0_attn_decay_slopes"))
    left = np.arange(L - 1, -1, -1, dtype=np.float32).reshape(2, T).T
    d["dist"] = np.repeat(left, KH, axis=1)
    d["W_gate"] = arr("L0_attn_W_gate")
    ro, sk = arr("L0_attn_W_readout"), arr("L0_attn_W_skip")
    gn, hs = arr("L0_attn_gnorm_w").reshape(KH, 2 * HD), arr("L0_attn_highway_scale")
    wr = np.zeros((112, 6, 2 * HW), np.float32)
    wf = np.ones((112, 6, 2 * HW), np.float32)
    for k in range(KH):
        p, e = k // 2, k % 2
        for half in range(2):
            c0, s0 = half * HW + e * FS, half * FS
            wr[32 * e:32 * e + 32, p, c0:c0 + FS] = ro[k, :, s0:s0 + FS]
            wf[32 * e:32 * e + 32, p, c0:c0 + FS] = gn[k][:, None]
            wr[64:112, p, c0:c0 + FS] = sk[:, k * HW + s0:k * HW + s0 + FS]
            wf[64:112, p, c0:c0 + FS] = hs[k]
    d["W_read"], d["W_read_f"] = wr, wf
    d["W_out"] = part(arr("L0_attn_W_out"), HW)
    d["ffn_w1"] = part(arr("L0_ffn_w_in").T, HW)
    d["ffn_w2"] = part(arr("L0_ffn_w_out").T, 128)
    d["g_in"] = twice(arr("L0_ffn_g_in"))
    d["g_out"] = rows(arr("L0_ffn_g_out"))
    d["W_qkv"] = part(arr("L1_attn_W_qkv"), HW)
    d["mix_l"] = part(np.repeat(arr("L1_attn_W_l"), HD, axis=0), HW)
    mw2 = np.zeros((SR + 1, KH, NB), np.float32)
    for n in range(NB):
        mw2[n:SR:NB, :, n] = arr("L1_attn_W_w")
    mw2[SR] = arr("L1_attn_b_w")[:, None]
    d["mix_w"] = mw2.reshape(SR + 1, SR)
    d["b_l"] = np.tile(np.repeat(arr("L1_attn_b_l"), NB), NT).reshape(1, NT * SR)
    d["lam"] = np.repeat(arr("L1_attn_lamb").reshape(3, 4), 32, axis=1).T
    wp = np.zeros((3, 4, 32, D), np.float32)
    wp[:, :, 0:HD, :] = arr("L1_attn_W_proj").reshape(3, 4, HD, D)
    d["W_proj"] = wp.reshape(3, 128, D).transpose(1, 0, 2)
    d["b_proj"] = twice(arr("L1_attn_b_proj"))
    d["W_route"] = part(arr("L1_ffn_Wg").T, HW)
    d["W1"] = arr("L1_ffn_W1").reshape(NE, 2, HW, FM).transpose(0, 2, 1, 3).reshape(NE, HW, 2 * FM)
    d["W2"] = arr("L1_ffn_W2").reshape(NE, 6, 128, D).transpose(0, 2, 1, 3).reshape(NE, 128, 6 * D)
    d["b1"] = arr("L1_ffn_b1").reshape(NE, 6, 128).transpose(0, 2, 1)
    b2 = arr("L1_ffn_b2")
    d["b2"] = np.broadcast_to(np.concatenate([b2, b2], axis=1)[:, None, :], (NE, T, 2 * D))
    d["upper"] = np.triu(np.ones((T, T), np.float32))
    d["ident"] = np.eye(128, dtype=np.float32)
    return {k: np.ascontiguousarray(v) for k, v in d.items()}


def kernel(**inputs):
    import concourse.bacc as _bacc
    from concourse.bass_utils import run_bass_kernel_spmd as _run

    arrays = {f"in_{k}": v for k, v in layout(inputs).items()}
    nc = _bacc.Bacc("TRN2", target_bir_lowering=False, num_devices=1)
    a = {k[3:]: nc.dram_tensor(k, v.shape, mybir.dt.from_np(v.dtype), kind="ExternalInput").ap()
         for k, v in arrays.items()}
    out = nc.dram_tensor("out_tokens", (B, L, D), mybir.dt.float32, kind="ExternalOutput").ap()
    vit_program(nc, a, out)
    r = _run(nc, [arrays], core_ids=[0])
    return r.results[0]["out_tokens"]
```

```python
import concourse.bass as bass
from concourse import mybir
from contextlib import ExitStack

B, C, IMG, PS = 64, 3, 224, 16
NH = IMG // PS
NP_ = NH * NH
L = NP_ + 2
D = 192
T = L // 2
HW = 96
KH, HD = 12, 16
NQ = 6
TAPS = 4
CONV = KH * HD + KH + NQ * HD * 2
SKIP = D // 4
FS = 48
FH = 512
FM = 768
NE = 3
PP = 7
NG = NP_ // PP
PD = PS * PS
NB = 10
NT = 20
NPAD = NB * NT
QT = 4
SR = KH * NB
EPS_LN = 1e-5
EPS_RMS = 1e-6
EPS_Q = 1e-5
MAGIC = 12582912.0
THETA_MIN, THETA_MAX = 0.001, 3.0
LOG1P_TERMS = 7


def vit_program(nc, a, out, images=B):
    f32, bf16, i32 = mybir.dt.float32, mybir.dt.bfloat16, mybir.dt.int32
    ALU, ACT, AX = mybir.AluOpType, mybir.ActivationFunctionType, mybir.AxisListType

    h_dram = nc.dram_tensor("h_tokens", (B, L, D), f32, kind="Internal").ap()

    ctx = ExitStack()
    with ctx:
        def sb(name, shape, dt=f32):
            return ctx.enter_context(nc.sbuf_tensor(name, list(shape), dt))

        def sems(names):
            return [ctx.enter_context(nc.semaphore(n)) for n in names.split()]

        ident = sb("ident", (128, 128))
        ident_b = sb("ident_b", (128, 128), bf16)
        upper = sb("upper", (T, T))
        ones = sb("ones", (128, 128))
        half_pi = sb("half_pi", (128, 1))
        neg_half = sb("neg_half", (128, 32))
        w_in = sb("w_in", (HW, 2, CONV + SKIP + KH))
        conv_w = sb("conv_w", (HW, 4, TAPS))
        conv_ws = sb("conv_ws", (KH, TAPS))
        k_norm = sb("k_norm", (T, 2 * D))
        tanh_scale = sb("tanh_scale", (T, 2 * D))
        theta = sb("theta", (T, 2 * D))
        q_w = sb("q_w", (T, 2, 2 * D))
        score_w = sb("score_w", (T, 2 * KH))
        score_b = sb("score_b", (T, 2 * KH))
        time_w = sb("time_w", (T, 2 * KH))
        dist = sb("dist", (T, 2 * KH))
        w_gate = sb("w_gate", (KH, 2 * D))
        w_read = sb("w_read", (112, 6, 2 * HW))
        w_out = sb("w_out", (HW, 6, D))
        fq1 = sb("fq1", (HW, 2, 2 * FH), bf16)
        fq2 = sb("fq2", (128, 4, D), bf16)
        g_in = sb("g_in", (T, 2 * D))
        g_out = sb("g_out", (T, FH))
        w_mean = sb("w_mean", (128, 2))
        w_abs = sb("w_abs", (128, 2))
        w_qkv = sb("w_qkv", (HW, 2, 3 * D))
        mix_l = sb("mix_l", (HW, 2, KH))
        mix_w = sb("mix_w", (SR + 1, SR))
        lam = sb("lam", (128, 3))
        lam_1 = sb("lam_1", (128, 3))
        lam_2 = sb("lam_2", (128, 3))
        w_proj = sb("w_proj", (128, 3, D))
        b_proj = sb("b_proj", (T, 2 * D))
        w_route = sb("w_route", (HW, 2, NE))

        psum = ctx.enter_context(nc.psum_tensor("psum", [128, 8, 512], f32))
        psum_a, psum_c, psum_z = psum[:, 0:3, :], psum[:, 3:6, :], psum[:, 6:8, :]

        (const_loaded, const_memset, ident_ready, setup_v, setup_a, setup_pe, setup_done_v,
         setup_done_a) = sems("const_loaded const_memset ident_ready setup_v setup_a setup_pe setup_done_v setup_done_a")

        with ExitStack() as tmp:
            def sbt(name, shape, dt=f32):
                return tmp.enter_context(nc.sbuf_tensor("init_" + name, list(shape), dt))
            w_read_f = sbt("w_read_f", (112, 6, 2 * HW))
            wf1 = sbt("wf1", (HW, 2, 2 * FH))
            wf2 = sbt("wf2", (128, 4, D))
            q_int = sbt("q_int", (T, 2, 2 * D))
            decay = sbt("decay", (T, 2 * KH))
            sp_u = sbt("sp_u", (T, 2 * KH))
            sp_z = sbt("sp_z", (T, 2 * KH))
            sp_z2 = sbt("sp_z2", (T, 2 * KH))
            sp_p = sbt("sp_p", (T, 2 * KH))
            scratch = sbt("scratch", (128, 2 * 2 * FH))
            rscale = sbt("rscale", (128, 2))
            cls = sbt("cls", (B, 3, D))

            loads = [(w_in, "W_in"), (conv_w, "conv_w"), (conv_ws, "conv_ws"), (k_norm, "k_norm"),
                     (tanh_scale, "tanh_scale"), (theta, "theta"), (q_w, "q_norm"), (q_int, "w_int"),
                     (score_w, "score_w"), (score_b, "score_b"), (dist, "dist"), (decay, "decay"),
                     (w_gate, "W_gate"), (w_read, "W_read"), (w_read_f, "W_read_f"), (w_out, "W_out"),
                     (wf1, "ffn_w1"), (wf2, "ffn_w2"), (g_in, "g_in"), (g_out, "g_out"),
                     (w_qkv, "W_qkv"), (mix_l, "mix_l"), (mix_w, "mix_w"), (lam, "lam"),
                     (w_proj, "W_proj"), (b_proj, "b_proj"), (w_route, "W_route"), (cls, "cls"),
                     (upper, "upper"), (ident, "ident")]
            LOADED = 16 * len(loads)
            cls_added, cls_stored = sems("cls_added cls_stored")
            block = tmp.enter_context(nc.Block())

            @block.sync
            def _(sp):
                for tile, name in loads:
                    full = tuple(slice(None) for _ in tile.shape)
                    sp.dma_start(tile[full], a[name]).then_inc(const_loaded, 16)
                sp.wait_ge(cls_added, 1)
                sp.dma_start(h_dram[:, 0:2, :], cls[:, 0:2, :]).then_inc(cls_stored, 16)
                sp.wait_ge(cls_stored, 16)

            @block.gpsimd
            def _(pool):
                nc.gpsimd.memset(ones[:, :], 1.0)
                nc.gpsimd.memset(half_pi[:, :], 1.5707963267948966)
                nc.gpsimd.memset(neg_half[:, :], -0.5).then_inc(const_memset, 1)

            @block.tensor
            def _(pe):
                pe.wait_ge(const_memset, 1)
                pe.wait_ge(setup_a, 5)
                nc.tensor.matmul(psum_a[:, 0, 0:1], ones[0:HW, :], w_abs[0:HW, 0:1], start=True, stop=True)
                nc.tensor.matmul(psum_a[:, 0, 1:2], ones[:, :], w_abs[:, 1:2], start=True,
                                 stop=True).then_inc(setup_pe, 1)

            @block.scalar
            def _(act):
                act.wait_ge(const_loaded, LOADED)
                nc.scalar.activation(sp_u[:, :], decay[:, :], ACT.Abs).then_inc(setup_a, 1)
                act.wait_ge(setup_a, 1)
                nc.scalar.activation(sp_u[:, :], sp_u[:, :], ACT.Exp, scale=-1.0).then_inc(setup_a, 1)
                nc.scalar.activation(theta[:, :], theta[:, :], ACT.Tanh, scale=0.5).then_inc(setup_a, 1)
                act.wait_ge(setup_a, 3)
                nc.scalar.activation(scratch[0:HW, :], wf1[:, :, :].rearrange("p k n -> p (k n)"), ACT.Abs,
                                     accum_out=w_abs[0:HW, 0:1]).then_inc(setup_a, 1)
                act.wait_ge(setup_a, 4)
                nc.scalar.activation(scratch[:, 0:4 * D], wf2[:, :, :].rearrange("p k n -> p (k n)"), ACT.Abs,
                                     accum_out=w_abs[:, 1:2]).then_inc(setup_a, 1)
                act.wait_ge(setup_v, 1)
                nc.scalar.activation(q_int[:, :, :], q_int[:, :, :], ACT.Exp).then_inc(setup_a, 1)
                act.wait_ge(setup_done_a, 1)
                nc.scalar.activation(sp_u[:, :], time_w[:, :], ACT.Exp).then_inc(setup_a, 1)

            @block.vector
            def _(dve):
                count = [0]

                def link(ins):
                    count[0] += 1
                    ins.then_inc(setup_v, 1)
                    dve.wait_ge(setup_v, count[0])

                dve.wait_ge(const_loaded, LOADED)
                link(nc.vector.tensor_scalar(q_int[:, :, :], q_int[:, :, :], -5.0, 5.0, ALU.max, ALU.min))
                nc.vector.tensor_tensor(cls[:, 1, :], cls[:, 1, :], cls[:, 2, :], ALU.add).then_inc(cls_added, 1)
                nc.vector.tensor_copy(ident_b[:, :], ident[:, :])
                nc.vector.tensor_tensor(w_read[:, :, :], w_read[:, :, :], w_read_f[:, :, :], ALU.mult)
                nc.vector.tensor_scalar(lam_1[:, :], lam[:, :], -2.0, 1.0, ALU.mult, ALU.add)
                link(nc.vector.tensor_scalar(lam_2[:, :], lam[:, :], 3.0, None, ALU.mult))
                dve.wait_ge(setup_a, 3)
                link(nc.vector.tensor_scalar(theta[:, :], theta[:, :], 0.5, 0.5, ALU.mult, ALU.add))
                link(nc.vector.tensor_scalar(theta[:, :], theta[:, :], THETA_MAX - THETA_MIN, THETA_MIN,
                                             ALU.mult, ALU.add))

                def log1p_u():
                    link(nc.vector.tensor_scalar(sp_p[:, :], sp_u[:, :], 2.0, None, ALU.add))
                    link(nc.vector.reciprocal(sp_p[:, :], sp_p[:, :]))
                    link(nc.vector.tensor_tensor(sp_z[:, :], sp_u[:, :], sp_p[:, :], ALU.mult))
                    link(nc.vector.tensor_tensor(sp_z2[:, :], sp_z[:, :], sp_z[:, :], ALU.mult))
                    link(nc.vector.tensor_scalar(sp_p[:, :], sp_z2[:, :], 2.0 / (2 * LOG1P_TERMS - 1), None, ALU.mult))
                    for k in range(LOG1P_TERMS - 2, 0, -1):
                        link(nc.vector.scalar_tensor_tensor(out=sp_p[:, :], in0=sp_p[:, :], scalar=2.0 / (2 * k + 1),
                                                            in1=sp_z2[:, :], op0=ALU.add, op1=ALU.mult))
                    link(nc.vector.scalar_tensor_tensor(out=sp_p[:, :], in0=sp_p[:, :], scalar=2.0,
                                                        in1=sp_z[:, :], op0=ALU.add, op1=ALU.mult))

                log1p_u()
                link(nc.vector.scalar_tensor_tensor(out=sp_p[:, :], in0=decay[:, :], scalar=0.0, in1=sp_p[:, :],
                                                    op0=ALU.max, op1=ALU.add))
                nc.vector.scalar_tensor_tensor(out=time_w[:, :], in0=sp_p[:, :], scalar=-1.0, in1=dist[:, :],
                                               op0=ALU.mult, op1=ALU.mult).then_inc(setup_done_a, 1)
                dve.wait_ge(setup_a, 6)
                link(nc.vector.tensor_tensor(q_w[:, :, :], q_w[:, :, :], q_int[:, :, :], ALU.mult))
                dve.wait_ge(setup_a, 7)
                log1p_u()
                link(nc.vector.tensor_copy(time_w[:, :], sp_p[:, :]))
                dve.wait_ge(setup_pe, 1)
                nc.vector.tensor_scalar(w_mean[:, 0:1], psum_a[:, 0, 0:1], 1.0 / (2 * FH * D), EPS_Q, ALU.mult, ALU.max)
                link(nc.vector.tensor_scalar(w_mean[:, 1:2], psum_a[:, 0, 1:2], 1.0 / (FH * D), EPS_Q, ALU.mult, ALU.max))
                link(nc.vector.reciprocal(rscale[:, :], w_mean[:, :]))
                for wf, wq, rows, n in ((wf1, fq1, HW, 0), (wf2, fq2, 128, 1)):
                    link(nc.vector.tensor_scalar(wf[:, :, :], wf[:, :, :], rscale[0:rows, n:n + 1], MAGIC,
                                                 ALU.mult, ALU.add))
                    link(nc.vector.tensor_scalar(wf[:, :, :], wf[:, :, :], MAGIC, 1.0, ALU.subtract, ALU.min))
                    link(nc.vector.tensor_scalar(wq[:, :, :], wf[:, :, :], -1.0, None, ALU.max))

        with ExitStack() as tmp:
            def sbt(name, shape, dt=f32):
                return tmp.enter_context(nc.sbuf_tensor("tok_" + name, list(shape), dt))
            XG = PP * C * 2 * B
            xg = [sbt(f"xg{k}", (128, XG + PP * C)) for k in range(2)]
            wg = [sbt(f"wg{k}", (128, PP, 2, D)) for k in range(2)]
            bs = [sbt(f"bs{k}", (5, PP, B)) for k in range(2)]
            bm = [sbt(f"bm{k}", (5, PP, D)) for k in range(2)]
            xm = [sbt(f"xm{k}", (128, PP, 2 * B)) for k in range(2)]
            hg = [sbt(f"hg{k}", (B, PP, D)) for k in range(2)]
            tok_pixels, tok_weights, tok_merged, tok_product, tok_ready, tok_stored = (
                sems(f"{name}0 {name}1") for name in
                ("tok_pixels", "tok_weights", "tok_merged", "tok_product", "tok_ready", "tok_stored"))
            tok_step, = sems("tok_step")
            block = tmp.enter_context(nc.Block())
            PAIRS = NG // 2

            @block.sync
            def _(sp):
                def load_pixels(g, k):
                    sp.dma_start(xg[k][:, :], a["pixels"][bass.ds(g, 1)].rearrange("o p n -> (o p) n")).then_inc(tok_pixels[k], 16)

                def load_weights(g, k):
                    sp.dma_start(wg[k][:, :, :].rearrange("p a b c -> p (a b c)"),
                                 a["dec_w"][bass.ds(g, 1)].rearrange("o p n -> (o p) n")).then_inc(tok_weights[k], 16)
                    sp.dma_start(bs[k][:, :, :].rearrange("p a b -> p (a b)"),
                                 a["bias_s"][bass.ds(g, 1)].rearrange("o p n -> (o p) n")).then_inc(tok_weights[k], 16)
                    sp.dma_start(bm[k][:, :, :].rearrange("p a b -> p (a b)"),
                                 a["bias_m"][bass.ds(g, 1)].rearrange("o p n -> (o p) n")).then_inc(tok_weights[k], 16)

                for k in range(2):
                    load_pixels(k, k)
                    load_weights(k, k)
                with sp.Fori(1, PAIRS) as i:
                    for k in range(2):
                        sp.wait_ge(tok_merged[k], i)
                        load_pixels(i * 2 + k, k)
                        sp.wait_ge(tok_product[k], i)
                        load_weights(i * 2 + k, k)

            @block.vector
            def _(dve):
                def merge(i, k):
                    dve.wait_ge(tok_pixels[k], i * 16 + 16)
                    px = xg[k][:, 0:XG].rearrange("p (n c m) -> p n c m", n=PP, c=C)
                    mw = xg[k][:, XG:XG + PP * C].unsqueeze(2).broadcast_to([128, PP * C, 2 * B])
                    flat = xg[k][:, 0:XG].rearrange("p (n m) -> p n m", m=2 * B)
                    nc.vector.tensor_tensor(flat, flat, mw, ALU.mult).then_inc(tok_step, 1)
                    dve.wait_ge(tok_step, i * 4 + (2 * k + 1))
                    if not (isinstance(i, int) and i == 0):
                        dve.wait_ge(tok_product[k], i)
                    nc.vector.tensor_tensor(xm[k][:, :, :], px[:, :, 0, :], px[:, :, 1, :], ALU.add).then_inc(tok_step, 1)
                    dve.wait_ge(tok_step, i * 4 + (2 * k + 2))
                    nc.vector.tensor_tensor(xm[k][:, :, :], xm[k][:, :, :], px[:, :, 2, :],
                                            ALU.add).then_inc(tok_merged[k], 1)

                for k in range(2):
                    merge(0, k)
                with dve.Fori(1, PAIRS) as i:
                    for k in range(2):
                        merge(i, k)

            @block.tensor
            def _(pe):
                def products(i, k):
                    pe.wait_ge(tok_weights[k], i * 48 + 48)
                    pe.wait_ge(tok_merged[k], i + 1)
                    bank = psum[:, 4 * k:4 * k + 4, :]
                    for n in range(PP):
                        o = bank[0:B, n // 2, (n % 2) * D:(n % 2 + 1) * D]
                        for c in range(2):
                            nc.tensor.matmul(o, xm[k][:, n, c * B:(c + 1) * B], wg[k][:, n, c, :],
                                             start=(c == 0), stop=False)
                        last = nc.tensor.matmul(o, bs[k][:, n, :], bm[k][:, n, :], start=False, stop=True)
                    last.then_inc(tok_product[k], 1)

                for k in range(2):
                    products(0, k)
                with pe.Fori(1, PAIRS) as i:
                    for k in range(2):
                        pe.wait_ge(tok_ready[k], i)
                        products(i, k)

            @block.scalar
            def _(act):
                def evacuate(i, k):
                    act.wait_ge(tok_product[k], i + 1)
                    bank = psum[:, 4 * k:4 * k + 4, :]
                    nc.scalar.activation(hg[k][:, 0:6, :].rearrange("p (a b) n -> p a (b n)", b=2),
                                         bank[0:B, 0:3, 0:2 * D], ACT.Copy)
                    nc.scalar.activation(hg[k][:, 6, :], bank[0:B, 3, 0:D], ACT.Copy).then_inc(tok_ready[k], 1)
                    act.wait_ge(tok_ready[k], i + 1)
                    act.dma_start(h_dram[:, bass.ds((i * 2 + k) * PP + 2, PP), :], hg[k][:, :, :]).then_inc(tok_stored[k], 16)

                for k in range(2):
                    evacuate(0, k)
                with act.Fori(1, PAIRS) as i:
                    for k in range(2):
                        act.wait_ge(tok_stored[k], i * 16)
                        evacuate(i, k)
                for k in range(2):
                    act.wait_ge(tok_stored[k], 16 * PAIRS)



        x = sb("x", (T, 2, D))
        x_kept = sb("x_kept", (T, 2, D))
        xn = sb("xn", (T, 2, D))
        xT = sb("xT", (HW, 2, L))
        zc = sb("zc", (HW, 4, L))
        zs = sb("zs", (KH, L))
        gT = sb("gT", (KH, L))
        skip_in = sb("skip_in", (T, 2, SKIP))
        gs = sb("gs", (T, 2, 6, 112))
        zk = sb("zk", (T, 2, D + KH))
        zq = sb("zq", (T, 2, D))
        var = sb("var", (T, 2 * KH + 2))
        rs = sb("rs", (T, 2 * KH + 2))
        score = sb("score", (T, 2, KH))
        sp_u = sb("sp_u", (T, 2 * KH))
        sp_z = sb("sp_z", (T, 2 * KH))
        sp_z2 = sb("sp_z2", (T, 2 * KH))
        sp_p = sb("sp_p", (T, 2 * KH))
        kv = sb("kv", (T, 2, D))
        kvw = sb("kvw", (T, 2, D))
        phi = sb("phi", (T, 2 * D))
        sin_p = sb("sin_p", (T, 2, D))
        cos_p = sb("cos_p", (T, 2, D))
        stack = sb("stack", (T, 2, 2 * D + KH))
        den = sb("den", (T, 2, KH))
        s_re = sb("s_re", (T, 2 * D))
        s_im = sb("s_im", (T, 2 * D))
        qx_re = sb("qx_re", (T, 2 * D))
        qx_im = sb("qx_im", (T, 2 * D))
        m_a = sb("m_a", (T, 2 * D))
        m_b = sb("m_b", (T, 2 * D))
        phi_abs, sq = m_a, m_b
        oc = sb("oc", (T, 2, 2 * D))
        gate_t = sb("gate_t", (T, 2, 2 * D))
        sum_g = sb("sum_g", (T, 2))
        rs_g = sb("rs_g", (T, 2))
        gsT = sb("gsT", (112, 6, L))
        y_silu_t = sb("y_silu_t", (HW, 3, L))
        yT = sb("yT", (HW, 6, L))
        h1 = sb("h1", (T, 2, D))
        stats = sb("stats", (T, 2, 6))
        mv = sb("mv", (T, 2, 2))
        rstd = sb("rstd", (T, 2))
        n2_a = sb("n2_a", (T, 2))
        n2_b = sb("n2_b", (T, 2))
        amax = sb("amax", (T, 2))
        qscale = sb("qscale", (T, 2))
        deq1 = sb("deq1", (T, 2))
        deq2 = sb("deq2", (T, 2))
        xqb = sb("xqb", (T, 2, D), bf16)
        xqT = sb("xqT", (HW, 4, 100), bf16)
        sg_f = sb("sg_f", (T, 2, FH))
        y_f = sb("y_f", (T, 2, FH))
        sum_f = sb("sum_f", (T, 2))
        f_a = sb("f_a", (T, 2))
        f_b = sb("f_b", (T, 2))
        f_c = sb("f_c", (T, 2))
        yqb = sb("yqb", (T, 2, FH), bf16)
        yqT = sb("yqT", (128, 8, 100), bf16)
        h1_b = sb("h1_b", (T, 2, D))
        xn_b = sb("xn_b", (T, 2, D))
        stats_b = sb("stats_b", (T, 2, 6))
        mv_b = sb("mv_b", (T, 2, 2))
        rstd_b = sb("rstd_b", (T, 2))
        h2 = sb("h2", (T, 2, D))
        h3 = sb("h3", (T, 2, D))
        h4 = sb("h4", (T, 2, D))
        stats_c = sb("stats_c", (T, 2, 6))
        mv_c = sb("mv_c", (T, 2, 2))
        rstd_c = sb("rstd_c", (T, 2))
        xn_c = sb("xn_c", (T, 2, D))
        xT_c = sb("xT_c", (HW, 2, L))
        qT = sb("qT", (HW, 2, NPAD))
        kT = sb("kT", (HW + 1, 2, L))
        vp = sb("vp", (T, 2, KH, 32))
        qm = sb("qm", (HW + 1, 2, NT, SR))
        nmax = sb("nmax", (SR, 2, NT // 2))
        expo = [sb(f"expo{k}", (SR + 1, 2, L)) for k in range(2)]
        zsum = sb("zsum", (SR, NT // 2, 2))
        rz = sb("rz", (SR, NT // 2, 2))
        wz = [sb(f"wz{k}", (SR + 1, 2, SR)) for k in range(2)]
        at = sb("at", (T, NT, 2, SR))
        wT = sb("wT", (128, 3, NPAD))
        wp = sb("wp", (T, 2, 3 * 128))
        o2 = sb("o2", (128, 3, NPAD))
        h4_d = sb("h4_d", (T, 2, D))
        stats_d = sb("stats_d", (T, 2, 6))
        mv_d = sb("mv_d", (T, 2, 2))
        rstd_d = sb("rstd_d", (T, 2))
        xn_d = sb("xn_d", (T, 2, D))
        xT_d = sb("xT_d", (HW, 2, L))
        xsum = sb("xsum", (HW, 2))
        lmax = sb("lmax", (T, 2))
        lexp = sb("lexp", (T, NE))
        lsum = sb("lsum", (T, 1))
        route_w = sb("route_w", (T, 1))
        sel_f = sb("sel_f", (1, 4))
        sel = sb("sel", (1, 1), i32)
        e_w1 = sb("e_w1", (HW, 2, FM))
        e_w2 = sb("e_w2", (128, 6, D))
        e_b1 = sb("e_b1", (128, 6))
        e_b2 = sb("e_b2", (T, 2 * D))
        hT = sb("hT", (128, 6, L))
        o = sb("o", (T, 2, D))

        (x_loaded, x_free, skip_ready, stat1, rstd1, xn1, xT1_ps, xT1, z_ps, z_tap, conv_done, zT_ps, silu_done, kq_var, kq_rs,
         exp_u, tanh_in, tanh_out, phi_ready, trig, stack_ready, gate_ps, cum_ps, gate_done, g_ready, g_sum,
         g_rs, gs_ready, gsT_ps, gsT_ready, y_ps, y_silu, y_ready, out1_ps, h1_ready) = sems(
            "x_loaded x_free skip_ready stat1 rstd1 xn1 xT1_ps xT1 z_ps z_tap conv_done zT_ps silu_done kq_var kq_rs "
            "exp_u tanh_in tanh_out phi_ready trig stack_ready gate_ps cum_ps gate_done g_ready g_sum "
            "g_rs gs_ready gsT_ps gsT_ready y_ps y_silu y_ready out1_ps h1_ready")
        (stat2, norm2_s, xq_ready, xqT_ps, xqT_ready, h_ps, sg_ready, yf_ready, yf_sum, yf_s, yq_ready,
         yqT_ps, yqT_ready, out2_ps, h2_ready) = sems(
            "stat2 norm2_s xq_ready xqT_ps xqT_ready h_ps sg_ready yf_ready yf_sum yf_s yq_ready "
            "yqT_ps yqT_ready out2_ps h2_ready")
        (stat3, rstd3, xn3, xT3_ps, xT3, qkv_ps, q_ready, k_ready, v_ready, qm_ready, s_ps, s_max, exp_done,
         rz_ready, wz_ready, at_ps, at_ready, w_ps, w_ready, wT_ps, wp_ready, w2_ps, o2_ready, proj_ps, h4_ready,
         stat4, rstd4, xn4, xT4_ps, xT4, xsum_ready, logit_ps, lmax_ready, lexp_ready, sel_ready,
         expert_loaded, hid_ps, hid_ready, ffn_ps, o_ready, o_stored) = sems(
            "stat3 rstd3 xn3 xT3_ps xT3 qkv_ps q_ready k_ready v_ready qm_ready s_ps s_max exp_done "
            "rz_ready wz_ready at_ps at_ready w_ps w_ready wT_ps wp_ready w2_ps o2_ready proj_ps h4_ready "
            "stat4 rstd4 xn4 xT4_ps xT4 xsum_ready logit_ps lmax_ready lexp_ready sel_ready "
            "expert_loaded hid_ps hid_ready ffn_ps o_ready o_stored")
        v_mix, v_read, v_ffn, v_att, v_exp, a_mix, a_ffn, p_mix, p_read, p_ffn, p_att, p_exp, pad_set, pad_loaded = sems(
            "v_mix v_read v_ffn v_att v_exp a_mix a_ffn p_mix p_read p_ffn p_att p_exp pad_set pad_loaded")
        VA, VR, VB, VC, VD, AA, AB, PA, PR, PB, PC, PE = 23, 8, 15, 4, 7, 2, 1, 2, 2, 10, 1, 1

        block = ctx.enter_context(nc.Block())
        SU = NT // 2

        def run(eng, phases):
            def step(i):
                for phase in ORDER:
                    n = i - LAG[phase]
                    if phase in phases and not (isinstance(n, int) and not 1 <= n <= images):
                        phases[phase](n)

            for i in range(1, STAGES + 1):
                step(i)
            with eng.Fori(STAGES + 1, images) as i:
                step(i)
            for i in range(images, images + STAGES):
                step(i)
            for count, steps in counts:
                assert count[0] == steps * (STAGES + 2), [c[0] / (STAGES + 2) for c, _ in counts]
            counts.clear()

        counts = []

        def linked(eng, sem, steps):
            count = [0]

            def link(ins, n):
                count[0] += 1
                ins.then_inc(sem, 1)
                eng.wait_ge(sem, n * steps + ((count[0] - 1) % steps + 1 - steps))
            counts.append((count, steps))
            return link

        def own_wait(eng):
            eng.nop(nofuse=True)

        def signal(eng, ins, sem, n, each=1, at=0):
            ins.then_inc(sem, 1)
            eng.wait_ge(sem, n if each == 1 else n * each + (at + 1 - each))

        @block.sync
        def _(sp):
            sp.wait_ge(pad_set, 3)
            for k in range(2):
                for t in range(2):
                    sp.dma_start(wz[k][:, t, :], mix_w[:, :]).then_inc(pad_loaded, 16)
            sp.dma_start(qm[HW:HW + 1, 1, :, :].rearrange("p t r -> p (t r)"), a["b_l"]).then_inc(pad_loaded, 16)

            def load(n):
                for j in range(2):
                    sp.dma_start(x[:, j, :], h_dram[bass.ds(n - 1, 1), j * T:(j + 1) * T, :]
                                 .rearrange("o p d -> (o p) d")).then_inc(x_loaded, 16)

            def load_next(n):
                sp.wait_ge(x_free, n)
                sp.wait_ge(xn1, n)
                if not (isinstance(n, int) and n >= images):
                    load(n + 1)

            def experts(n):
                sp.wait_ge(sel_ready, n)
                own_wait(sp)
                e = sp.value_load(sel[0:1, 0:1], min_val=0, max_val=NE - 1)
                sp.dma_start(e_w1[:, :, :].rearrange("p a b -> p (a b)"),
                             a["W1"][bass.ds(e, 1)].rearrange("o p n -> (o p) n")).then_inc(expert_loaded, 16)
                sp.dma_start(e_w2[:, :, :].rearrange("p a b -> p (a b)"),
                             a["W2"][bass.ds(e, 1)].rearrange("o p n -> (o p) n")).then_inc(expert_loaded, 16)
                sp.dma_start(e_b1[:, :], a["b1"][bass.ds(e, 1)].rearrange("o p n -> (o p) n")).then_inc(expert_loaded, 16)
                sp.dma_start(e_b2[:, :], a["b2"][bass.ds(e, 1)].rearrange("o p n -> (o p) n")).then_inc(expert_loaded, 16)

            def store(n):
                sp.wait_ge(o_ready, n)
                for j in range(2):
                    sp.dma_start(out[bass.ds(n - 1, 1), j * T:(j + 1) * T, :].rearrange("o p d -> (o p) d"),
                                 o[:, j, :]).then_inc(o_stored, 16)

            load(1)
            sp_phases = {"keep_x": load_next, "choose": experts, "ffn_out": store}
            run(sp, sp_phases)
            sp.wait_ge(o_stored, 32 * images)

        @block.gpsimd
        def _(pool):
            nc.gpsimd.memset(kT[:, :, :], 1.0)
            nc.gpsimd.memset(vp[:, :, :, :], 0.0)
            nc.gpsimd.memset(qm[:, :, :, :], 0.0)
            nc.gpsimd.memset(qT[:, :, :], 0.0).then_inc(pad_set, 1)
            for k in range(2):
                nc.gpsimd.memset(expo[k][:, :, :], 1.0).then_inc(pad_set, 1)
            pool.wait_ge(pad_set, 3)
            link_a, link_r, link_b, link_c, link_d = (linked(pool, sem, steps) for sem, steps in
                                              ((p_mix, PA), (p_read, PR), (p_ffn, PB), (p_att, PC), (p_exp, PE)))

            def power(out_, in_, w):
                return nc.gpsimd.tensor_tensor(out_, in_, neg_half[0:T, 0:w], ALU.pow)

            def norm1(n):
                pool.wait_ge(stat1, n)
                own_wait(pool)
                link_a(nc.gpsimd.tensor_scalar(rstd[:, :], mv[:, :, 1], EPS_LN, 1.0, ALU.add, ALU.mult), n)
                signal(pool, power(rstd[:, :], rstd[:, :], 2), rstd1, n)

            def keep_x(n):
                if not (isinstance(n, int) and n == 1):
                    pool.wait_ge(h1_ready, n - 1)
                pool.wait_ge(x_loaded, n * 32)
                own_wait(pool)
                signal(pool, nc.gpsimd.tensor_copy(x_kept[:, :, :], x[:, :, :]), x_free, n)

            def kq(n):
                pool.wait_ge(kq_var, n)
                own_wait(pool)
                nc.gpsimd.tensor_scalar(rs[:, 0:2 * KH], var[:, 0:2 * KH], 1.0 / HD, EPS_RMS, ALU.mult, ALU.add)
                link_a(nc.gpsimd.tensor_scalar(rs[:, 2 * KH:], var[:, 2 * KH:], 1.0 / D, EPS_RMS, ALU.mult, ALU.add), n)
                signal(pool, power(rs[:, :], rs[:, :], 2 * KH + 2), kq_rs, n)

            def gated(n):
                pool.wait_ge(g_sum, n)
                own_wait(pool)
                link_r(nc.gpsimd.tensor_scalar(rs_g[:, :], sum_g[:, :], 0.25 / (2 * D), EPS_RMS, ALU.mult, ALU.add), n)
                link_r(power(rs_g[:, :], rs_g[:, :], 2), n)
                own_wait(pool)
                signal(pool, nc.gpsimd.tensor_scalar(rs_g[:, :], rs_g[:, :], 0.5, 0.0, ALU.mult, ALU.add), g_rs, n)

            def norm2(n):
                pool.wait_ge(stat2, n)
                own_wait(pool)
                link_b(nc.gpsimd.tensor_scalar(n2_a[:, :], mv_b[:, :, 1], EPS_LN, 1.0, ALU.add, ALU.mult), n)
                link_b(power(rstd_b[:, :], n2_a[:, :], 2), n)
                link_b(nc.gpsimd.tensor_tensor(n2_a[:, :], rstd_b[:, :], rstd_b[:, :], ALU.mult), n)
                link_b(nc.gpsimd.tensor_tensor(n2_a[:, :], n2_a[:, :], mv_b[:, :, 1], ALU.mult), n)
                own_wait(pool)
                link_b(nc.gpsimd.tensor_scalar(n2_a[:, :], n2_a[:, :], EPS_RMS, 1.0, ALU.add, ALU.mult), n)
                link_b(power(n2_b[:, :], n2_a[:, :], 2), n)
                signal(pool, nc.gpsimd.tensor_tensor(rstd_b[:, :], rstd_b[:, :], n2_b[:, :], ALU.mult), norm2_s, n)

            def ffn_norm(n):
                pool.wait_ge(yf_sum, n)
                link_b(nc.gpsimd.tensor_tensor(f_a[:, :], sum_f[:, :], deq1[:, :], ALU.mult), n)
                link_b(nc.gpsimd.tensor_tensor(f_a[:, :], f_a[:, :], deq1[:, :], ALU.mult), n)
                own_wait(pool)
                link_b(nc.gpsimd.tensor_scalar(f_a[:, :], f_a[:, :], 1.0 / FH, EPS_RMS, ALU.mult, ALU.add), n)
                link_b(power(f_b[:, :], f_a[:, :], 2), n)
                signal(pool, nc.gpsimd.tensor_tensor(f_b[:, :], f_b[:, :], deq1[:, :], ALU.mult), yf_s, n)

            def norm3(n):
                pool.wait_ge(stat3, n)
                own_wait(pool)
                link_c(nc.gpsimd.tensor_scalar(rstd_c[:, :], mv_c[:, :, 1], EPS_LN, 1.0, ALU.add, ALU.mult), n)
                signal(pool, power(rstd_c[:, :], rstd_c[:, :], 2), rstd3, n)

            def mix_queries(n, q):
                if q == 0:
                    pool.wait_ge(q_ready, n)
                t0 = q * QT
                for c in range(2):
                    last = nc.gpsimd.tensor_tensor(
                        qm[0:HW, c, t0:t0 + QT, :].rearrange("p t (g n) -> p t g n", n=NB),
                        qT[:, c, t0 * NB:(t0 + QT) * NB].rearrange("p (t n) -> p t n", n=NB)
                        .unsqueeze(2).broadcast_to([HW, QT, KH, NB]),
                        mix_l[:, c, :].unsqueeze(1).unsqueeze(3).broadcast_to([HW, QT, KH, NB]), ALU.mult)
                signal(pool, last, qm_ready, n, NT // QT, q)

            def first_queries(n):
                mix_queries(n, 0)
                mix_queries(n, 1)

            def mix_weights(u):
                def step(n):
                    if u % 2 == 0 and u // 2 + 2 < NT // QT:
                        mix_queries(n, u // 2 + 2)
                    pool.wait_ge(rz_ready, n * SU + (u + 1 - SU))
                    if u >= 2:
                        pool.wait_ge(at_ps, n * SU + (u - 1 - SU))
                    own_wait(pool)
                    for t in range(2):
                        last = nc.gpsimd.tensor_scalar(wz[u % 2][0:SR, t, :], mix_w[0:SR, :], rz[:, u, t:t + 1], 0.0,
                                                       ALU.mult, ALU.add)
                    signal(pool, last, wz_ready, n, SU, u)
                return step

            def norm4(n):
                pool.wait_ge(stat4, n)
                own_wait(pool)
                link_d(nc.gpsimd.tensor_scalar(rstd_d[:, :], mv_d[:, :, 1], EPS_LN, 1.0, ALU.add, ALU.mult), n)
                signal(pool, power(rstd_d[:, :], rstd_d[:, :], 2), rstd4, n)

            phases = {"norm1": norm1, "keep_x": keep_x, "kq": kq, "gated": gated, "norm2": norm2, "ffn_norm": ffn_norm,
                      "norm3": norm3, "qkv": first_queries, "norm4": norm4}
            for u in range(SU):
                phases[f"exp{u}"] = mix_weights(u)
            run(pool, phases)

        @block.scalar
        def _(act):
            link_a, link_b = linked(act, a_mix, AA), linked(act, a_ffn, AB)
            activation = nc.scalar.activation

            def xT1_(n):
                act.wait_ge(xT1_ps, n)
                signal(act, activation(xT[:, :, :].rearrange("p a b -> p (a b)"), psum_a[0:HW, 0, 0:2 * L], ACT.Copy), xT1, n)

            def z(n):
                act.wait_ge(z_ps, n)
                for g in range(4):
                    activation(zc[:, g, :], psum_a[0:HW, g // 2, (g % 2) * L:(g % 2 + 1) * L], ACT.Identity,
                               bias=0.0, scale=conv_w[:, g, TAPS - 1:TAPS])
                activation(zs[:, :], psum_a[0:KH, 2, 0:L], ACT.Identity, bias=0.0, scale=conv_ws[:, TAPS - 1:TAPS])
                activation(gT[:, :], psum_a[0:KH, 2, L:2 * L], ACT.Copy)
                signal(act, activation(skip_in[:, :, :].rearrange("p a b -> p (a b)"),
                                       psum_a[0:T, 2, 2 * L:2 * L + 2 * SKIP], ACT.Copy), z_tap, n)

            def skip(n):
                if not (isinstance(n, int) and n == 1):
                    act.wait_ge(gsT_ps, n - 1)
                for j in range(2):
                    last = activation(gs[:, j, :, 64:112], skip_in[:, j, :].unsqueeze(1).broadcast_to([T, 6, SKIP]), ACT.Copy)
                signal(act, last, skip_ready, n)

            def silu(n):
                act.wait_ge(zT_ps, n)
                activation(zk[:, :, :], psum_a[0:T, 0:2, 0:D + KH], ACT.Silu)
                signal(act, activation(zq[:, :, :], psum_a[0:T, 0:2, D + KH:CONV], ACT.Silu), silu_done, n)

            def kq(n):
                act.wait_ge(kq_var, n)
                link_a(activation(sp_u[:, :], score[:, :, :].rearrange("p a b -> p (a b)"), ACT.Abs), n)
                signal(act, activation(sp_u[:, :], sp_u[:, :], ACT.Exp, scale=-1.0), exp_u, n)

            def tanh_(n):
                act.wait_ge(tanh_in, n)
                signal(act, activation(phi[:, :], phi[:, :], ACT.Tanh), tanh_out, n)

            def gate(n):
                act.wait_ge(gate_ps, n)
                if not (isinstance(n, int) and n == 1):
                    act.wait_ge(g_ready, n - 1)
                activation(gate_t[:, 0, :], psum_a[0:T, 2, 0:2 * D], ACT.Tanh, scale=0.5)
                signal(act, activation(gate_t[:, 1, :], psum_a[0:T, 0, 0:2 * D], ACT.Tanh, scale=0.5), gate_done, n)

            def trig_(n):
                act.wait_ge(phi_ready, n)
                activation(sin_p[:, :, :].rearrange("p a b -> p (a b)"), phi[:, :], ACT.Sin)
                link_a(activation(phi_abs[:, :], phi[:, :], ACT.Abs), n)
                signal(act, activation(cos_p[:, :, :].rearrange("p a b -> p (a b)"), phi_abs[:, :], ACT.Sin,
                                       bias=half_pi[0:T, :], scale=-1.0), trig, n)

            def gated(n):
                act.wait_ge(g_ready, n)
                activation(s_re[:, :], oc[:, 0, :], ACT.Square, accum_out=sum_g[:, 0:1])
                signal(act, activation(s_im[:, :], oc[:, 1, :], ACT.Square, accum_out=sum_g[:, 1:2]), g_sum, n)

            def gsT_(n):
                act.wait_ge(gsT_ps, n)
                signal(act, activation(gsT[:, :, :].rearrange("p (a b) n -> p a (b n)", b=2),
                                       psum_a[0:112, 0:3, 0:2 * L], ACT.Copy), gsT_ready, n)

            def y_silu_(p):
                def step(n):
                    act.wait_ge(y_ps, n * 6 + (p - 5))
                    if p >= 3:
                        act.wait_ge(y_ready, n * 6 + (p - 8))
                    signal(act, activation(y_silu_t[:, p % 3, :], psum_a[0:HW, p % 3, L:2 * L], ACT.Silu), y_silu, n, 6, p)
                return step

            def xqT_(n):
                act.wait_ge(xqT_ps, n)
                signal(act, activation(xqT[:, :, 0:T], psum_z[0:HW, 0, 0:200].bitcast(bf16)
                                       .rearrange("p (k t) -> p k t", k=4)[:, :, 0:T], ACT.Copy), xqT_ready, n)

            def f_silu(j):
                def step(n):
                    act.wait_ge(h_ps, n * 2 + (j - 1))
                    signal(act, activation(sg_f[:, j, :], psum_z[0:T, 0, :], ACT.Silu, scale=deq1[:, j:j + 1]), sg_ready, n, 2, j)
                return step

            def ffn_norm(n):
                act.wait_ge(yf_ready, n * 2)
                link_b(activation(sg_f[:, 0, :], y_f[:, 0, :], ACT.Square, accum_out=sum_f[:, 0:1]), n)
                signal(act, activation(sg_f[:, 1, :], y_f[:, 1, :], ACT.Square, accum_out=sum_f[:, 1:2]), yf_sum, n)

            def yqT_(n):
                act.wait_ge(yqT_ps, n)
                signal(act, activation(yqT[:, :, 0:T], psum_z[:, 0, 0:400].bitcast(bf16)
                                       .rearrange("p (k t) -> p k t", k=8)[:, :, 0:T], ACT.Copy), yqT_ready, n)

            def xT3_(n):
                act.wait_ge(xT3_ps, n)
                signal(act, activation(xT_c[:, :, :].rearrange("p a b -> p (a b)"), psum_c[0:HW, 0, 0:2 * L], ACT.Copy), xT3, n)

            def qkv(n):
                act.wait_ge(qkv_ps, n)
                signal(act, activation(qT[:, :, 0:L], psum_c[0:HW, 1, 0:2 * L].rearrange("p (a b) -> p a b", a=2),
                                       ACT.Copy, scale=HD ** -0.5), q_ready, n)
                signal(act, activation(kT[0:HW, :, :].rearrange("p a b -> p (a b)"), psum_c[0:HW, 2, 0:2 * L], ACT.Copy), k_ready, n)
                signal(act, activation(vp[:, :, :, 0:HD].rearrange("p a g d -> p (a g) d"),
                                       psum_c[0:T, 0, 0:2 * D].rearrange("p (h d) -> p h d", d=HD), ACT.Copy), v_ready, n)

            def exps(u):
                def step(n):
                    act.wait_ge(s_max, n * SU + (u + 1 - SU))
                    if u >= 2:
                        act.wait_ge(at_ps, n * SU + (u - 1 - SU))
                    for t in range(2):
                        last = activation(expo[u % 2][0:SR, t, :], psum_c[0:SR, u % 2, t * L:(t + 1) * L], ACT.Exp,
                                          bias=nmax[:, t, u:u + 1], accum_out=zsum[:, u, t:t + 1])
                    signal(act, last, exp_done, n, SU, u)
                return step

            def keep_mixed(u):
                def step(n):
                    act.wait_ge(at_ps, n * SU + (u + 1 - SU))
                    signal(act, activation(at[:, 2 * u:2 * u + 2, :, :].rearrange("p t a n -> p (t a n)"),
                                           psum_c[0:T, 2, 0:4 * SR], ACT.Copy), at_ready, n, SU, u)
                return step

            def w_(n):
                act.wait_ge(w_ps, n)
                activation(wT[:, 0:2, :].rearrange("p a b -> p (a b)"), psum_c[:, 0, 0:2 * NPAD], ACT.Copy)
                signal(act, activation(wT[:, 2, :], psum_c[:, 1, 0:NPAD], ACT.Copy), w_ready, n)

            def wp_(n):
                act.wait_ge(wT_ps, n)
                activation(wp[:, 0, :], psum_c[0:T, 2, 0:384], ACT.Copy)
                signal(act, activation(wp[:, 1, :], psum_c[0:T, 0, 0:384], ACT.Copy), wp_ready, n)

            def xT4_(n):
                act.wait_ge(xT4_ps, n)
                signal(act, activation(xT_d[:, :, :].rearrange("p a b -> p (a b)"), psum_z[0:HW, 0, 0:2 * L], ACT.Copy), xT4, n)

            def route(n):
                act.wait_ge(lmax_ready, n)
                signal(act, activation(lexp[:, :], psum_z[0:T, 1, 0:NE], ACT.Exp, bias=lmax[:, 1:2], scale=1.0 / L,
                                       accum_out=lsum[:, :]), lexp_ready, n)

            def hidden(r):
                def step(n):
                    act.wait_ge(expert_loaded, n * 64)
                    act.wait_ge(hid_ps, n * 3 + (r - 2))
                    for k in range(2):
                        ins = activation(hT[:, 2 * r + k, :], psum_z[:, r % 2, k * L:(k + 1) * L], ACT.Gelu,
                                          bias=e_b1[:, 2 * r + k:2 * r + k + 1])
                    signal(act, ins, hid_ready, n, 3, r)
                return step

            phases = {"xT1": xT1_, "z": z, "skip": skip, "zT": silu, "kq": kq, "tanh": tanh_, "gate_t": gate, "trig": trig_,
                      "gated": gated, "gsT": gsT_, "xqT": xqT_, "ffn_norm": ffn_norm, "yqT": yqT_,
                      "xT3": xT3_, "qkv": qkv, "w": w_, "wp": wp_, "xT4": xT4_, "route": route}
            for p in range(6):
                phases[f"y{p}"] = y_silu_(p)
            for j in range(2):
                phases[f"hid{j}"] = f_silu(j)
            for r in range(3):
                phases[f"hidden{r}"] = hidden(r)
            for u in range(SU):
                phases[f"exp{u}"] = exps(u)
                if u % 2 == 1:
                    phases[f"mixed{u}"] = keep_mixed(u)
            run(act, phases)

        @block.tensor
        def _(pe):
            matmul, transpose = nc.tensor.matmul, nc.tensor.transpose

            def halves_T(src, bank):
                for c in range(2):
                    for j in range(2):
                        last = transpose(bank[0:HW, c * L + j * T:c * L + (j + 1) * T],
                                         src[:, j, c * HW:(c + 1) * HW], ident[0:T, 0:T])
                return last

            def xT1_(n):
                pe.wait_ge(xn1, n)
                halves_T(xn, psum_a[:, 0, :]).then_inc(xT1_ps, 1)

            def z(n):
                pe.wait_ge(xT1, n)
                if not (isinstance(n, int) and n == 1):
                    pe.wait_ge(g_ready, n - 1)

                def channels(o_, c0, width):
                    for c in range(2):
                        matmul(o_, w_in[:, c, c0:c0 + width], xT[:, c, :], start=(c == 0), stop=(c == 1))
                for g, c0 in enumerate((0, HW, D + KH, D + KH + HW)):
                    channels(psum_a[0:HW, g // 2, (g % 2) * L:(g % 2 + 1) * L], c0, HW)
                channels(psum_a[0:KH, 2, 0:L], D, KH)
                channels(psum_a[0:KH, 2, L:2 * L], CONV + SKIP, KH)
                for j in range(2):
                    for c in range(2):
                        last = matmul(psum_a[0:T, 2, 2 * L + j * SKIP:2 * L + (j + 1) * SKIP], xT[:, c, j * T:(j + 1) * T],
                                      w_in[:, c, CONV:CONV + SKIP], start=(c == 0), stop=(c == 1))
                last.then_inc(z_ps, 1)

            def zT(n):
                pe.wait_ge(conv_done, n)
                for j in range(2):
                    t = slice(j * T, (j + 1) * T)
                    for src, rows, c0 in ((zc[:, 0, t], HW, 0), (zc[:, 1, t], HW, HW), (zs[:, t], KH, D),
                                          (zc[:, 2, t], HW, D + KH), (zc[:, 3, t], HW, D + KH + HW)):
                        last = transpose(psum_a[0:T, j, c0:c0 + rows], src, ident[0:rows, 0:rows])
                last.then_inc(zT_ps, 1)

            def gate(n):
                for j in range(2):
                    if j == 1:
                        pe.wait_ge(silu_done, n)
                    last = matmul(psum_a[0:T, 2 * (1 - j), 0:2 * D], gT[:, j * T:(j + 1) * T], w_gate[:, :],
                                  start=True, stop=True)
                last.then_inc(gate_ps, 1)

            def cum(n):
                pe.wait_ge(stack_ready, n)
                pe.wait_ge(gate_done, n)
                matmul(psum_a[0:T, 1, 0:CONV], upper[:, :], stack[:, 0, :], start=True, stop=True)
                matmul(psum_a[0:T, 2, 0:CONV], ones[0:T, 0:T], stack[:, 0, :], start=True, stop=False)
                matmul(psum_a[0:T, 2, 0:CONV], upper[:, :], stack[:, 1, :], start=False, stop=True).then_inc(cum_ps, 1)

            def gsT_(n):
                pe.wait_ge(gs_ready, n)
                pe.wait_ge(skip_ready, n)
                pe.wait_ge(gate_done, min(n + 1, images) if isinstance(n, int) else n + 1)
                for p in range(6):
                    for j in range(2):
                        c0 = (p % 2) * L + j * T
                        last = transpose(psum_a[0:112, p // 2, c0:c0 + T], gs[:, j, p, :], ident[0:T, 0:T])
                last.then_inc(gsT_ps, 1)

            def y(p):
                def step(n):
                    pe.wait_ge(gsT_ready, n)
                    if p >= 3:
                        pe.wait_ge(y_ready, n * 6 + (p - 8))
                    for half in range(2):
                        last = matmul(psum_a[0:HW, p % 3, half * L:(half + 1) * L],
                                      w_read[:, p, half * HW:(half + 1) * HW], gsT[:, p, :], start=True, stop=True)
                    last.then_inc(y_ps, 1)
                return step

            def out1(n):
                pe.wait_ge(y_ready, n * 6)
                for j in range(2):
                    for p in range(6):
                        last = matmul(psum_a[0:T, 0, j * D:(j + 1) * D], yT[:, p, j * T:(j + 1) * T], w_out[:, p, :],
                                      start=(p == 0), stop=(p == 5))
                last.then_inc(out1_ps, 1)

            def xqT_(n):
                pe.wait_ge(xq_ready, n)
                bank = psum_z[0:HW, 0, 0:200].bitcast(bf16)
                for c in range(2):
                    for j in range(2):
                        c0 = (2 * c + j) * 100
                        last = transpose(bank[:, c0:c0 + T], xqb[:, j, c * HW:(c + 1) * HW], ident_b[0:T, 0:T])
                last.then_inc(xqT_ps, 1)

            def hid1(j):
                def step(n):
                    pe.wait_ge(xqT_ready, n)
                    if j == 1:
                        pe.wait_ge(yf_ready, n * 2 - 1)
                    for part, bank in ((1, 0), (0, 1)):
                        for c in range(2):
                            last = matmul(psum_z[0:T, bank, :], xqT[:, 2 * c + j, 0:T],
                                          fq1[:, c, part * FH:(part + 1) * FH], start=(c == 0), stop=(c == 1))
                    last.then_inc(h_ps, 1)
                return step

            def yqT_(n):
                pe.wait_ge(yq_ready, n)
                bank = psum_z[:, 0, 0:400].bitcast(bf16)
                for c in range(4):
                    for j in range(2):
                        c0 = (2 * c + j) * 100
                        last = transpose(bank[:, c0:c0 + T], yqb[:, j, c * 128:(c + 1) * 128], ident_b[0:T, 0:T])
                last.then_inc(yqT_ps, 1)

            def out2(n):
                pe.wait_ge(yqT_ready, n)
                for j in range(2):
                    for c in range(4):
                        last = matmul(psum_z[0:T, 1, j * D:(j + 1) * D], yqT[:, 2 * c + j, 0:T], fq2[:, c, :],
                                      start=(c == 0), stop=(c == 3))
                last.then_inc(out2_ps, 1)

            def xT3_(n):
                pe.wait_ge(xn3, n)
                halves_T(xn_c, psum_c[:, 0, :]).then_inc(xT3_ps, 1)

            def qkv(n):
                pe.wait_ge(xT3, n)
                for bank, c0 in ((1, 0), (2, D)):
                    for half in range(2):
                        for c in range(2):
                            matmul(psum_c[0:HW, bank, half * L:(half + 1) * L],
                                   w_qkv[:, c, c0 + half * HW:c0 + (half + 1) * HW], xT_c[:, c, :],
                                   start=(c == 0), stop=(c == 1))
                for j in range(2):
                    for c in range(2):
                        last = matmul(psum_c[0:T, 0, j * D:(j + 1) * D], xT_c[:, c, j * T:(j + 1) * T],
                                      w_qkv[:, c, 2 * D:3 * D], start=(c == 0), stop=(c == 1))
                last.then_inc(qkv_ps, 1)

            def scores(u):
                def step(n):
                    if u == 0:
                        pe.wait_ge(pad_loaded, 80)
                        pe.wait_ge(v_ready, n)
                    if u % 2 == 0:
                        pe.wait_ge(qm_ready, n * (NT // QT) + (u // 2 + 1 - NT // QT))
                    if u >= 2:
                        pe.wait_ge(exp_done, n * SU + (u - 1 - SU))
                    for t in range(2):
                        o_ = psum_c[0:SR, u % 2, t * L:(t + 1) * L]
                        matmul(o_, qm[0:HW, 0, 2 * u + t, :], kT[0:HW, 0, :], start=True, stop=False)
                        last = matmul(o_, qm[:, 1, 2 * u + t, :], kT[:, 1, :], start=False, stop=True)
                    last.then_inc(s_ps, 1)
                return step

            def mixed(u):
                def step(n):
                    pe.wait_ge(exp_done, n * SU + (u + 1 - SU))
                    pe.wait_ge(wz_ready, n * SU + (u + 1 - SU))
                    if u >= 1:
                        pe.wait_ge(at_ready, n * SU + (u - SU))
                    for t in range(2):
                        for half in range(2):
                            c0 = (2 * t + half) * SR
                            last = matmul(psum_c[0:T, 2, c0:c0 + SR], expo[u % 2][:, t, half * T:(half + 1) * T],
                                          wz[u % 2][:, t, :], start=True, stop=True)
                    last.then_inc(at_ps, 1)
                return step

            def apply_attention(values):
                for g in range(KH):
                    r, q = g // 4, g % 4
                    for half in range(2):
                        last = matmul(psum_c[32 * q:32 * q + 32, r // 2, (r % 2) * NPAD:(r % 2 + 1) * NPAD],
                                      values[:, half, g, :], at[:, :, half, g * NB:(g + 1) * NB],
                                      start=(half == 0), stop=(half == 1))
                return last

            def w_(n):
                pe.wait_ge(at_ready, n * SU)
                pe.wait_ge(v_ready, n)
                apply_attention(vp).then_inc(w_ps, 1)

            def wp_(n):
                pe.wait_ge(w_ready, n)
                for j in range(2):
                    for r in range(3):
                        last = transpose(psum_c[0:T, 2 * (1 - j), r * 128:(r + 1) * 128], wT[:, r, j * T:(j + 1) * T], ident[:, :])
                last.then_inc(wT_ps, 1)

            def w2(n):
                pe.wait_ge(wp_ready, n)
                apply_attention(wp[:, :, :].rearrange("p a (g d) -> p a g d", d=32)).then_inc(w2_ps, 1)

            def proj(n):
                pe.wait_ge(o2_ready, n)
                for j in range(2):
                    for r in range(3):
                        last = matmul(psum_c[0:T, 2, j * D:(j + 1) * D], o2[:, r, j * T:(j + 1) * T], w_proj[:, r, :],
                                      start=(r == 0), stop=(r == 2))
                last.then_inc(proj_ps, 1)

            def xT4_(n):
                pe.wait_ge(xn4, n)
                halves_T(xn_d, psum_z[:, 0, :]).then_inc(xT4_ps, 1)

            def route(n):
                pe.wait_ge(xsum_ready, n)
                for c in range(2):
                    last = matmul(psum_z[0:T, 1, 0:NE], xsum[:, c:c + 1].broadcast_to([HW, T]), w_route[:, c, :],
                                  start=(c == 0), stop=(c == 1))
                last.then_inc(logit_ps, 1)

            def hidden(r):
                def step(n):
                    pe.wait_ge(expert_loaded, n * 64)
                    if r == 0:
                        pe.wait_ge(lexp_ready, n)
                        pe.wait_ge(h2_ready, min(n + 2, images) if isinstance(n, int) else n + 2)
                    if r == 2:
                        pe.wait_ge(hid_ready, n * 3 - 2)
                    for k in range(2):
                        f = 2 * r + k
                        for c in range(2):
                            last = matmul(psum_z[:, r % 2, k * L:(k + 1) * L], e_w1[:, c, f * 128:(f + 1) * 128],
                                          xT_d[:, c, :], start=(c == 0), stop=(c == 1))
                    last.then_inc(hid_ps, 1)
                return step

            def ffn_out(n):
                pe.wait_ge(hid_ready, n * 3)
                for j in range(2):
                    for f in range(6):
                        last = matmul(psum_z[0:T, 1, j * D:(j + 1) * D], hT[:, f, j * T:(j + 1) * T], e_w2[:, f, :],
                                      start=(f == 0), stop=(f == 5))
                last.then_inc(ffn_ps, 1)

            phases = {"xT1": xT1_, "z": z, "zT": zT, "gate_t": gate, "cum": cum, "gsT": gsT_, "h1": out1, "xqT": xqT_,
                      "yqT": yqT_, "out2": out2, "xT3": xT3_, "qkv": qkv, "w": w_, "wp": wp_, "w2": w2,
                      "proj": proj, "xT4": xT4_, "route": route, "ffn_out": ffn_out}
            for p in range(6):
                phases[f"y{p}"] = y(p)
            for j in range(2):
                phases[f"hid{j}"] = hid1(j)
            for r in range(3):
                phases[f"hidden{r}"] = hidden(r)
            for u in range(SU):
                phases[f"score{u}"] = scores(u)
                phases[f"mixed{u}"] = mixed(u)
            run(pe, phases)

        @block.vector
        def _(dve):
            link_a, link_r, link_b, link_c, link_d = (linked(dve, sem, steps) for sem, steps in
                                              ((v_mix, VA), (v_read, VR), (v_ffn, VB), (v_att, VC), (v_exp, VD)))
            tt, ts, stt = nc.vector.tensor_tensor, nc.vector.tensor_scalar, nc.vector.scalar_tensor_tensor

            def heads(ap, width=HD):
                return ap.rearrange("p (h d) -> p h d", d=width)

            def flat(t):
                return t[:, :, :].rearrange("p a b -> p (a b)")

            def halves(t):
                return t[:, :].rearrange("p (a b) -> p a b", a=2)

            def row_stats(h, stats_, mv_, link, n, ready):
                for j in range(2):
                    last = nc.vector.bn_stats(stats_[:, j, :], h[:, j, :])
                link(last, n)
                own_wait(dve)
                nc.vector.bn_aggr(mv_[:, 0, :], stats_[:, 0, :])
                signal(dve, nc.vector.bn_aggr(mv_[:, 1, :], stats_[:, 1, :]), ready, n)

            def normalise(out_, h, mv_, rstd_):
                for j in range(2):
                    last = ts(out_[:, j, :], h[:, j, :], mv_[:, j, 0:1], rstd_[:, j:j + 1], ALU.subtract, ALU.mult)
                return last

            def norm1(n):
                dve.wait_ge(x_loaded, n * 32)
                row_stats(x, stats, mv, link_a, n, stat1)

            def norm1_apply(n):
                dve.wait_ge(rstd1, n)
                signal(dve, normalise(xn, x, mv, rstd), xn1, n)

            def conv(n):
                dve.wait_ge(z_tap, n)
                for s in range(1, TAPS):
                    w = TAPS - 1 - s
                    for g in range(4):
                        c0 = (g % 2) * L
                        stt(out=zc[:, g, s:L], in0=psum_a[0:HW, g // 2, c0:c0 + L - s], scalar=conv_w[:, g, w:w + 1],
                            in1=zc[:, g, s:L], op0=ALU.mult, op1=ALU.add)
                    last = stt(out=zs[:, s:L], in0=psum_a[0:KH, 2, 0:L - s], scalar=conv_ws[:, w:w + 1], in1=zs[:, s:L],
                               op0=ALU.mult, op1=ALU.add)
                    if s < TAPS - 1:
                        link_a(last, n)
                signal(dve, last, conv_done, n)

            def kq(n):
                dve.wait_ge(silu_done, n)
                tt(score[:, :, :], zk[:, :, D:D + KH], score_w[:, :].rearrange("p (a b) -> p a b", a=2), ALU.mult)
                link_a(tt(halves(sq), zk[:, :, 0:D], zk[:, :, 0:D], ALU.mult), n)
                tt(score[:, :, :], score[:, :, :], score_b[:, :].rearrange("p (a b) -> p a b", a=2), ALU.add)
                link_a(nc.vector.reduce_sum(var[:, 0:2 * KH], heads(sq[:, :]), axis=AX.X), n)
                link_a(tt(sq[:, :], flat(zq), flat(zq), ALU.mult), n)
                signal(dve, nc.vector.reduce_sum(var[:, 2 * KH:], halves(sq), axis=AX.X), kq_var, n)
                for c, q in ((0, qx_re), (1, qx_im)):
                    src = flat(zq).rearrange("p (q h c) -> p q h c", h=HD, c=2)[:, :, :, c]
                    tt(q[:, :].rearrange("p (q r h) -> p q r h", r=2, h=HD),
                       src.unsqueeze(2).broadcast_to([T, 2 * NQ, 2, HD]),
                       q_w[:, c, :].rearrange("p (q r h) -> p q r h", r=2, h=HD), ALU.mult)

            def keys(n):
                dve.wait_ge(kq_rs, n)
                link_a(tt(kv[:, :, :].rearrange("p a (k h) -> p a k h", h=HD),
                         zk[:, :, 0:D].rearrange("p a (k h) -> p a k h", h=HD),
                         rs[:, 0:2 * KH].rearrange("p (a k) -> p a k", a=2).unsqueeze(3).broadcast_to([T, 2, KH, HD]),
                         ALU.mult), n)
                link_a(tt(flat(kv), flat(kv), k_norm[:, :], ALU.mult), n)
                signal(dve, tt(phi[:, :], flat(kv), tanh_scale[:, :], ALU.mult), tanh_in, n)

            def softplus(n):
                dve.wait_ge(exp_u, n)
                link_a(ts(sp_p[:, :], sp_u[:, :], 2.0, None, ALU.add), n)
                link_a(nc.vector.reciprocal(sp_p[:, :], sp_p[:, :]), n)
                link_a(tt(sp_z[:, :], sp_u[:, :], sp_p[:, :], ALU.mult), n)
                link_a(tt(sp_z2[:, :], sp_z[:, :], sp_z[:, :], ALU.mult), n)
                link_a(ts(sp_p[:, :], sp_z2[:, :], 2.0 / (2 * LOG1P_TERMS - 1), None, ALU.mult), n)
                for k in range(LOG1P_TERMS - 2, 0, -1):
                    link_a(stt(out=sp_p[:, :], in0=sp_p[:, :], scalar=2.0 / (2 * k + 1), in1=sp_z2[:, :],
                              op0=ALU.add, op1=ALU.mult), n)
                link_a(stt(out=sp_p[:, :], in0=sp_p[:, :], scalar=2.0, in1=sp_z[:, :], op0=ALU.add, op1=ALU.mult), n)
                link_a(stt(out=sp_p[:, :], in0=flat(score), scalar=0.0, in1=sp_p[:, :], op0=ALU.max, op1=ALU.add), n)
                link_a(tt(sp_p[:, :], sp_p[:, :], time_w[:, :], ALU.mult), n)
                p_w = stack[:, :, 2 * D:2 * D + KH]
                link_a(ts(p_w, sp_p[:, :].rearrange("p (a k) -> p a k", a=2), 1e-6, 1000.0, ALU.max, ALU.min), n)

            def angles(n):
                dve.wait_ge(tanh_out, n)
                signal(dve, tt(phi[:, :], phi[:, :], theta[:, :], ALU.mult), phi_ready, n)

            def weighted(n):
                p_w = stack[:, :, 2 * D:2 * D + KH]
                link_a(tt(kvw[:, :, :].rearrange("p a (k h) -> p a k h", h=HD),
                         kv[:, :, :].rearrange("p a (k h) -> p a k h", h=HD),
                         p_w.unsqueeze(3).broadcast_to([T, 2, KH, HD]), ALU.mult), n)

            def trig_(n):
                dve.wait_ge(trig, n)
                tt(stack[:, :, 0:D], kvw[:, :, :], cos_p[:, :, :], ALU.mult)
                signal(dve, tt(stack[:, :, D:2 * D], kvw[:, :, :], sin_p[:, :, :], ALU.mult), stack_ready, n)

            def match(n):
                dve.wait_ge(cum_ps, n)
                link_r(ts(den[:, :, :], psum_a[0:T, 1:3, 2 * D:2 * D + KH], 1e-4, None, ALU.max), n)
                link_r(nc.vector.reciprocal(den[:, :, :], den[:, :, :]), n)
                link_r(tt(den[:, :, :], den[:, :, :],
                         rs[:, 2 * KH:].unsqueeze(2).broadcast_to([T, 2, KH]), ALU.mult), n)
                for c, s in ((0, s_re), (1, s_im)):
                    last = tt(s[:, :].rearrange("p (a k h) -> p a k h", a=2, h=HD),
                              psum_a[0:T, 1:3, c * D:(c + 1) * D].rearrange("p a (k h) -> p a k h", h=HD),
                              den[:, :, :].unsqueeze(3).broadcast_to([T, 2, KH, HD]), ALU.mult)
                link_r(last, n)
                oc_h = flat(oc).rearrange("p (k c h) -> p k c h", c=2, h=HD)
                tt(m_a[:, :], s_re[:, :], qx_re[:, :], ALU.mult)
                link_r(tt(m_b[:, :], s_im[:, :], qx_im[:, :], ALU.mult), n)
                link_r(tt(oc_h[:, :, 0, :], heads(m_a[:, :]), heads(m_b[:, :]), ALU.add), n)
                tt(m_a[:, :], s_im[:, :], qx_re[:, :], ALU.mult)
                link_r(tt(m_b[:, :], s_re[:, :], qx_im[:, :], ALU.mult), n)
                link_r(tt(oc_h[:, :, 1, :], heads(m_a[:, :]), heads(m_b[:, :]), ALU.subtract), n)

            def gate(n):
                dve.wait_ge(gate_done, n)
                signal(dve, stt(out=flat(oc), in0=flat(gate_t), scalar=1.0, in1=flat(oc), op0=ALU.add, op1=ALU.mult),
                       g_ready, n)

            def gated(n):
                dve.wait_ge(g_rs, n)
                for j in range(2):
                    last = ts(gs[:, j, :, 0:64], oc[:, j, :].rearrange("p (q c) -> p q c", c=64), rs_g[:, j:j + 1], None,
                              ALU.mult)
                signal(dve, last, gs_ready, n)

            def y(p):
                def step(n):
                    dve.wait_ge(y_silu, n * 6 + (p - 5))
                    signal(dve, tt(yT[:, p, :], psum_a[0:HW, p % 3, 0:L], y_silu_t[:, p % 3, :], ALU.mult), y_ready, n, 6, p)
                return step

            def h1_(n):
                dve.wait_ge(out1_ps, n)
                dve.wait_ge(x_free, n)
                signal(dve, tt(flat(h1), psum_a[0:T, 0, 0:2 * D], flat(x_kept), ALU.add), h1_ready, n)

            def quantise(src, out_, w, deq, n):
                link_b(nc.vector.tensor_reduce(amax[:, :], src, axis=AX.X, op=ALU.max, apply_absolute_value=True), n)
                link_b(ts(amax[:, :], amax[:, :], EPS_Q, None, ALU.max), n)
                ts(deq[:, :], amax[:, :], 1.0 / 127.0, w_mean[0:T, w:w + 1], ALU.mult, ALU.mult)
                link_b(nc.vector.reciprocal(qscale[:, :], amax[:, :]), n)
                link_b(ts(qscale[:, :], qscale[:, :], 127.0, None, ALU.mult), n)
                for j in range(2):
                    last = ts(src[:, j, :], src[:, j, :], qscale[:, j:j + 1], MAGIC, ALU.mult, ALU.add)
                link_b(last, n)
                return ts(out_, src, MAGIC, None, ALU.subtract)

            def norm2(n):
                dve.wait_ge(h1_ready, n)
                link_b(nc.vector.tensor_copy(flat(h1_b), flat(h1)), n)
                row_stats(h1_b, stats_b, mv_b, link_b, n, stat2)

            def norm2_apply(n):
                dve.wait_ge(norm2_s, n)
                link_b(normalise(xn_b, h1_b, mv_b, rstd_b), n)
                link_b(tt(flat(xn_b), flat(xn_b), g_in[:, :], ALU.mult), n)
                signal(dve, quantise(xn_b[:, :, :], xqb[:, :, :], 0, deq1, n), xq_ready, n)

            def hid1(j):
                def step(n):
                    dve.wait_ge(sg_ready, n * 2 + (j - 1))
                    signal(dve, tt(y_f[:, j, :], psum_z[0:T, 1, :], sg_f[:, j, :], ALU.mult), yf_ready, n, 2, j)
                return step

            def ffn_norm(n):
                dve.wait_ge(yf_s, n)
                for j in range(2):
                    last = stt(out=y_f[:, j, :], in0=y_f[:, j, :], scalar=f_b[:, j:j + 1], in1=g_out[:, :],
                               op0=ALU.mult, op1=ALU.mult)
                link_b(last, n)
                signal(dve, quantise(y_f[:, :, :], yqb[:, :, :], 1, deq2, n), yq_ready, n)

            def out2(n):
                dve.wait_ge(out2_ps, n)
                for j in range(2):
                    last = stt(out=h2[:, j, :], in0=psum_z[0:T, 1, j * D:(j + 1) * D], scalar=deq2[:, j:j + 1],
                               in1=h1_b[:, j, :], op0=ALU.mult, op1=ALU.add)
                signal(dve, last, h2_ready, n)

            def norm3(n):
                dve.wait_ge(h2_ready, n)
                link_c(nc.vector.tensor_copy(flat(h3), flat(h2)), n)
                row_stats(h3, stats_c, mv_c, link_c, n, stat3)

            def norm3_apply(n):
                dve.wait_ge(rstd3, n)
                signal(dve, normalise(xn_c, h3, mv_c, rstd_c), xn3, n)

            def score_max(u):
                def step(n):
                    dve.wait_ge(s_ps, n * SU + (u + 1 - SU))
                    signal(dve, nc.vector.tensor_reduce(nmax[:, :, u], psum_c[0:SR, u % 2, 0:2 * L]
                                                        .rearrange("p (t m) -> p t m", t=2),
                                                        axis=AX.X, op=ALU.max, negate=True), s_max, n, SU, u)
                return step

            def denominators(u):
                def step(n):
                    dve.wait_ge(exp_done, n * SU + (u + 1 - SU))
                    signal(dve, nc.vector.reciprocal(rz[:, u, :], zsum[:, u, :]), rz_ready, n, SU, u)
                return step

            def keep_mixed(u):
                def step(n):
                    dve.wait_ge(at_ps, n * SU + (u + 1 - SU))
                    signal(dve, nc.vector.tensor_copy(at[:, 2 * u:2 * u + 2, :, :].rearrange("p t a n -> p (t a n)"),
                                                      psum_c[0:T, 2, 0:4 * SR]), at_ready, n, SU, u)
                return step

            def w2(n):
                dve.wait_ge(w_ready, n)
                for r in range(3):
                    last = ts(o2[:, r, :], wT[:, r, :], lam_1[:, r:r + 1], None, ALU.mult)
                link_c(last, n)

            def w2_add(n):
                dve.wait_ge(w2_ps, n)
                for r in range(3):
                    last = stt(out=o2[:, r, :], in0=psum_c[:, r // 2, (r % 2) * NPAD:(r % 2 + 1) * NPAD],
                               scalar=lam_2[:, r:r + 1], in1=o2[:, r, :], op0=ALU.mult, op1=ALU.add)
                signal(dve, last, o2_ready, n)

            def proj(n):
                dve.wait_ge(proj_ps, n)
                link_c(tt(flat(h4), psum_c[0:T, 2, 0:2 * D], flat(h3), ALU.add), n)
                signal(dve, tt(flat(h4), flat(h4), b_proj[:, :], ALU.add), h4_ready, n)

            def norm4(n):
                dve.wait_ge(h4_ready, n)
                link_d(nc.vector.tensor_copy(flat(h4_d), flat(h4)), n)
                row_stats(h4_d, stats_d, mv_d, link_d, n, stat4)

            def norm4_apply(n):
                dve.wait_ge(rstd4, n)
                signal(dve, normalise(xn_d, h4_d, mv_d, rstd_d), xn4, n)

            def route(n):
                dve.wait_ge(xT4, n)
                signal(dve, nc.vector.reduce_sum(xsum[:, :], xT_d[:, :, :], axis=AX.X), xsum_ready, n)

            def choose(n):
                dve.wait_ge(logit_ps, n)
                link_d(nc.vector.reduce_max(lmax[:, 0:1], psum_z[0:T, 1, 0:NE], axis=AX.X), n)
                link_d(ts(sel_f[:, 0:2], psum_z[0:1, 1, 0:2], lmax[0:1, 0:1], None, ALU.is_ge), n)
                signal(dve, ts(lmax[:, 1:2], lmax[:, 0:1], -1.0 / L, None, ALU.mult), lmax_ready, n)
                ts(sel_f[:, 2:3], sel_f[:, 0:1], -1.0, 1.0, ALU.mult, ALU.add)
                link_d(ts(sel_f[:, 3:4], sel_f[:, 1:2], -1.0, 2.0, ALU.mult, ALU.add), n)
                signal(dve, tt(sel[:, :], sel_f[:, 2:3], sel_f[:, 3:4], ALU.mult), sel_ready, n)

            def chosen_p(n):
                dve.wait_ge(lexp_ready, n)
                link_d(nc.vector.reciprocal(route_w[:, :], lsum[:, :]), n)

            def ffn_out(n):
                dve.wait_ge(ffn_ps, n)
                dve.wait_ge(expert_loaded, n * 64)
                if not (isinstance(n, int) and n == 1):
                    dve.wait_ge(o_stored, n * 32 - 32)
                link_d(tt(flat(o), psum_z[0:T, 1, 0:2 * D], e_b2[:, :], ALU.add), n)
                signal(dve, stt(out=flat(o), in0=flat(o), scalar=route_w[:, :], in1=flat(h4_d), op0=ALU.mult, op1=ALU.add),
                       o_ready, n)

            phases = {"norm1": norm1, "norm1_apply": norm1_apply, "conv": conv, "kq": kq, "keys": keys,
                      "softplus": softplus, "angles": angles, "weighted": weighted, "trig": trig_, "match": match,
                      "gate": gate, "gated": gated, "h1": h1_, "norm2": norm2, "norm2_apply": norm2_apply,
                      "ffn_quant": ffn_norm, "out2": out2, "norm3": norm3, "norm3_apply": norm3_apply,
                      "w2_scale": w2, "w2": w2_add, "proj": proj, "norm4": norm4, "norm4_apply": norm4_apply,
                      "xsum": route, "choose": choose, "chosen_p": chosen_p, "ffn_out": ffn_out}
            for p in range(6):
                phases[f"y{p}"] = y(p)
            for j in range(2):
                phases[f"hid{j}"] = hid1(j)
            for u in range(SU):
                phases[f"score{u}"] = score_max(u)
                phases[f"exp{u}"] = denominators(u)
                if u % 2 == 0:
                    phases[f"mixed{u}"] = keep_mixed(u)
            run(dve, phases)


MIXER = ["norm1", "norm1_apply", "xT1", "z", "conv", "zT", "gate_t", "kq", "keys", "tanh", "softplus", "angles",
         "weighted", "trig"]
EXTRA = ["keep_x", "skip"]
READOUT = ["cum", "match", "gate", "gated", "gsT", "y0", "y1", "y2", "y3", "y4", "y5", "h1"]
QUANT = ["norm2", "norm2_apply", "xqT", "hid0", "hid1", "ffn_norm", "ffn_quant", "yqT", "out2"]
ATTENTION = (["norm3", "norm3_apply", "xT3", "qkv", "score0", "score1", "exp0"]
             + [p for u in range(2, NT // 2) for p in (f"score{u}", f"exp{u - 1}", f"mixed{u - 2}")]
             + [f"exp{NT // 2 - 1}", f"mixed{NT // 2 - 2}", f"mixed{NT // 2 - 1}", "w", "w2_scale", "wp", "w2", "proj"])
EXPERTS = ["norm4", "norm4_apply", "xT4", "xsum", "route", "choose", "chosen_p", "hidden0", "hidden1", "hidden2",
           "ffn_out"]
STAGES = 5
LAG = {p: k for k, stage in enumerate((MIXER + EXTRA, READOUT, QUANT, ATTENTION, EXPERTS)) for p in stage}


ORDER = [
    "norm3", "norm4", "cum", "norm3_apply", "norm4_apply", "xT3", "qkv", "match", "gate", "norm1", "xT4",
    "score0", "xsum", "norm1_apply", "score1", "exp0", "xT1", "norm2", "route", "choose", "score2", "exp1",
    "chosen_p", "mixed0", "norm2_apply", "gated", "exp2", "z", "score3", "score4", "mixed1", "conv", "exp3",
    "xqT", "mixed2", "exp4", "hid0", "score5", "zT", "mixed3", "hid1", "exp5", "score6", "ffn_norm", "mixed4",
    "exp6", "gate_t", "score7", "mixed5", "gsT", "ffn_quant", "exp7", "score8", "y0", "mixed6", "y1", "y2",
    "yqT", "score9", "out2", "exp8", "mixed7", "skip", "exp9", "hidden0", "mixed8", "hidden1", "mixed9",
    "hidden2", "kq", "w", "y3", "w2_scale", "wp", "keys", "tanh", "y4", "y5", "w2", "softplus", "angles",
    "weighted", "ffn_out", "trig", "proj", "h1", "keep_x"]
assert sorted(ORDER) == sorted(LAG)


def layout(x):
    import numpy as np

    def arr(name):
        return np.asarray(x[name])

    def rows(v, n=T):
        return np.broadcast_to(v.reshape(1, -1), (n, v.size))

    def twice(v):
        return rows(np.concatenate([v.reshape(-1)] * 2))

    def part(w, p):
        return w.reshape(w.shape[0] // p, p, w.shape[1]).transpose(1, 0, 2)

    d = {}
    px = arr("x").reshape(B, C, NH, PS, NH, PS).transpose(2, 4, 3, 5, 1, 0)
    px = px.reshape(NG, PP, 2, 128, C, B).transpose(0, 3, 1, 4, 2, 5).reshape(NG, 128, PP * C * 2 * B)
    mw = arr("L0_tok_merge_weights")
    mws = np.broadcast_to(mw.reshape(NG, 1, PP * C), (NG, 128, PP * C))
    d["pixels"] = np.concatenate([px, mws], axis=2)
    dw = arr("L0_tok_decode_weights").reshape(NG, PP, D, 2, 128)
    d["dec_w"] = dw.transpose(0, 4, 1, 3, 2).reshape(NG, 128, PP * 2 * D)
    one = np.ones((1, NP_), np.float32)
    stat = np.concatenate([mw.T, arr("L0_tok_merge_biases").reshape(1, NP_), one])
    stat = np.broadcast_to(stat[:, :, None], (5, NP_, B)).reshape(5, NG, PP * B)
    d["bias_s"] = stat.transpose(1, 0, 2)
    db = arr("L0_tok_decode_biases")
    mov = np.stack([db, db, db, np.ones((NP_, D), np.float32), arr("L0_tok_pos_embedding")[1:]])
    d["bias_m"] = mov.reshape(5, NG, PP * D).transpose(1, 0, 2)
    cls = np.stack([arr("cls_tok").reshape(D), arr("L0_tok_cls_embedding"), arr("L0_tok_pos_embedding")[0]])
    d["cls"] = np.broadcast_to(cls[None], (B, 3, D))
    d["W_in"] = part(arr("L0_attn_W_in"), HW)
    cw = arr("L0_attn_conv_w").T
    q0 = KH * HD + KH
    d["conv_w"] = np.stack([cw[0:HW], cw[HW:2 * HW], cw[q0:q0 + HW], cw[q0 + HW:q0 + 2 * HW]], axis=1)
    d["conv_ws"] = cw[KH * HD:q0]
    d["k_norm"] = twice(np.broadcast_to(arr("L0_attn_k_norm_w"), (KH, HD)))
    d["tanh_scale"] = twice(np.broadcast_to(arr("L0_attn_tanh_scale")[:, None], (KH, HD)))
    d["theta"] = twice(arr("L0_attn_theta_raw"))
    qn = arr("L0_attn_q_norm_w").reshape(NQ, 1, HD, 2)
    qn = np.broadcast_to(qn, (NQ, 2, HD, 2)).transpose(3, 0, 1, 2)
    wi = np.broadcast_to(arr("L0_attn_w_int_raw").reshape(1, D), (2, D))
    d["q_norm"] = rows(np.concatenate([qn[0].reshape(-1)] * 2 + [qn[1].reshape(-1)] * 2)).reshape(T, 2, 2 * D)
    d["w_int"] = rows(np.concatenate([wi[0]] * 4)).reshape(T, 2, 2 * D)
    d["score_w"] = twice(arr("L0_attn_score_scale"))
    d["score_b"] = twice(arr("L0_attn_score_bias"))
    d["decay"] = twice(arr("L0_attn_decay_slopes"))
    left = np.arange(L - 1, -1, -1, dtype=np.float32).reshape(2, T).T
    d["dist"] = np.repeat(left, KH, axis=1)
    d["W_gate"] = arr("L0_attn_W_gate")
    ro, sk = arr("L0_attn_W_readout"), arr("L0_attn_W_skip")
    gn, hs = arr("L0_attn_gnorm_w").reshape(KH, 2 * HD), arr("L0_attn_highway_scale")
    wr = np.zeros((112, 6, 2 * HW), np.float32)
    wf = np.ones((112, 6, 2 * HW), np.float32)
    for k in range(KH):
        p, e = k // 2, k % 2
        for half in range(2):
            c0, s0 = half * HW + e * FS, half * FS
            wr[32 * e:32 * e + 32, p, c0:c0 + FS] = ro[k, :, s0:s0 + FS]
            wf[32 * e:32 * e + 32, p, c0:c0 + FS] = gn[k][:, None]
            wr[64:112, p, c0:c0 + FS] = sk[:, k * HW + s0:k * HW + s0 + FS]
            wf[64:112, p, c0:c0 + FS] = hs[k]
    d["W_read"], d["W_read_f"] = wr, wf
    d["W_out"] = part(arr("L0_attn_W_out"), HW)
    d["ffn_w1"] = part(arr("L0_ffn_w_in").T, HW)
    d["ffn_w2"] = part(arr("L0_ffn_w_out").T, 128)
    d["g_in"] = twice(arr("L0_ffn_g_in"))
    d["g_out"] = rows(arr("L0_ffn_g_out"))
    d["W_qkv"] = part(arr("L1_attn_W_qkv"), HW)
    d["mix_l"] = part(np.repeat(arr("L1_attn_W_l"), HD, axis=0), HW)
    mw2 = np.zeros((SR + 1, KH, NB), np.float32)
    for n in range(NB):
        mw2[n:SR:NB, :, n] = arr("L1_attn_W_w")
    mw2[SR] = arr("L1_attn_b_w")[:, None]
    d["mix_w"] = mw2.reshape(SR + 1, SR)
    d["b_l"] = np.tile(np.repeat(arr("L1_attn_b_l"), NB), NT).reshape(1, NT * SR)
    d["lam"] = np.repeat(arr("L1_attn_lamb").reshape(3, 4), 32, axis=1).T
    wp = np.zeros((3, 4, 32, D), np.float32)
    wp[:, :, 0:HD, :] = arr("L1_attn_W_proj").reshape(3, 4, HD, D)
    d["W_proj"] = wp.reshape(3, 128, D).transpose(1, 0, 2)
    d["b_proj"] = twice(arr("L1_attn_b_proj"))
    d["W_route"] = part(arr("L1_ffn_Wg").T, HW)
    d["W1"] = arr("L1_ffn_W1").reshape(NE, 2, HW, FM).transpose(0, 2, 1, 3).reshape(NE, HW, 2 * FM)
    d["W2"] = arr("L1_ffn_W2").reshape(NE, 6, 128, D).transpose(0, 2, 1, 3).reshape(NE, 128, 6 * D)
    d["b1"] = arr("L1_ffn_b1").reshape(NE, 6, 128).transpose(0, 2, 1)
    b2 = arr("L1_ffn_b2")
    d["b2"] = np.broadcast_to(np.concatenate([b2, b2], axis=1)[:, None, :], (NE, T, 2 * D))
    d["upper"] = np.triu(np.ones((T, T), np.float32))
    d["ident"] = np.eye(128, dtype=np.float32)
    return {k: np.ascontiguousarray(v) for k, v in d.items()}


def kernel(**inputs):
    import concourse.bacc as _bacc
    from concourse.bass_utils import run_bass_kernel_spmd as _run

    arrays = {f"in_{k}": v for k, v in layout(inputs).items()}
    nc = _bacc.Bacc("TRN2", target_bir_lowering=False, num_devices=1)
    a = {k[3:]: nc.dram_tensor(k, v.shape, mybir.dt.from_np(v.dtype), kind="ExternalInput").ap()
         for k, v in arrays.items()}
    out = nc.dram_tensor("out_tokens", (B, L, D), mybir.dt.float32, kind="ExternalOutput").ap()
    vit_program(nc, a, out)
    r = _run(nc, [arrays], core_ids=[0])
    return r.results[0]["out_tokens"]
```

```python
import concourse.bass as bass
from concourse import mybir
from contextlib import ExitStack

B, C, IMG, PS = 64, 3, 224, 16
NH = IMG // PS
NP_ = NH * NH
L = NP_ + 2
D = 192
T = L // 2
HW = 96
KH, HD = 12, 16
NQ = 6
TAPS = 4
GR = 32
CONV = KH * HD + KH + NQ * HD * 2
SKIP = D // 4
FS = 48
FH = 512
FM = 768
NE = 3
PP = 7
NG = NP_ // PP
NB = 10
NT = 20
NPAD = NB * NT
QT = 4
SR = KH * NB
EPS_LN = 1e-5
EPS_RMS = 1e-6
EPS_Q = 1e-5
MAGIC = 12582912.0
THETA_MIN, THETA_MAX = 0.001, 3.0
LOG1P_TERMS = 7
SOFTPLUS_STEPS = LOG1P_TERMS + 7


def vit_program(nc, a, out, images=B):
    f32, bf16, i32 = mybir.dt.float32, mybir.dt.bfloat16, mybir.dt.int32
    ALU, ACT, AX = mybir.AluOpType, mybir.ActivationFunctionType, mybir.AxisListType

    h_dram = nc.dram_tensor("h_tokens", (B, L, D), f32, kind="Internal").ap()

    ctx = ExitStack()
    with ctx:
        def sb(name, shape, dt=f32):
            return ctx.enter_context(nc.sbuf_tensor(name, list(shape), dt))

        def sems(names):
            return [ctx.enter_context(nc.semaphore(n)) for n in names.split()]

        ident = sb("ident", (128, 128))
        ident_b = sb("ident_b", (128, 128), bf16)
        upper = sb("upper", (T, T))
        ones = sb("ones", (128, 128))
        half_pi = sb("half_pi", (128, 1))
        neg_half = sb("neg_half", (128, 32))
        w_in = sb("w_in", (HW, 2, CONV + SKIP))
        w_heads = sb("w_heads", (HW, 2, GR + KH))
        conv_w = sb("conv_w", (HW, 4, TAPS))
        conv_ws = sb("conv_ws", (KH, TAPS))
        k_norm = sb("k_norm", (T, 2 * D))
        tanh_scale = sb("tanh_scale", (T, 2 * D))
        theta = sb("theta", (T, 2 * D))
        q_w = sb("q_w", (T, 2, 2 * D))
        score_w = sb("score_w", (T, 2 * KH))
        score_b = sb("score_b", (T, 2 * KH))
        time_w = sb("time_w", (T, 2 * KH))
        dist = sb("dist", (T, 2 * KH))
        w_gate = sb("w_gate", (GR + KH, 2 * D))
        w_read = sb("w_read", (112, 6, 2 * HW))
        w_out = sb("w_out", (HW, 6, D))
        fq1 = sb("fq1", (HW, 2, 2 * FH), bf16)
        fq2 = sb("fq2", (128, 4, D), bf16)
        g_in = sb("g_in", (T, 2 * D))
        g_out = sb("g_out", (T, FH))
        w_mean = sb("w_mean", (128, 2))
        w_abs = sb("w_abs", (128, 2))
        w_qkv = sb("w_qkv", (HW, 2, 3 * D))
        mix_l = sb("mix_l", (HW, 2, KH))
        mix_w = sb("mix_w", (SR + 1, SR))
        lam = sb("lam", (128, 3))
        lam_1 = sb("lam_1", (128, 3))
        lam_2 = sb("lam_2", (128, 3))
        w_proj = sb("w_proj", (128, 3, D))
        b_proj = sb("b_proj", (T, 2 * D))
        w_route = sb("w_route", (HW, 2, NE))

        psum = ctx.enter_context(nc.psum_tensor("psum", [128, 8, 512], f32))
        psum_a, psum_c, psum_z = psum[:, 0:3, :], psum[:, 3:6, :], psum[:, 6:8, :]

        (const_loaded, const_memset, setup_v, setup_a, setup_pe, setup_done_a) = sems(
            "const_loaded const_memset setup_v setup_a setup_pe setup_done_a")

        tok = ctx.enter_context(ExitStack())

        def tok_sb(name, shape, dt=f32):
            return tok.enter_context(nc.sbuf_tensor("tok_" + name, list(shape), dt))
        XG = PP * C * 2 * B
        xg = [tok_sb(f"xg{k}", (128, XG + PP * C)) for k in range(2)]
        wg = [tok_sb(f"wg{k}", (128, PP, 2, D)) for k in range(2)]
        bs = [tok_sb(f"bs{k}", (5, PP, B)) for k in range(2)]
        bm = [tok_sb(f"bm{k}", (5, PP, D)) for k in range(2)]
        xm = [tok_sb(f"xm{k}", (128, PP, 2 * B)) for k in range(2)]
        hg = [tok_sb(f"hg{k}", (B, PP, D)) for k in range(2)]
        tok_pixels, tok_weights, tok_merged, tok_product, tok_ready, tok_stored = (
            sems(f"{name}0 {name}1") for name in
            ("tok_pixels", "tok_weights", "tok_merged", "tok_product", "tok_ready", "tok_stored"))
        tok_step, = sems("tok_step")

        def load_pixels(sp, g, k):
            sp.dma_start(xg[k][:, :], a["pixels"][bass.ds(g, 1)].rearrange("o p n -> (o p) n")).then_inc(tok_pixels[k], 16)

        def load_weights(sp, g, k):
            sp.dma_start(wg[k][:, :, :].rearrange("p a b c -> p (a b c)"),
                         a["dec_w"][bass.ds(g, 1)].rearrange("o p n -> (o p) n")).then_inc(tok_weights[k], 16)
            sp.dma_start(bs[k][:, :, :].rearrange("p a b -> p (a b)"),
                         a["bias_s"][bass.ds(g, 1)].rearrange("o p n -> (o p) n")).then_inc(tok_weights[k], 16)
            sp.dma_start(bm[k][:, :, :].rearrange("p a b -> p (a b)"),
                         a["bias_m"][bass.ds(g, 1)].rearrange("o p n -> (o p) n")).then_inc(tok_weights[k], 16)

        with ExitStack() as tmp:
            def sbt(name, shape, dt=f32):
                return tmp.enter_context(nc.sbuf_tensor("init_" + name, list(shape), dt))
            w_read_f = sbt("w_read_f", (112, 6, 2 * HW))
            wf1 = sbt("wf1", (HW, 2, 2 * FH))
            wf2 = sbt("wf2", (128, 4, D))
            q_int = sbt("q_int", (T, 2, 2 * D))
            decay = sbt("decay", (T, 2 * KH))
            sp_u = sbt("sp_u", (T, 2 * KH))
            sp_z = sbt("sp_z", (T, 2 * KH))
            sp_z2 = sbt("sp_z2", (T, 2 * KH))
            sp_p = sbt("sp_p", (T, 2 * KH))
            scratch = sbt("scratch", (128, 2 * 2 * FH))
            rscale = sbt("rscale", (128, 2))
            cls = sbt("cls", (B, 3, D))

            loads = [(w_in, "W_in"), (w_heads, "W_heads"), (conv_w, "conv_w"), (conv_ws, "conv_ws"), (k_norm, "k_norm"),
                     (tanh_scale, "tanh_scale"), (theta, "theta"), (q_w, "q_norm"), (q_int, "w_int"),
                     (score_w, "score_w"), (score_b, "score_b"), (dist, "dist"), (decay, "decay"),
                     (w_read, "W_read"), (w_read_f, "W_read_f"), (w_out, "W_out"),
                     (wf1, "ffn_w1"), (wf2, "ffn_w2"), (g_in, "g_in"), (g_out, "g_out"),
                     (w_qkv, "W_qkv"), (mix_l, "mix_l"), (mix_w, "mix_w"), (lam, "lam"),
                     (w_proj, "W_proj"), (b_proj, "b_proj"), (w_route, "W_route"), (cls, "cls"),
                     (upper, "upper"), (ident, "ident")]
            LOADED = 16 * len(loads) + 16
            cls_added, cls_stored = sems("cls_added cls_stored")
            block = tmp.enter_context(nc.Block())

            @block.sync
            def _(sp):
                for tile, name in loads:
                    full = tuple(slice(None) for _ in tile.shape)
                    sp.dma_start(tile[full], a[name]).then_inc(const_loaded, 16)
                sp.dma_start(w_gate[GR:GR + KH, :], a["W_gate"]).then_inc(const_loaded, 16)
                for k in range(2):
                    load_pixels(sp, k, k)
                    load_weights(sp, k, k)
                sp.wait_ge(cls_added, 1)
                sp.dma_start(h_dram[:, 0:2, :], cls[:, 0:2, :]).then_inc(cls_stored, 16)
                sp.wait_ge(cls_stored, 16)

            @block.gpsimd
            def _(pool):
                nc.gpsimd.memset(ones[:, :], 1.0)
                nc.gpsimd.memset(half_pi[:, :], 1.5707963267948966)
                nc.gpsimd.memset(neg_half[:, :], -0.5).then_inc(const_memset, 1)

            @block.tensor
            def _(pe):
                pe.wait_ge(const_memset, 1)
                pe.wait_ge(setup_a, 5)
                nc.tensor.matmul(psum_a[:, 0, 0:1], ones[0:HW, :], w_abs[0:HW, 0:1], start=True, stop=True)
                nc.tensor.matmul(psum_a[:, 0, 1:2], ones[:, :], w_abs[:, 1:2], start=True,
                                 stop=True).then_inc(setup_pe, 1)

            @block.scalar
            def _(act):
                act.wait_ge(const_loaded, LOADED)
                nc.scalar.activation(sp_u[:, :], decay[:, :], ACT.Abs).then_inc(setup_a, 1)
                act.wait_ge(setup_a, 1)
                nc.scalar.activation(sp_u[:, :], sp_u[:, :], ACT.Exp, scale=-1.0).then_inc(setup_a, 1)
                nc.scalar.activation(theta[:, :], theta[:, :], ACT.Tanh, scale=0.5).then_inc(setup_a, 1)
                act.wait_ge(setup_a, 3)
                nc.scalar.activation(scratch[0:HW, :], wf1[:, :, :].rearrange("p k n -> p (k n)"), ACT.Abs,
                                     accum_out=w_abs[0:HW, 0:1]).then_inc(setup_a, 1)
                act.wait_ge(setup_a, 4)
                nc.scalar.activation(scratch[:, 0:4 * D], wf2[:, :, :].rearrange("p k n -> p (k n)"), ACT.Abs,
                                     accum_out=w_abs[:, 1:2]).then_inc(setup_a, 1)
                act.wait_ge(setup_v, 1)
                nc.scalar.activation(q_int[:, :, :], q_int[:, :, :], ACT.Exp).then_inc(setup_a, 1)
                act.wait_ge(setup_done_a, 1)
                nc.scalar.activation(sp_u[:, :], time_w[:, :], ACT.Exp).then_inc(setup_a, 1)

            @block.vector
            def _(dve):
                count = [0]

                def link(ins):
                    count[0] += 1
                    ins.then_inc(setup_v, 1)
                    dve.wait_ge(setup_v, count[0])

                dve.wait_ge(const_loaded, LOADED)
                link(nc.vector.tensor_scalar(q_int[:, :, :], q_int[:, :, :], -5.0, 5.0, ALU.max, ALU.min))
                nc.vector.tensor_tensor(cls[:, 1, :], cls[:, 1, :], cls[:, 2, :], ALU.add).then_inc(cls_added, 1)
                nc.vector.tensor_copy(ident_b[:, :], ident[:, :])
                nc.vector.tensor_tensor(w_read[:, :, :], w_read[:, :, :], w_read_f[:, :, :], ALU.mult)
                nc.vector.tensor_scalar(lam_1[:, :], lam[:, :], -2.0, 1.0, ALU.mult, ALU.add)
                link(nc.vector.tensor_scalar(lam_2[:, :], lam[:, :], 3.0, None, ALU.mult))
                dve.wait_ge(setup_a, 3)
                link(nc.vector.tensor_scalar(theta[:, :], theta[:, :], 0.5, 0.5, ALU.mult, ALU.add))
                link(nc.vector.tensor_scalar(theta[:, :], theta[:, :], THETA_MAX - THETA_MIN, THETA_MIN,
                                             ALU.mult, ALU.add))

                def log1p_u():
                    link(nc.vector.tensor_scalar(sp_p[:, :], sp_u[:, :], 2.0, None, ALU.add))
                    link(nc.vector.reciprocal(sp_p[:, :], sp_p[:, :]))
                    link(nc.vector.tensor_tensor(sp_z[:, :], sp_u[:, :], sp_p[:, :], ALU.mult))
                    link(nc.vector.tensor_tensor(sp_z2[:, :], sp_z[:, :], sp_z[:, :], ALU.mult))
                    link(nc.vector.tensor_scalar(sp_p[:, :], sp_z2[:, :], 2.0 / (2 * LOG1P_TERMS - 1), None, ALU.mult))
                    for k in range(LOG1P_TERMS - 2, 0, -1):
                        link(nc.vector.scalar_tensor_tensor(out=sp_p[:, :], in0=sp_p[:, :], scalar=2.0 / (2 * k + 1),
                                                            in1=sp_z2[:, :], op0=ALU.add, op1=ALU.mult))
                    link(nc.vector.scalar_tensor_tensor(out=sp_p[:, :], in0=sp_p[:, :], scalar=2.0,
                                                        in1=sp_z[:, :], op0=ALU.add, op1=ALU.mult))

                log1p_u()
                link(nc.vector.scalar_tensor_tensor(out=sp_p[:, :], in0=decay[:, :], scalar=0.0, in1=sp_p[:, :],
                                                    op0=ALU.max, op1=ALU.add))
                nc.vector.scalar_tensor_tensor(out=time_w[:, :], in0=sp_p[:, :], scalar=-1.0, in1=dist[:, :],
                                               op0=ALU.mult, op1=ALU.mult).then_inc(setup_done_a, 1)
                dve.wait_ge(setup_a, 6)
                link(nc.vector.tensor_tensor(q_w[:, :, :], q_w[:, :, :], q_int[:, :, :], ALU.mult))
                dve.wait_ge(setup_a, 7)
                log1p_u()
                link(nc.vector.tensor_copy(time_w[:, :], sp_p[:, :]))
                dve.wait_ge(setup_pe, 1)
                nc.vector.tensor_scalar(w_mean[:, 0:1], psum_a[:, 0, 0:1], 1.0 / (2 * FH * D), EPS_Q, ALU.mult, ALU.max)
                link(nc.vector.tensor_scalar(w_mean[:, 1:2], psum_a[:, 0, 1:2], 1.0 / (FH * D), EPS_Q, ALU.mult, ALU.max))
                link(nc.vector.reciprocal(rscale[:, :], w_mean[:, :]))
                for wf, wq, rows, n in ((wf1, fq1, HW, 0), (wf2, fq2, 128, 1)):
                    link(nc.vector.tensor_scalar(wf[:, :, :], wf[:, :, :], rscale[0:rows, n:n + 1], MAGIC,
                                                 ALU.mult, ALU.add))
                    link(nc.vector.tensor_scalar(wf[:, :, :], wf[:, :, :], MAGIC, 1.0, ALU.subtract, ALU.min))
                    link(nc.vector.tensor_scalar(wq[:, :, :], wf[:, :, :], -1.0, None, ALU.max))

        with ExitStack() as tmp:
            block = tmp.enter_context(nc.Block())
            PAIRS = NG // 2

            @block.sync
            def _(sp):
                with sp.Fori(1, PAIRS) as i:
                    for k in range(2):
                        sp.wait_ge(tok_merged[k], i)
                        load_pixels(sp, i * 2 + k, k)
                        sp.wait_ge(tok_product[k], i)
                        load_weights(sp, i * 2 + k, k)

            @block.vector
            def _(dve):
                def merge(i, k):
                    dve.wait_ge(tok_pixels[k], i * 16 + 16)
                    px = xg[k][:, 0:XG].rearrange("p (n c m) -> p n c m", n=PP, c=C)
                    mw = xg[k][:, XG:XG + PP * C].unsqueeze(2).broadcast_to([128, PP * C, 2 * B])
                    flat = xg[k][:, 0:XG].rearrange("p (n m) -> p n m", m=2 * B)
                    nc.vector.tensor_tensor(flat, flat, mw, ALU.mult).then_inc(tok_step, 1)
                    dve.wait_ge(tok_step, i * 4 + (2 * k + 1))
                    if not (isinstance(i, int) and i == 0):
                        dve.wait_ge(tok_product[k], i)
                    nc.vector.tensor_tensor(xm[k][:, :, :], px[:, :, 0, :], px[:, :, 1, :], ALU.add).then_inc(tok_step, 1)
                    dve.wait_ge(tok_step, i * 4 + (2 * k + 2))
                    nc.vector.tensor_tensor(xm[k][:, :, :], xm[k][:, :, :], px[:, :, 2, :],
                                            ALU.add).then_inc(tok_merged[k], 1)

                for k in range(2):
                    merge(0, k)
                with dve.Fori(1, PAIRS) as i:
                    for k in range(2):
                        merge(i, k)

            @block.tensor
            def _(pe):
                def products(i, k):
                    pe.wait_ge(tok_weights[k], i * 48 + 48)
                    pe.wait_ge(tok_merged[k], i + 1)
                    bank = psum[:, 4 * k:4 * k + 4, :]
                    for n in range(PP):
                        o = bank[0:B, n // 2, (n % 2) * D:(n % 2 + 1) * D]
                        for c in range(2):
                            nc.tensor.matmul(o, xm[k][:, n, c * B:(c + 1) * B], wg[k][:, n, c, :],
                                             start=(c == 0), stop=False)
                        last = nc.tensor.matmul(o, bs[k][:, n, :], bm[k][:, n, :], start=False, stop=True)
                    last.then_inc(tok_product[k], 1)

                for k in range(2):
                    products(0, k)
                with pe.Fori(1, PAIRS) as i:
                    for k in range(2):
                        pe.wait_ge(tok_ready[k], i)
                        products(i, k)

            @block.scalar
            def _(act):
                def evacuate(i, k):
                    act.wait_ge(tok_product[k], i + 1)
                    bank = psum[:, 4 * k:4 * k + 4, :]
                    nc.scalar.activation(hg[k][:, 0:6, :].rearrange("p (a b) n -> p a (b n)", b=2),
                                         bank[0:B, 0:3, 0:2 * D], ACT.Copy)
                    nc.scalar.activation(hg[k][:, 6, :], bank[0:B, 3, 0:D], ACT.Copy).then_inc(tok_ready[k], 1)
                    act.wait_ge(tok_ready[k], i + 1)
                    act.dma_start(h_dram[:, bass.ds((i * 2 + k) * PP + 2, PP), :], hg[k][:, :, :]).then_inc(tok_stored[k], 16)

                for k in range(2):
                    evacuate(0, k)
                with act.Fori(1, PAIRS) as i:
                    for k in range(2):
                        act.wait_ge(tok_stored[k], i * 16)
                        evacuate(i, k)
                for k in range(2):
                    act.wait_ge(tok_stored[k], 16 * PAIRS)

        tok.close()


        x = sb("x", (T, 2, D))
        x_kept = sb("x_kept", (T, 2, D))
        xn = sb("xn", (T, 2, D))
        xT = sb("xT", (HW, 2, L))
        zc = sb("zc", (HW, 4, L))
        zs = sb("zs", (KH, L))
        gT = sb("gT", (GR + KH, L))
        skip_in = sb("skip_in", (T, 2, SKIP))
        gs = sb("gs", (T, 2, 6, 112))
        zk = sb("zk", (T, 2, D + KH))
        zq = sb("zq", (T, 2, D))
        var = sb("var", (T, 2 * KH + 2))
        rs = sb("rs", (T, 2 * KH + 2))
        score = sb("score", (T, 2, KH))
        sp_u = sb("sp_u", (T, 2 * KH))
        sp_z = sb("sp_z", (T, 2 * KH))
        sp_z2 = sb("sp_z2", (T, 2 * KH))
        sp_p = sb("sp_p", (T, 2 * KH))
        kv = sb("kv", (T, 2, D))
        kvw = sb("kvw", (T, 2, D))
        phi = sb("phi", (T, 2 * D))
        sin_p = sb("sin_p", (T, 2, D))
        cos_p = sb("cos_p", (T, 2, D))
        stack = sb("stack", (T, 2, 2 * D + KH))
        den = sb("den", (T, 2, KH))
        s_re = sb("s_re", (T, 2 * D))
        s_im = sb("s_im", (T, 2 * D))
        qx_re = sb("qx_re", (T, 2 * D))
        qx_im = sb("qx_im", (T, 2 * D))
        m_a = sb("m_a", (T, 2 * D))
        m_b = sb("m_b", (T, 2 * D))
        phi_abs, sq = m_a, m_b
        oc = sb("oc", (T, 2, 2 * D))
        gate_t = sb("gate_t", (T, 2, 2 * D))
        sum_g = sb("sum_g", (T, 2))
        rs_g = sb("rs_g", (T, 2))
        gsT = sb("gsT", (112, 6, L))
        y_silu_t = sb("y_silu_t", (HW, 3, L))
        yT = sb("yT", (HW, 6, L))
        h1 = sb("h1", (T, 2, D))
        stats = sb("stats", (T, 2, 6))
        mv = sb("mv", (T, 2, 2))
        rstd = sb("rstd", (T, 2))
        n2_a = sb("n2_a", (T, 2))
        n2_b = sb("n2_b", (T, 2))
        amax = sb("amax", (T, 2))
        qscale = sb("qscale", (T, 2))
        deq1 = sb("deq1", (T, 2))
        deq2 = sb("deq2", (T, 2))
        xqb = sb("xqb", (T, 2, D), bf16)
        xqT = sb("xqT", (HW, 4, 100), bf16)
        sg_f = sb("sg_f", (T, 2, FH))
        y_f = sb("y_f", (T, 2, FH))
        sum_f = sb("sum_f", (T, 2))
        f_a = sb("f_a", (T, 2))
        f_b = sb("f_b", (T, 2))
        yqb = sb("yqb", (T, 2, FH), bf16)
        yqT = sb("yqT", (128, 8, 100), bf16)
        h1_b = sb("h1_b", (T, 2, D))
        xn_b = sb("xn_b", (T, 2, D))
        stats_b = sb("stats_b", (T, 2, 6))
        mv_b = sb("mv_b", (T, 2, 2))
        rstd_b = sb("rstd_b", (T, 2))
        h2 = sb("h2", (T, 2, D))
        h3 = sb("h3", (T, 2, D))
        h4 = sb("h4", (T, 2, D))
        stats_c = sb("stats_c", (T, 2, 6))
        mv_c = sb("mv_c", (T, 2, 2))
        rstd_c = sb("rstd_c", (T, 2))
        xn_c = sb("xn_c", (T, 2, D))
        xT_c = sb("xT_c", (HW, 2, L))
        qT = sb("qT", (HW, 2, NPAD))
        kT = sb("kT", (HW + 1, 2, L))
        vp = sb("vp", (T, 2, KH, 32))
        qm = sb("qm", (HW + 1, 2, NT, SR))
        nmax = sb("nmax", (SR, 2, NT // 2))
        expo = [sb(f"expo{k}", (SR + 1, 2, L)) for k in range(2)]
        zsum = sb("zsum", (SR, NT // 2, 2))
        rz = sb("rz", (SR, NT // 2, 2))
        wz = [sb(f"wz{k}", (SR + 1, 2, SR)) for k in range(2)]
        at = sb("at", (T, NT, 2, SR))
        wT = sb("wT", (128, 3, NPAD))
        wp = sb("wp", (T, 2, 3 * 128))
        o2 = sb("o2", (128, 3, NPAD))
        h4_d = sb("h4_d", (T, 2, D))
        stats_d = sb("stats_d", (T, 2, 6))
        mv_d = sb("mv_d", (T, 2, 2))
        rstd_d = sb("rstd_d", (T, 2))
        xn_d = sb("xn_d", (T, 2, D))
        xT_d = sb("xT_d", (HW, 2, L))
        xsum = sb("xsum", (HW, 2))
        lmax = sb("lmax", (T, 2))
        lexp = sb("lexp", (T, NE))
        lsum = sb("lsum", (T, 1))
        route_w = sb("route_w", (T, 1))
        sel_f = sb("sel_f", (1, 4))
        sel = sb("sel", (1, 1), i32)
        e_w1 = sb("e_w1", (HW, 2, FM))
        e_w2 = sb("e_w2", (128, 6, D))
        e_b1 = sb("e_b1", (128, 6))
        e_b2 = sb("e_b2", (T, 2 * D))
        hT = sb("hT", (128, 6, L))
        o = sb("o", (T, 2, D))

        (x_loaded, x_free, skip_ready, stat1, rstd1, xn1, xT1_ps, xT1, z_ps, z_tap, conv_done, zT_ps, silu_done, kq_var, kq_rs,
         exp_u, tanh_in, tanh_out, phi_ready, trig, stack_ready, gate_ps, cum_ps, gate_done, g_ready, g_sum,
         g_rs, gs_ready, gsT_ps, gsT_ready, y_ps, y_silu, y_ready, out1_ps, h1_ready) = sems(
            "x_loaded x_free skip_ready stat1 rstd1 xn1 xT1_ps xT1 z_ps z_tap conv_done zT_ps silu_done kq_var kq_rs "
            "exp_u tanh_in tanh_out phi_ready trig stack_ready gate_ps cum_ps gate_done g_ready g_sum "
            "g_rs gs_ready gsT_ps gsT_ready y_ps y_silu y_ready out1_ps h1_ready")
        (stat2, norm2_s, xq_ready, xqT_ps, xqT_ready, h_ps, sg_ready, yf_ready, yf_sum, yf_s, yq_ready,
         yqT_ps, yqT_ready, out2_ps, h2_ready) = sems(
            "stat2 norm2_s xq_ready xqT_ps xqT_ready h_ps sg_ready yf_ready yf_sum yf_s yq_ready "
            "yqT_ps yqT_ready out2_ps h2_ready")
        (stat3, rstd3, xn3, xT3_ps, xT3, qkv_ps, q_ready, v_ready, qm_ready, s_ps, s_max, exp_done,
         rz_ready, wz_ready, at_ps, at_ready, w_ps, w_ready, wT_ps, wp_ready, w2_ps, o2_ready, proj_ps, h4_ready,
         stat4, rstd4, xn4, xT4_ps, xT4, xsum_ready, logit_ps, lmax_ready, lexp_ready, sel_ready,
         expert_loaded, hid_ps, hid_ready, ffn_ps, o_ready, o_stored) = sems(
            "stat3 rstd3 xn3 xT3_ps xT3 qkv_ps q_ready v_ready qm_ready s_ps s_max exp_done "
            "rz_ready wz_ready at_ps at_ready w_ps w_ready wT_ps wp_ready w2_ps o2_ready proj_ps h4_ready "
            "stat4 rstd4 xn4 xT4_ps xT4 xsum_ready logit_ps lmax_ready lexp_ready sel_ready "
            "expert_loaded hid_ps hid_ready ffn_ps o_ready o_stored")
        v_mix, v_read, v_ffn, v_att, v_exp, a_mix, a_ffn, p_mix, p_read, p_ffn, p_att, p_exp, pad_set, pad_loaded = sems(
            "v_mix v_read v_ffn v_att v_exp a_mix a_ffn p_mix p_read p_ffn p_att p_exp pad_set pad_loaded")
        VA, VR, VB, VC, VD, AA, AB, PA, PR, PB, PC, PE = 24, 8, 15, 4, 7, 2, 1, 2, 2, 10, 1, 1

        block = ctx.enter_context(nc.Block())
        SU = NT // 2

        def run(eng, phases):
            def step(i):
                for phase in ORDER:
                    n = i - LAG[phase]
                    if phase in phases and not (isinstance(n, int) and not 1 <= n <= images):
                        phases[phase](n)

            for i in range(1, STAGES + 1):
                step(i)
            with eng.Fori(STAGES + 1, images) as i:
                step(i)
            for i in range(images, images + STAGES):
                step(i)
            for count, steps in counts:
                assert count[0] == steps * (STAGES + 2), [c[0] / (STAGES + 2) for c, _ in counts]
            counts.clear()

        counts = []

        def linked(eng, sem, steps):
            count = [0]

            def mark(ins):
                count[0] += 1
                ins.then_inc(sem, 1)

            def done(n):
                eng.wait_ge(sem, n * steps + ((count[0] - 1) % steps + 1 - steps))

            def link(ins, n):
                mark(ins)
                done(n)
            counts.append((count, steps))
            return link, mark, done

        def own_wait(eng):
            eng.nop(nofuse=True)

        @block.sync
        def _(sp):
            sp.wait_ge(pad_set, 3)
            for k in range(2):
                for t in range(2):
                    sp.dma_start(wz[k][:, t, :], mix_w[:, :]).then_inc(pad_loaded, 16)
            sp.dma_start(qm[HW:HW + 1, 1, :, :].rearrange("p t r -> p (t r)"), a["b_l"]).then_inc(pad_loaded, 16)

            def load(n):
                for j in range(2):
                    sp.dma_start(x[:, j, :], h_dram[bass.ds(n - 1, 1), j * T:(j + 1) * T, :]
                                 .rearrange("o p d -> (o p) d")).then_inc(x_loaded, 16)

            def load_next(n):
                sp.wait_ge(x_free, n)
                sp.wait_ge(xn1, n)
                if not (isinstance(n, int) and n >= images):
                    load(n + 1)

            def experts(n):
                sp.wait_ge(sel_ready, n)
                own_wait(sp)
                e = sp.value_load(sel[0:1, 0:1], min_val=0, max_val=NE - 1)
                sp.dma_start(e_w1[:, :, :].rearrange("p a b -> p (a b)"),
                             a["W1"][bass.ds(e, 1)].rearrange("o p n -> (o p) n")).then_inc(expert_loaded, 16)
                sp.dma_start(e_w2[:, :, :].rearrange("p a b -> p (a b)"),
                             a["W2"][bass.ds(e, 1)].rearrange("o p n -> (o p) n")).then_inc(expert_loaded, 16)
                sp.dma_start(e_b1[:, :], a["b1"][bass.ds(e, 1)].rearrange("o p n -> (o p) n")).then_inc(expert_loaded, 16)
                sp.dma_start(e_b2[:, :], a["b2"][bass.ds(e, 1)].rearrange("o p n -> (o p) n")).then_inc(expert_loaded, 16)

            def store(n):
                sp.wait_ge(o_ready, n)
                for j in range(2):
                    sp.dma_start(out[bass.ds(n - 1, 1), j * T:(j + 1) * T, :].rearrange("o p d -> (o p) d"),
                                 o[:, j, :]).then_inc(o_stored, 16)

            load(1)
            sp_phases = {"keep_x": load_next, "choose": experts, "ffn_out": store}
            run(sp, sp_phases)
            sp.wait_ge(o_stored, 32 * images)

        @block.gpsimd
        def _(pool):
            nc.gpsimd.memset(kT[:, :, :], 1.0)
            nc.gpsimd.memset(vp[:, :, :, :], 0.0)
            nc.gpsimd.memset(qm[:, :, :, :], 0.0)
            nc.gpsimd.memset(qT[:, :, :], 0.0).then_inc(pad_set, 1)
            for k in range(2):
                nc.gpsimd.memset(expo[k][:, :, :], 1.0).then_inc(pad_set, 1)
            pool.wait_ge(pad_set, 3)
            link_a, link_r, link_b, link_c, link_d = (linked(pool, sem, steps)[0] for sem, steps in
                                              ((p_mix, PA), (p_read, PR), (p_ffn, PB), (p_att, PC), (p_exp, PE)))

            def power(out_, in_, w):
                return nc.gpsimd.tensor_tensor(out_, in_, neg_half[0:T, 0:w], ALU.pow)

            def norm1(n):
                pool.wait_ge(stat1, n)
                own_wait(pool)
                link_a(nc.gpsimd.tensor_scalar(rstd[:, :], mv[:, :, 1], EPS_LN, 1.0, ALU.add, ALU.mult), n)
                power(rstd[:, :], rstd[:, :], 2).then_inc(rstd1, 1)

            def keep_x(n):
                if not (isinstance(n, int) and n == 1):
                    pool.wait_ge(h1_ready, n - 1)
                pool.wait_ge(x_loaded, n * 32)
                own_wait(pool)
                nc.gpsimd.tensor_copy(x_kept[:, :, :], x[:, :, :]).then_inc(x_free, 1)

            def kq(n):
                pool.wait_ge(kq_var, n)
                own_wait(pool)
                nc.gpsimd.tensor_scalar(rs[:, 0:2 * KH], var[:, 0:2 * KH], 1.0 / HD, EPS_RMS, ALU.mult, ALU.add)
                link_a(nc.gpsimd.tensor_scalar(rs[:, 2 * KH:], var[:, 2 * KH:], 1.0 / D, EPS_RMS, ALU.mult, ALU.add), n)
                power(rs[:, :], rs[:, :], 2 * KH + 2).then_inc(kq_rs, 1)

            def gated(n):
                pool.wait_ge(g_sum, n)
                own_wait(pool)
                link_r(nc.gpsimd.tensor_scalar(rs_g[:, :], sum_g[:, :], 0.25 / (2 * D), EPS_RMS, ALU.mult, ALU.add), n)
                link_r(power(rs_g[:, :], rs_g[:, :], 2), n)
                own_wait(pool)
                nc.gpsimd.tensor_scalar(rs_g[:, :], rs_g[:, :], 0.5, 0.0, ALU.mult, ALU.add).then_inc(g_rs, 1)

            def norm2(n):
                pool.wait_ge(stat2, n)
                own_wait(pool)
                link_b(nc.gpsimd.tensor_scalar(n2_a[:, :], mv_b[:, :, 1], EPS_LN, 1.0, ALU.add, ALU.mult), n)
                link_b(power(rstd_b[:, :], n2_a[:, :], 2), n)
                link_b(nc.gpsimd.tensor_tensor(n2_a[:, :], rstd_b[:, :], rstd_b[:, :], ALU.mult), n)
                link_b(nc.gpsimd.tensor_tensor(n2_a[:, :], n2_a[:, :], mv_b[:, :, 1], ALU.mult), n)
                own_wait(pool)
                link_b(nc.gpsimd.tensor_scalar(n2_a[:, :], n2_a[:, :], EPS_RMS, 1.0, ALU.add, ALU.mult), n)
                link_b(power(n2_b[:, :], n2_a[:, :], 2), n)
                nc.gpsimd.tensor_tensor(rstd_b[:, :], rstd_b[:, :], n2_b[:, :], ALU.mult).then_inc(norm2_s, 1)

            def ffn_norm(n):
                pool.wait_ge(yf_sum, n)
                link_b(nc.gpsimd.tensor_tensor(f_a[:, :], sum_f[:, :], deq1[:, :], ALU.mult), n)
                link_b(nc.gpsimd.tensor_tensor(f_a[:, :], f_a[:, :], deq1[:, :], ALU.mult), n)
                own_wait(pool)
                link_b(nc.gpsimd.tensor_scalar(f_a[:, :], f_a[:, :], 1.0 / FH, EPS_RMS, ALU.mult, ALU.add), n)
                link_b(power(f_b[:, :], f_a[:, :], 2), n)
                nc.gpsimd.tensor_tensor(f_b[:, :], f_b[:, :], deq1[:, :], ALU.mult).then_inc(yf_s, 1)

            def norm3(n):
                pool.wait_ge(stat3, n)
                own_wait(pool)
                link_c(nc.gpsimd.tensor_scalar(rstd_c[:, :], mv_c[:, :, 1], EPS_LN, 1.0, ALU.add, ALU.mult), n)
                power(rstd_c[:, :], rstd_c[:, :], 2).then_inc(rstd3, 1)

            def mix_queries(n, q):
                if q == 0:
                    pool.wait_ge(q_ready, n)
                t0 = q * QT
                for c in range(2):
                    last = nc.gpsimd.tensor_tensor(
                        qm[0:HW, c, t0:t0 + QT, :].rearrange("p t (g n) -> p t g n", n=NB),
                        qT[:, c, t0 * NB:(t0 + QT) * NB].rearrange("p (t n) -> p t n", n=NB)
                        .unsqueeze(2).broadcast_to([HW, QT, KH, NB]),
                        mix_l[:, c, :].unsqueeze(1).unsqueeze(3).broadcast_to([HW, QT, KH, NB]), ALU.mult)
                last.then_inc(qm_ready, 1)

            def first_queries(n):
                mix_queries(n, 0)
                mix_queries(n, 1)

            def mix_weights(u):
                def step(n):
                    if u % 2 == 0 and u // 2 + 2 < NT // QT:
                        mix_queries(n, u // 2 + 2)
                    pool.wait_ge(rz_ready, n * SU + (u + 1 - SU))
                    if u >= 2:
                        pool.wait_ge(at_ps, n * SU + (u - 1 - SU))
                    own_wait(pool)
                    for t in range(2):
                        last = nc.gpsimd.tensor_scalar(wz[u % 2][0:SR, t, :], mix_w[0:SR, :], rz[:, u, t:t + 1], 0.0,
                                                       ALU.mult, ALU.add)
                    last.then_inc(wz_ready, 1)
                return step

            def norm4(n):
                pool.wait_ge(stat4, n)
                own_wait(pool)
                link_d(nc.gpsimd.tensor_scalar(rstd_d[:, :], mv_d[:, :, 1], EPS_LN, 1.0, ALU.add, ALU.mult), n)
                power(rstd_d[:, :], rstd_d[:, :], 2).then_inc(rstd4, 1)

            phases = {"norm1_rstd": norm1, "keep_x": keep_x, "kq_rstd": kq, "gated_rms": gated, "norm2_rstd": norm2, "ffn_norm": ffn_norm,
                      "norm3_rstd": norm3, "qkv": first_queries, "norm4_rstd": norm4}
            for u in range(SU):
                phases[f"exp{u}"] = mix_weights(u)
            run(pool, phases)

        @block.scalar
        def _(act):
            link_a, link_b = linked(act, a_mix, AA)[0], linked(act, a_ffn, AB)[0]
            activation = nc.scalar.activation

            def xT1_(n):
                act.wait_ge(xT1_ps, n)
                activation(xT[:, :, :].rearrange("p a b -> p (a b)"), psum_a[0:HW, 0, 0:2 * L], ACT.Copy).then_inc(xT1, 1)

            def z(n):
                act.wait_ge(z_ps, n)
                for g in range(4):
                    activation(zc[:, g, :], psum_a[0:HW, g // 2, (g % 2) * L:(g % 2 + 1) * L], ACT.Identity,
                               bias=0.0, scale=conv_w[:, g, TAPS - 1:TAPS])
                activation(zs[:, :], psum_a[0:KH, 2, 0:L], ACT.Identity, bias=0.0, scale=conv_ws[:, TAPS - 1:TAPS])
                activation(gT[GR:GR + KH, :], psum_a[GR:GR + KH, 2, 0:L], ACT.Copy)
                activation(skip_in[:, :, :].rearrange("p a b -> p (a b)"),
                                       psum_a[0:T, 2, 2 * L:2 * L + 2 * SKIP], ACT.Copy).then_inc(z_tap, 1)

            def skip(n):
                if not (isinstance(n, int) and n == 1):
                    act.wait_ge(gsT_ps, n - 1)
                for j in range(2):
                    last = activation(gs[:, j, :, 64:112], skip_in[:, j, :].unsqueeze(1).broadcast_to([T, 6, SKIP]), ACT.Copy)
                last.then_inc(skip_ready, 1)

            def silu(n):
                act.wait_ge(zT_ps, n)
                activation(zk[:, :, :], psum_a[0:T, 0:2, 0:D + KH], ACT.Silu)
                activation(zq[:, :, :], psum_a[0:T, 0:2, D + KH:CONV], ACT.Silu).then_inc(silu_done, 1)

            def kq(n):
                act.wait_ge(kq_var, n)
                link_a(activation(sp_u[:, :], score[:, :, :].rearrange("p a b -> p (a b)"), ACT.Abs), n)
                activation(sp_u[:, :], sp_u[:, :], ACT.Exp, scale=-1.0).then_inc(exp_u, 1)

            def tanh_(n):
                act.wait_ge(tanh_in, n)
                activation(phi[:, :], phi[:, :], ACT.Tanh).then_inc(tanh_out, 1)

            def gate(n):
                act.wait_ge(gate_ps, n)
                if not (isinstance(n, int) and n == 1):
                    act.wait_ge(g_ready, n - 1)
                activation(gate_t[:, 0, :], psum_a[0:T, 2, 0:2 * D], ACT.Tanh, scale=0.5)
                activation(gate_t[:, 1, :], psum_a[0:T, 0, 0:2 * D], ACT.Tanh, scale=0.5).then_inc(gate_done, 1)

            def trig_(n):
                act.wait_ge(phi_ready, n)
                activation(sin_p[:, :, :].rearrange("p a b -> p (a b)"), phi[:, :], ACT.Sin)
                link_a(activation(phi_abs[:, :], phi[:, :], ACT.Abs), n)
                activation(cos_p[:, :, :].rearrange("p a b -> p (a b)"), phi_abs[:, :], ACT.Sin,
                                       bias=half_pi[0:T, :], scale=-1.0).then_inc(trig, 1)

            def gated(n):
                act.wait_ge(g_ready, n)
                activation(s_re[:, :], oc[:, 0, :], ACT.Square, accum_out=sum_g[:, 0:1])
                activation(s_im[:, :], oc[:, 1, :], ACT.Square, accum_out=sum_g[:, 1:2]).then_inc(g_sum, 1)

            def gsT_(n):
                act.wait_ge(gsT_ps, n)
                activation(gsT[:, :, :].rearrange("p (a b) n -> p a (b n)", b=2),
                                       psum_a[0:112, 0:3, 0:2 * L], ACT.Copy).then_inc(gsT_ready, 1)

            def y_silu_(p):
                def step(n):
                    act.wait_ge(y_ps, n * 6 + (p - 5))
                    if p >= 3:
                        act.wait_ge(y_ready, n * 6 + (p - 8))
                    activation(y_silu_t[:, p % 3, :], psum_a[0:HW, p % 3, L:2 * L], ACT.Silu).then_inc(y_silu, 1)
                return step

            def xqT_(n):
                act.wait_ge(xqT_ps, n)
                activation(xqT[:, :, 0:T], psum_z[0:HW, 0, 0:200].bitcast(bf16)
                                       .rearrange("p (k t) -> p k t", k=4)[:, :, 0:T], ACT.Copy).then_inc(xqT_ready, 1)

            def f_silu(j):
                def step(n):
                    act.wait_ge(h_ps, n * 2 + (j - 1))
                    activation(sg_f[:, j, :], psum_z[0:T, 0, :], ACT.Silu, scale=deq1[:, j:j + 1]).then_inc(sg_ready, 1)
                return step

            def ffn_norm(n):
                act.wait_ge(yf_ready, n * 2)
                link_b(activation(sg_f[:, 0, :], y_f[:, 0, :], ACT.Square, accum_out=sum_f[:, 0:1]), n)
                activation(sg_f[:, 1, :], y_f[:, 1, :], ACT.Square, accum_out=sum_f[:, 1:2]).then_inc(yf_sum, 1)

            def yqT_(n):
                act.wait_ge(yqT_ps, n)
                activation(yqT[:, :, 0:T], psum_z[:, 0, 0:400].bitcast(bf16)
                                       .rearrange("p (k t) -> p k t", k=8)[:, :, 0:T], ACT.Copy).then_inc(yqT_ready, 1)

            def xT3_(n):
                act.wait_ge(xT3_ps, n)
                activation(xT_c[:, :, :].rearrange("p a b -> p (a b)"), psum_c[0:HW, 0, 0:2 * L], ACT.Copy).then_inc(xT3, 1)

            def qkv(n):
                act.wait_ge(qkv_ps, n)
                activation(qT[:, :, 0:L], psum_c[0:HW, 1, 0:2 * L].rearrange("p (a b) -> p a b", a=2),
                                       ACT.Copy, scale=HD ** -0.5).then_inc(q_ready, 1)
                activation(kT[0:HW, :, :].rearrange("p a b -> p (a b)"), psum_c[0:HW, 2, 0:2 * L], ACT.Copy)
                activation(vp[:, :, :, 0:HD].rearrange("p a g d -> p (a g) d"),
                                       psum_c[0:T, 0, 0:2 * D].rearrange("p (h d) -> p h d", d=HD), ACT.Copy).then_inc(v_ready, 1)

            def exps(u):
                def step(n):
                    act.wait_ge(s_max, n * SU + (u + 1 - SU))
                    if u >= 2:
                        act.wait_ge(at_ps, n * SU + (u - 1 - SU))
                    for t in range(2):
                        last = activation(expo[u % 2][0:SR, t, :], psum_c[0:SR, u % 2, t * L:(t + 1) * L], ACT.Exp,
                                          bias=nmax[:, t, u:u + 1], accum_out=zsum[:, u, t:t + 1])
                    last.then_inc(exp_done, 1)
                return step

            def keep_mixed(u):
                def step(n):
                    act.wait_ge(at_ps, n * SU + (u + 1 - SU))
                    activation(at[:, 2 * u:2 * u + 2, :, :].rearrange("p t a n -> p (t a n)"),
                                           psum_c[0:T, 2, 0:4 * SR], ACT.Copy).then_inc(at_ready, 1)
                return step

            def w_(n):
                act.wait_ge(w_ps, n)
                activation(wT[:, 0:2, :].rearrange("p a b -> p (a b)"), psum_c[:, 0, 0:2 * NPAD], ACT.Copy)
                activation(wT[:, 2, :], psum_c[:, 1, 0:NPAD], ACT.Copy).then_inc(w_ready, 1)

            def wp_(n):
                act.wait_ge(wT_ps, n)
                activation(wp[:, 0, :], psum_c[0:T, 2, 0:384], ACT.Copy)
                activation(wp[:, 1, :], psum_c[0:T, 0, 0:384], ACT.Copy).then_inc(wp_ready, 1)

            def xT4_(n):
                act.wait_ge(xT4_ps, n)
                activation(xT_d[:, :, :].rearrange("p a b -> p (a b)"), psum_z[0:HW, 0, 0:2 * L], ACT.Copy).then_inc(xT4, 1)

            def route(n):
                act.wait_ge(lmax_ready, n)
                activation(lexp[:, :], psum_z[0:T, 1, 0:NE], ACT.Exp, bias=lmax[:, 1:2], scale=1.0 / L,
                                       accum_out=lsum[:, :]).then_inc(lexp_ready, 1)

            def hidden(r):
                def step(n):
                    act.wait_ge(expert_loaded, n * 64)
                    act.wait_ge(hid_ps, n * 3 + (r - 2))
                    for k in range(2):
                        ins = activation(hT[:, 2 * r + k, :], psum_z[:, r % 2, k * L:(k + 1) * L], ACT.Gelu,
                                          bias=e_b1[:, 2 * r + k:2 * r + k + 1])
                    ins.then_inc(hid_ready, 1)
                return step

            phases = {"xT1": xT1_, "z": z, "skip": skip, "zT": silu, "kq_exp": kq, "tanh_act": tanh_, "gate_t": gate, "trig": trig_,
                      "gated_sum": gated, "gsT": gsT_, "xqT": xqT_, "ffn_norm": ffn_norm, "yqT": yqT_,
                      "xT3": xT3_, "qkv": qkv, "w": w_, "wp": wp_, "xT4": xT4_, "lexp": route}
            for p in range(6):
                phases[f"y{p}"] = y_silu_(p)
            for j in range(2):
                phases[f"hid{j}"] = f_silu(j)
            for r in range(3):
                phases[f"hidden{r}"] = hidden(r)
            for u in range(SU):
                phases[f"exp{u}"] = exps(u)
                if u % 2 == 1:
                    phases[f"mixed{u}"] = keep_mixed(u)
            run(act, phases)

        @block.tensor
        def _(pe):
            matmul, transpose = nc.tensor.matmul, nc.tensor.transpose

            def halves_T(src, bank):
                for c in range(2):
                    for j in range(2):
                        last = transpose(bank[0:HW, c * L + j * T:c * L + (j + 1) * T],
                                         src[:, j, c * HW:(c + 1) * HW], ident[0:T, 0:T])
                return last

            def xT1_(n):
                pe.wait_ge(xn1, n)
                halves_T(xn, psum_a[:, 0, :]).then_inc(xT1_ps, 1)

            def z(n):
                pe.wait_ge(xT1, n)
                if not (isinstance(n, int) and n == 1):
                    pe.wait_ge(g_ready, n - 1)

                def channels(o_, c0, width):
                    for c in range(2):
                        matmul(o_, w_in[:, c, c0:c0 + width], xT[:, c, :], start=(c == 0), stop=(c == 1))
                for g, c0 in enumerate((0, HW, D + KH, D + KH + HW)):
                    channels(psum_a[0:HW, g // 2, (g % 2) * L:(g % 2 + 1) * L], c0, HW)
                for c in range(2):
                    matmul(psum_a[0:GR + KH, 2, 0:L], w_heads[:, c, :], xT[:, c, :], start=(c == 0), stop=(c == 1))
                for j in range(2):
                    for c in range(2):
                        last = matmul(psum_a[0:T, 2, 2 * L + j * SKIP:2 * L + (j + 1) * SKIP], xT[:, c, j * T:(j + 1) * T],
                                      w_in[:, c, CONV:CONV + SKIP], start=(c == 0), stop=(c == 1))
                last.then_inc(z_ps, 1)

            def zT(n):
                pe.wait_ge(conv_done, n)
                for j in range(2):
                    t = slice(j * T, (j + 1) * T)
                    for src, rows, c0 in ((zc[:, 0, t], HW, 0), (zc[:, 1, t], HW, HW), (zs[:, t], KH, D),
                                          (zc[:, 2, t], HW, D + KH), (zc[:, 3, t], HW, D + KH + HW)):
                        last = transpose(psum_a[0:T, j, c0:c0 + rows], src, ident[0:rows, 0:rows])
                last.then_inc(zT_ps, 1)

            def gate(n):
                for j in range(2):
                    if j == 1:
                        pe.wait_ge(silu_done, n)
                    last = matmul(psum_a[0:T, 2 * (1 - j), 0:2 * D], gT[GR:GR + KH, j * T:(j + 1) * T], w_gate[GR:GR + KH, :],
                                  start=True, stop=True)
                last.then_inc(gate_ps, 1)

            def cum(n):
                pe.wait_ge(stack_ready, n)
                pe.wait_ge(gate_done, n)
                matmul(psum_a[0:T, 1, 0:CONV], upper[:, :], stack[:, 0, :], start=True, stop=True)
                matmul(psum_a[0:T, 2, 0:CONV], ones[0:T, 0:T], stack[:, 0, :], start=True, stop=False)
                matmul(psum_a[0:T, 2, 0:CONV], upper[:, :], stack[:, 1, :], start=False, stop=True).then_inc(cum_ps, 1)

            def gsT_(n):
                pe.wait_ge(gs_ready, n)
                pe.wait_ge(skip_ready, n)
                pe.wait_ge(gate_done, min(n + 1, images) if isinstance(n, int) else n + 1)
                for p in range(6):
                    for j in range(2):
                        c0 = (p % 2) * L + j * T
                        last = transpose(psum_a[0:112, p // 2, c0:c0 + T], gs[:, j, p, :], ident[0:T, 0:T])
                last.then_inc(gsT_ps, 1)

            def y(p):
                def step(n):
                    pe.wait_ge(gsT_ready, n)
                    if p >= 3:
                        pe.wait_ge(y_ready, n * 6 + (p - 8))
                    for half in range(2):
                        last = matmul(psum_a[0:HW, p % 3, half * L:(half + 1) * L],
                                      w_read[:, p, half * HW:(half + 1) * HW], gsT[:, p, :], start=True, stop=True)
                    last.then_inc(y_ps, 1)
                return step

            def out1(n):
                pe.wait_ge(y_ready, n * 6)
                for j in range(2):
                    for p in range(6):
                        last = matmul(psum_a[0:T, 0, j * D:(j + 1) * D], yT[:, p, j * T:(j + 1) * T], w_out[:, p, :],
                                      start=(p == 0), stop=(p == 5))
                last.then_inc(out1_ps, 1)

            def xqT_(n):
                pe.wait_ge(xq_ready, n)
                bank = psum_z[0:HW, 0, 0:200].bitcast(bf16)
                for c in range(2):
                    for j in range(2):
                        c0 = (2 * c + j) * 100
                        last = transpose(bank[:, c0:c0 + T], xqb[:, j, c * HW:(c + 1) * HW], ident_b[0:T, 0:T])
                last.then_inc(xqT_ps, 1)

            def hid1(j):
                def step(n):
                    pe.wait_ge(xqT_ready, n)
                    if j == 1:
                        pe.wait_ge(yf_ready, n * 2 - 1)
                    for part, bank in ((1, 0), (0, 1)):
                        for c in range(2):
                            last = matmul(psum_z[0:T, bank, :], xqT[:, 2 * c + j, 0:T],
                                          fq1[:, c, part * FH:(part + 1) * FH], start=(c == 0), stop=(c == 1))
                    last.then_inc(h_ps, 1)
                return step

            def yqT_(n):
                pe.wait_ge(yq_ready, n)
                bank = psum_z[:, 0, 0:400].bitcast(bf16)
                for c in range(4):
                    for j in range(2):
                        c0 = (2 * c + j) * 100
                        last = transpose(bank[:, c0:c0 + T], yqb[:, j, c * 128:(c + 1) * 128], ident_b[0:T, 0:T])
                last.then_inc(yqT_ps, 1)

            def out2(n):
                pe.wait_ge(yqT_ready, n)
                for j in range(2):
                    for c in range(4):
                        last = matmul(psum_z[0:T, 1, j * D:(j + 1) * D], yqT[:, 2 * c + j, 0:T], fq2[:, c, :],
                                      start=(c == 0), stop=(c == 3))
                last.then_inc(out2_ps, 1)

            def xT3_(n):
                pe.wait_ge(xn3, n)
                halves_T(xn_c, psum_c[:, 0, :]).then_inc(xT3_ps, 1)

            def qkv(n):
                pe.wait_ge(xT3, n)
                for bank, c0 in ((1, 0), (2, D)):
                    for half in range(2):
                        for c in range(2):
                            matmul(psum_c[0:HW, bank, half * L:(half + 1) * L],
                                   w_qkv[:, c, c0 + half * HW:c0 + (half + 1) * HW], xT_c[:, c, :],
                                   start=(c == 0), stop=(c == 1))
                for j in range(2):
                    for c in range(2):
                        last = matmul(psum_c[0:T, 0, j * D:(j + 1) * D], xT_c[:, c, j * T:(j + 1) * T],
                                      w_qkv[:, c, 2 * D:3 * D], start=(c == 0), stop=(c == 1))
                last.then_inc(qkv_ps, 1)

            def scores(u):
                def step(n):
                    if u == 0:
                        pe.wait_ge(pad_loaded, 80)
                        pe.wait_ge(v_ready, n)
                    if u % 2 == 0:
                        pe.wait_ge(qm_ready, n * (NT // QT) + (u // 2 + 1 - NT // QT))
                    if u >= 2:
                        pe.wait_ge(exp_done, n * SU + (u - 1 - SU))
                    for t in range(2):
                        o_ = psum_c[0:SR, u % 2, t * L:(t + 1) * L]
                        matmul(o_, qm[0:HW, 0, 2 * u + t, :], kT[0:HW, 0, :], start=True, stop=False)
                        last = matmul(o_, qm[:, 1, 2 * u + t, :], kT[:, 1, :], start=False, stop=True)
                    last.then_inc(s_ps, 1)
                return step

            def mixed(u):
                def step(n):
                    pe.wait_ge(exp_done, n * SU + (u + 1 - SU))
                    pe.wait_ge(wz_ready, n * SU + (u + 1 - SU))
                    if u >= 1:
                        pe.wait_ge(at_ready, n * SU + (u - SU))
                    for t in range(2):
                        for half in range(2):
                            c0 = (2 * t + half) * SR
                            last = matmul(psum_c[0:T, 2, c0:c0 + SR], expo[u % 2][:, t, half * T:(half + 1) * T],
                                          wz[u % 2][:, t, :], start=True, stop=True)
                    last.then_inc(at_ps, 1)
                return step

            def apply_attention(values):
                for g in range(KH):
                    r, q = g // 4, g % 4
                    for half in range(2):
                        last = matmul(psum_c[32 * q:32 * q + 32, r // 2, (r % 2) * NPAD:(r % 2 + 1) * NPAD],
                                      values[:, half, g, :], at[:, :, half, g * NB:(g + 1) * NB],
                                      start=(half == 0), stop=(half == 1))
                return last

            def w_(n):
                pe.wait_ge(at_ready, n * SU)
                pe.wait_ge(v_ready, n)
                apply_attention(vp).then_inc(w_ps, 1)

            def wp_(n):
                pe.wait_ge(w_ready, n)
                for j in range(2):
                    for r in range(3):
                        last = transpose(psum_c[0:T, 2 * (1 - j), r * 128:(r + 1) * 128], wT[:, r, j * T:(j + 1) * T], ident[:, :])
                last.then_inc(wT_ps, 1)

            def w2(n):
                pe.wait_ge(wp_ready, n)
                apply_attention(wp[:, :, :].rearrange("p a (g d) -> p a g d", d=32)).then_inc(w2_ps, 1)

            def proj(n):
                pe.wait_ge(o2_ready, n)
                for j in range(2):
                    for r in range(3):
                        last = matmul(psum_c[0:T, 2, j * D:(j + 1) * D], o2[:, r, j * T:(j + 1) * T], w_proj[:, r, :],
                                      start=(r == 0), stop=(r == 2))
                last.then_inc(proj_ps, 1)

            def xT4_(n):
                pe.wait_ge(xn4, n)
                halves_T(xn_d, psum_z[:, 0, :]).then_inc(xT4_ps, 1)

            def route(n):
                pe.wait_ge(xsum_ready, n)
                for c in range(2):
                    last = matmul(psum_z[0:T, 1, 0:NE], xsum[:, c:c + 1].broadcast_to([HW, T]), w_route[:, c, :],
                                  start=(c == 0), stop=(c == 1))
                last.then_inc(logit_ps, 1)

            def hidden(r):
                def step(n):
                    pe.wait_ge(expert_loaded, n * 64)
                    if r == 0:
                        pe.wait_ge(lexp_ready, n)
                        pe.wait_ge(h2_ready, min(n + 2, images) if isinstance(n, int) else n + 2)
                    if r == 2:
                        pe.wait_ge(hid_ready, n * 3 - 2)
                    for k in range(2):
                        f = 2 * r + k
                        for c in range(2):
                            last = matmul(psum_z[:, r % 2, k * L:(k + 1) * L], e_w1[:, c, f * 128:(f + 1) * 128],
                                          xT_d[:, c, :], start=(c == 0), stop=(c == 1))
                    last.then_inc(hid_ps, 1)
                return step

            def ffn_out(n):
                pe.wait_ge(hid_ready, n * 3)
                for j in range(2):
                    for f in range(6):
                        last = matmul(psum_z[0:T, 1, j * D:(j + 1) * D], hT[:, f, j * T:(j + 1) * T], e_w2[:, f, :],
                                      start=(f == 0), stop=(f == 5))
                last.then_inc(ffn_ps, 1)

            phases = {"xT1": xT1_, "z": z, "zT": zT, "gate_t": gate, "cum": cum, "gsT": gsT_, "out1": out1, "xqT": xqT_,
                      "yqT": yqT_, "out2": out2, "xT3": xT3_, "qkv": qkv, "w": w_, "wp": wp_, "w2": w2,
                      "proj": proj, "xT4": xT4_, "route": route, "ffn_mm": ffn_out}
            for p in range(6):
                phases[f"y{p}"] = y(p)
            for j in range(2):
                phases[f"hid{j}"] = hid1(j)
            for r in range(3):
                phases[f"hidden{r}"] = hidden(r)
            for u in range(SU):
                phases[f"score{u}"] = scores(u)
                phases[f"mixed{u}"] = mixed(u)
            run(pe, phases)

        @block.vector
        def _(dve):
            streams = [linked(dve, sem, steps) for sem, steps in
                       ((v_mix, VA), (v_read, VR), (v_ffn, VB), (v_att, VC), (v_exp, VD))]
            (link_a, mark_a, done_a), (link_r, mark_r, done_r), (link_b, mark_b, done_b) = streams[:3]
            (link_c, mark_c, done_c), (link_d, mark_d, done_d) = streams[3:]
            tt, ts, stt = nc.vector.tensor_tensor, nc.vector.tensor_scalar, nc.vector.scalar_tensor_tensor

            def heads(ap, width=HD):
                return ap.rearrange("p (h d) -> p h d", d=width)

            def flat(t):
                return t[:, :, :].rearrange("p a b -> p (a b)")

            def halves(t):
                return t[:, :].rearrange("p (a b) -> p a b", a=2)

            def stats_of(h, stats_, mark):
                for j in range(2):
                    last = nc.vector.bn_stats(stats_[:, j, :], h[:, j, :])
                mark(last)

            def row_stats(stats_, mv_, done, n, ready):
                done(n)
                own_wait(dve)
                nc.vector.bn_aggr(mv_[:, 0, :], stats_[:, 0, :])
                nc.vector.bn_aggr(mv_[:, 1, :], stats_[:, 1, :]).then_inc(ready, 1)

            def normalise(out_, h, mv_, rstd_):
                for j in range(2):
                    last = ts(out_[:, j, :], h[:, j, :], mv_[:, j, 0:1], rstd_[:, j:j + 1], ALU.subtract, ALU.mult)
                return last

            def norm1(n):
                dve.wait_ge(x_loaded, n * 32)
                stats_of(x, stats, mark_a)

            def norm1_stats(n):
                row_stats(stats, mv, done_a, n, stat1)

            def norm1_apply(n):
                dve.wait_ge(rstd1, n)
                normalise(xn, x, mv, rstd).then_inc(xn1, 1)

            def conv(s):
                def step(n):
                    if s == 1:
                        dve.wait_ge(z_tap, n)
                    else:
                        done_a(n)
                    w = TAPS - 1 - s
                    for g in range(4):
                        c0 = (g % 2) * L
                        stt(out=zc[:, g, s:L], in0=psum_a[0:HW, g // 2, c0:c0 + L - s], scalar=conv_w[:, g, w:w + 1],
                            in1=zc[:, g, s:L], op0=ALU.mult, op1=ALU.add)
                    last = stt(out=zs[:, s:L], in0=psum_a[0:KH, 2, 0:L - s], scalar=conv_ws[:, w:w + 1], in1=zs[:, s:L],
                               op0=ALU.mult, op1=ALU.add)
                    if s < TAPS - 1:
                        mark_a(last)
                    else:
                        last.then_inc(conv_done, 1)
                return step

            def kq_square(n):
                dve.wait_ge(silu_done, n)
                tt(score[:, :, :], zk[:, :, D:D + KH], score_w[:, :].rearrange("p (a b) -> p a b", a=2), ALU.mult)
                mark_a(tt(halves(sq), zk[:, :, 0:D], zk[:, :, 0:D], ALU.mult))

            def kq_sum(n):
                done_a(n)
                tt(score[:, :, :], score[:, :, :], score_b[:, :].rearrange("p (a b) -> p a b", a=2), ALU.add)
                mark_a(nc.vector.reduce_sum(var[:, 0:2 * KH], heads(sq[:, :]), axis=AX.X))

            def kq_square_q(n):
                done_a(n)
                mark_a(tt(sq[:, :], flat(zq), flat(zq), ALU.mult))

            def kq(n):
                done_a(n)
                nc.vector.reduce_sum(var[:, 2 * KH:], halves(sq), axis=AX.X).then_inc(kq_var, 1)

            def queries(n):
                for c, q in ((0, qx_re), (1, qx_im)):
                    src = flat(zq).rearrange("p (q h c) -> p q h c", h=HD, c=2)[:, :, :, c]
                    last = tt(q[:, :].rearrange("p (q r h) -> p q r h", r=2, h=HD),
                              src.unsqueeze(2).broadcast_to([T, 2 * NQ, 2, HD]),
                              q_w[:, c, :].rearrange("p (q r h) -> p q r h", r=2, h=HD), ALU.mult)
                mark_a(last)

            def keys(n):
                dve.wait_ge(kq_rs, n)
                mark_a(tt(kv[:, :, :].rearrange("p a (k h) -> p a k h", h=HD),
                          zk[:, :, 0:D].rearrange("p a (k h) -> p a k h", h=HD),
                          rs[:, 0:2 * KH].rearrange("p (a k) -> p a k", a=2).unsqueeze(3).broadcast_to([T, 2, KH, HD]),
                          ALU.mult))

            def keys_norm(n):
                done_a(n)
                mark_a(tt(flat(kv), flat(kv), k_norm[:, :], ALU.mult))

            def keys_scaled(n):
                done_a(n)
                tt(phi[:, :], flat(kv), tanh_scale[:, :], ALU.mult).then_inc(tanh_in, 1)

            def softplus_step(k):
                if k == 0:
                    return ts(sp_p[:, :], sp_u[:, :], 2.0, None, ALU.add)
                if k == 1:
                    return nc.vector.reciprocal(sp_p[:, :], sp_p[:, :])
                if k == 2:
                    return tt(sp_z[:, :], sp_u[:, :], sp_p[:, :], ALU.mult)
                if k == 3:
                    return tt(sp_z2[:, :], sp_z[:, :], sp_z[:, :], ALU.mult)
                if k == 4:
                    return ts(sp_p[:, :], sp_z2[:, :], 2.0 / (2 * LOG1P_TERMS - 1), None, ALU.mult)
                term = LOG1P_TERMS + 3 - k
                if term > 0:
                    return stt(out=sp_p[:, :], in0=sp_p[:, :], scalar=2.0 / (2 * term + 1), in1=sp_z2[:, :],
                               op0=ALU.add, op1=ALU.mult)
                if term == 0:
                    return stt(out=sp_p[:, :], in0=sp_p[:, :], scalar=2.0, in1=sp_z[:, :], op0=ALU.add, op1=ALU.mult)
                if term == -1:
                    return stt(out=sp_p[:, :], in0=flat(score), scalar=0.0, in1=sp_p[:, :], op0=ALU.max, op1=ALU.add)
                if term == -2:
                    return tt(sp_p[:, :], sp_p[:, :], time_w[:, :], ALU.mult)
                return ts(stack[:, :, 2 * D:2 * D + KH], sp_p[:, :].rearrange("p (a k) -> p a k", a=2), 1e-6, 1000.0,
                          ALU.max, ALU.min)

            def softplus(k):
                def step(n):
                    if k == 0:
                        dve.wait_ge(exp_u, n)
                    else:
                        done_a(n)
                    mark_a(softplus_step(k))
                return step

            def angles(n):
                dve.wait_ge(tanh_out, n)
                tt(phi[:, :], phi[:, :], theta[:, :], ALU.mult).then_inc(phi_ready, 1)

            def weighted(n):
                done_a(n)
                p_w = stack[:, :, 2 * D:2 * D + KH]
                mark_a(tt(kvw[:, :, :].rearrange("p a (k h) -> p a k h", h=HD),
                          kv[:, :, :].rearrange("p a (k h) -> p a k h", h=HD),
                          p_w.unsqueeze(3).broadcast_to([T, 2, KH, HD]), ALU.mult))

            def trig_(n):
                done_a(n)
                dve.wait_ge(trig, n)
                tt(stack[:, :, 0:D], kvw[:, :, :], cos_p[:, :, :], ALU.mult)
                tt(stack[:, :, D:2 * D], kvw[:, :, :], sin_p[:, :, :], ALU.mult).then_inc(stack_ready, 1)

            def match_den(n):
                dve.wait_ge(cum_ps, n)
                mark_r(ts(den[:, :, :], psum_a[0:T, 1:3, 2 * D:2 * D + KH], 1e-4, None, ALU.max))

            def match_inv(n):
                done_r(n)
                mark_r(nc.vector.reciprocal(den[:, :, :], den[:, :, :]))

            def match_scale(n):
                done_r(n)
                mark_r(tt(den[:, :, :], den[:, :, :],
                          rs[:, 2 * KH:].unsqueeze(2).broadcast_to([T, 2, KH]), ALU.mult))

            def match_sums(n):
                done_r(n)
                for c, s in ((0, s_re), (1, s_im)):
                    last = tt(s[:, :].rearrange("p (a k h) -> p a k h", a=2, h=HD),
                              psum_a[0:T, 1:3, c * D:(c + 1) * D].rearrange("p a (k h) -> p a k h", h=HD),
                              den[:, :, :].unsqueeze(3).broadcast_to([T, 2, KH, HD]), ALU.mult)
                mark_r(last)

            oc_h = flat(oc).rearrange("p (k c h) -> p k c h", c=2, h=HD)

            def match_products(c):
                def step(n):
                    done_r(n)
                    tt(m_a[:, :], (s_re, s_im)[c][:, :], qx_re[:, :], ALU.mult)
                    mark_r(tt(m_b[:, :], (s_im, s_re)[c][:, :], qx_im[:, :], ALU.mult))
                return step

            def match_add(c):
                def step(n):
                    done_r(n)
                    mark_r(tt(oc_h[:, :, c, :], heads(m_a[:, :]), heads(m_b[:, :]), (ALU.add, ALU.subtract)[c]))
                return step

            def gate(n):
                done_r(n)
                dve.wait_ge(gate_done, n)
                stt(out=flat(oc), in0=flat(gate_t), scalar=1.0, in1=flat(oc), op0=ALU.add, op1=ALU.mult).then_inc(g_ready, 1)

            def gated(n):
                dve.wait_ge(g_rs, n)
                for j in range(2):
                    last = ts(gs[:, j, :, 0:64], oc[:, j, :].rearrange("p (q c) -> p q c", c=64), rs_g[:, j:j + 1], None,
                              ALU.mult)
                last.then_inc(gs_ready, 1)

            def y(p):
                def step(n):
                    dve.wait_ge(y_silu, n * 6 + (p - 5))
                    tt(yT[:, p, :], psum_a[0:HW, p % 3, 0:L], y_silu_t[:, p % 3, :], ALU.mult).then_inc(y_ready, 1)
                return step

            def h1_(n):
                dve.wait_ge(out1_ps, n)
                dve.wait_ge(x_free, n)
                tt(flat(h1), psum_a[0:T, 0, 0:2 * D], flat(x_kept), ALU.add).then_inc(h1_ready, 1)

            def quantise(k, src, out_, w, deq, n):
                done_b(n)
                if k == 0:
                    return nc.vector.tensor_reduce(amax[:, :], src, axis=AX.X, op=ALU.max, apply_absolute_value=True)
                if k == 1:
                    return ts(amax[:, :], amax[:, :], EPS_Q, None, ALU.max)
                if k == 2:
                    ts(deq[:, :], amax[:, :], 1.0 / 127.0, w_mean[0:T, w:w + 1], ALU.mult, ALU.mult)
                    return nc.vector.reciprocal(qscale[:, :], amax[:, :])
                if k == 3:
                    return ts(qscale[:, :], qscale[:, :], 127.0, None, ALU.mult)
                if k == 4:
                    for j in range(2):
                        last = ts(src[:, j, :], src[:, j, :], qscale[:, j:j + 1], MAGIC, ALU.mult, ALU.add)
                    return last
                return ts(out_, src, MAGIC, None, ALU.subtract)

            def norm2(n):
                dve.wait_ge(h1_ready, n)
                if not (isinstance(n, int) and n == 1):
                    dve.wait_ge(h2_ready, n - 1)
                mark_b(nc.vector.tensor_copy(flat(h1_b), flat(h1)))

            def norm2_sum(n):
                done_b(n)
                stats_of(h1_b, stats_b, mark_b)

            def norm2_stats(n):
                row_stats(stats_b, mv_b, done_b, n, stat2)

            def norm2_apply(n):
                dve.wait_ge(norm2_s, n)
                mark_b(normalise(xn_b, h1_b, mv_b, rstd_b))

            def norm2_gain(n):
                done_b(n)
                mark_b(tt(flat(xn_b), flat(xn_b), g_in[:, :], ALU.mult))

            def in_quant(k):
                def step(n):
                    ins = quantise(k, xn_b[:, :, :], xqb[:, :, :], 0, deq1, n)
                    if k == 5:
                        ins.then_inc(xq_ready, 1)
                    else:
                        mark_b(ins)
                return step

            def out_quant(k):
                def step(n):
                    ins = quantise(k, y_f[:, :, :], yqb[:, :, :], 1, deq2, n)
                    if k == 5:
                        ins.then_inc(yq_ready, 1)
                    else:
                        mark_b(ins)
                return step

            def hid1(j):
                def step(n):
                    dve.wait_ge(sg_ready, n * 2 + (j - 1))
                    tt(y_f[:, j, :], psum_z[0:T, 1, :], sg_f[:, j, :], ALU.mult).then_inc(yf_ready, 1)
                return step

            def ffn_gain(n):
                dve.wait_ge(yf_s, n)
                for j in range(2):
                    last = stt(out=y_f[:, j, :], in0=y_f[:, j, :], scalar=f_b[:, j:j + 1], in1=g_out[:, :],
                               op0=ALU.mult, op1=ALU.mult)
                mark_b(last)

            def out2(n):
                dve.wait_ge(out2_ps, n)
                for j in range(2):
                    last = stt(out=h2[:, j, :], in0=psum_z[0:T, 1, j * D:(j + 1) * D], scalar=deq2[:, j:j + 1],
                               in1=h1_b[:, j, :], op0=ALU.mult, op1=ALU.add)
                last.then_inc(h2_ready, 1)

            def norm3(n):
                dve.wait_ge(h2_ready, n)
                mark_c(nc.vector.tensor_copy(flat(h3), flat(h2)))

            def norm3_sum(n):
                done_c(n)
                stats_of(h3, stats_c, mark_c)

            def norm3_stats(n):
                row_stats(stats_c, mv_c, done_c, n, stat3)

            def norm3_apply(n):
                dve.wait_ge(rstd3, n)
                normalise(xn_c, h3, mv_c, rstd_c).then_inc(xn3, 1)

            def score_max(u):
                def step(n):
                    dve.wait_ge(s_ps, n * SU + (u + 1 - SU))
                    nc.vector.tensor_reduce(nmax[:, :, u], psum_c[0:SR, u % 2, 0:2 * L]
                                                        .rearrange("p (t m) -> p t m", t=2),
                                                        axis=AX.X, op=ALU.max, negate=True).then_inc(s_max, 1)
                return step

            def denominators(u):
                def step(n):
                    dve.wait_ge(exp_done, n * SU + (u + 1 - SU))
                    nc.vector.reciprocal(rz[:, u, :], zsum[:, u, :]).then_inc(rz_ready, 1)
                return step

            def keep_mixed(u):
                def step(n):
                    dve.wait_ge(at_ps, n * SU + (u + 1 - SU))
                    nc.vector.tensor_copy(at[:, 2 * u:2 * u + 2, :, :].rearrange("p t a n -> p (t a n)"),
                                                      psum_c[0:T, 2, 0:4 * SR]).then_inc(at_ready, 1)
                return step

            def w2(n):
                dve.wait_ge(w_ready, n)
                for r in range(3):
                    last = ts(o2[:, r, :], wT[:, r, :], lam_1[:, r:r + 1], None, ALU.mult)
                mark_c(last)

            def w2_add(n):
                done_c(n)
                dve.wait_ge(w2_ps, n)
                for r in range(3):
                    last = stt(out=o2[:, r, :], in0=psum_c[:, r // 2, (r % 2) * NPAD:(r % 2 + 1) * NPAD],
                               scalar=lam_2[:, r:r + 1], in1=o2[:, r, :], op0=ALU.mult, op1=ALU.add)
                last.then_inc(o2_ready, 1)

            def proj(n):
                dve.wait_ge(proj_ps, n)
                mark_c(tt(flat(h4), psum_c[0:T, 2, 0:2 * D], flat(h3), ALU.add))

            def proj_bias(n):
                done_c(n)
                tt(flat(h4), flat(h4), b_proj[:, :], ALU.add).then_inc(h4_ready, 1)

            def norm4(n):
                dve.wait_ge(h4_ready, n)
                if not (isinstance(n, int) and n == 1):
                    dve.wait_ge(o_ready, n - 1)
                mark_d(nc.vector.tensor_copy(flat(h4_d), flat(h4)))

            def norm4_sum(n):
                done_d(n)
                stats_of(h4_d, stats_d, mark_d)

            def norm4_stats(n):
                row_stats(stats_d, mv_d, done_d, n, stat4)

            def norm4_apply(n):
                dve.wait_ge(rstd4, n)
                normalise(xn_d, h4_d, mv_d, rstd_d).then_inc(xn4, 1)

            def route(n):
                dve.wait_ge(xT4, n)
                nc.vector.reduce_sum(xsum[:, :], xT_d[:, :, :], axis=AX.X).then_inc(xsum_ready, 1)

            def logit_max(n):
                dve.wait_ge(logit_ps, n)
                mark_d(nc.vector.reduce_max(lmax[:, 0:1], psum_z[0:T, 1, 0:NE], axis=AX.X))

            def choose_flags(n):
                done_d(n)
                mark_d(ts(sel_f[:, 0:2], psum_z[0:1, 1, 0:2], lmax[0:1, 0:1], None, ALU.is_ge))
                ts(lmax[:, 1:2], lmax[:, 0:1], -1.0 / L, None, ALU.mult).then_inc(lmax_ready, 1)

            def choose_terms(n):
                done_d(n)
                ts(sel_f[:, 2:3], sel_f[:, 0:1], -1.0, 1.0, ALU.mult, ALU.add)
                mark_d(ts(sel_f[:, 3:4], sel_f[:, 1:2], -1.0, 2.0, ALU.mult, ALU.add))

            def choose(n):
                done_d(n)
                tt(sel[:, :], sel_f[:, 2:3], sel_f[:, 3:4], ALU.mult).then_inc(sel_ready, 1)

            def chosen_p(n):
                dve.wait_ge(lexp_ready, n)
                mark_d(nc.vector.reciprocal(route_w[:, :], lsum[:, :]))

            def ffn_bias(n):
                dve.wait_ge(ffn_ps, n)
                dve.wait_ge(expert_loaded, n * 64)
                if not (isinstance(n, int) and n == 1):
                    dve.wait_ge(o_stored, n * 32 - 32)
                mark_d(tt(flat(o), psum_z[0:T, 1, 0:2 * D], e_b2[:, :], ALU.add))

            def ffn_out(n):
                done_d(n)
                stt(out=flat(o), in0=flat(o), scalar=route_w[:, :], in1=flat(h4_d), op0=ALU.mult,
                    op1=ALU.add).then_inc(o_ready, 1)

            phases = {"norm1": norm1, "norm1_stats": norm1_stats, "norm1_apply": norm1_apply, "kq_square": kq_square,
                      "kq_sum": kq_sum, "kq_square_q": kq_square_q, "kq": kq, "queries": queries, "keys": keys,
                      "keys_norm": keys_norm, "tanh": keys_scaled, "angles": angles, "weighted": weighted,
                      "trig_out": trig_, "match_den": match_den, "match_inv": match_inv, "match_scale": match_scale,
                      "match_sums": match_sums, "gate": gate, "gated": gated, "h1": h1_, "norm2": norm2,
                      "norm2_sum": norm2_sum, "norm2_stats": norm2_stats, "norm2_apply": norm2_apply,
                      "norm2_gain": norm2_gain, "ffn_gain": ffn_gain, "out2": out2, "norm3": norm3,
                      "norm3_sum": norm3_sum, "norm3_stats": norm3_stats, "norm3_apply": norm3_apply,
                      "w2_scale": w2, "w2": w2_add, "proj": proj, "proj_bias": proj_bias, "norm4": norm4,
                      "norm4_sum": norm4_sum, "norm4_stats": norm4_stats, "norm4_apply": norm4_apply,
                      "xsum": route, "logit_max": logit_max, "choose_flags": choose_flags,
                      "choose_terms": choose_terms, "choose": choose, "chosen_p": chosen_p, "ffn_bias": ffn_bias,
                      "ffn_out": ffn_out}
            for k in range(1, TAPS):
                phases[f"conv{k}"] = conv(k)
            for k in range(SOFTPLUS_STEPS):
                phases[f"softplus{k}"] = softplus(k)
            for c in range(2):
                phases[f"match_products{c}"] = match_products(c)
                phases[f"match_add{c}"] = match_add(c)
            for k in range(6):
                phases[f"in_quant{k}"] = in_quant(k)
                phases[f"out_quant{k}"] = out_quant(k)
            for p in range(6):
                phases[f"y{p}"] = y(p)
            for j in range(2):
                phases[f"hid{j}"] = hid1(j)
            for u in range(SU):
                phases[f"score{u}"] = score_max(u)
                phases[f"exp{u}"] = denominators(u)
                if u % 2 == 0:
                    phases[f"mixed{u}"] = keep_mixed(u)
            run(dve, phases)


MIXER = (["norm1", "norm1_stats", "norm1_rstd", "norm1_apply", "keep_x", "xT1", "z", "conv1", "conv2", "conv3", "zT",
          "gate_t", "kq_square", "kq_sum", "kq_square_q", "kq", "kq_exp", "kq_rstd", "queries", "keys", "keys_norm",
          "tanh", "tanh_act", "angles", "trig"]
         + [f"softplus{k}" for k in range(SOFTPLUS_STEPS)] + ["weighted", "trig_out", "skip"])
READOUT = ["cum", "match_den", "match_inv", "match_scale", "match_sums", "match_products0", "match_add0",
           "match_products1", "match_add1", "gate", "gated_sum", "gated_rms", "gated", "gsT", "y0", "y1", "y2", "y3",
           "y4", "y5", "out1", "h1"]
QUANT = (["norm2", "norm2_sum", "norm2_stats", "norm2_rstd", "norm2_apply", "norm2_gain"]
         + [f"in_quant{k}" for k in range(6)] + ["xqT", "hid0", "hid1", "ffn_norm", "ffn_gain"]
         + [f"out_quant{k}" for k in range(6)] + ["yqT", "out2"])
ATTENTION = (["norm3", "norm3_sum", "norm3_stats", "norm3_rstd", "norm3_apply", "xT3", "qkv"]
             + [f"{p}{u}" for u in range(NT // 2) for p in ("score", "exp", "mixed")]
             + ["w", "w2_scale", "wp", "w2", "proj", "proj_bias"])
EXPERTS = ["norm4", "norm4_sum", "norm4_stats", "norm4_rstd", "norm4_apply", "xT4", "xsum", "route", "logit_max",
           "choose_flags", "lexp", "choose_terms", "choose", "chosen_p", "hidden0", "hidden1", "hidden2", "ffn_mm",
           "ffn_bias", "ffn_out"]
STAGES = 5
LAG = {p: k for k, stage in enumerate((MIXER, READOUT, QUANT, ATTENTION, EXPERTS)) for p in stage}


ORDER = [
    "norm3", "norm2", "norm3_sum", "norm3_stats", "norm3_rstd", "norm2_sum", "norm4", "norm2_stats", "cum",
    "norm2_rstd", "match_den", "norm3_apply", "norm4_sum", "match_inv", "xT3", "norm1", "match_scale",
    "match_sums", "norm4_stats", "norm1_stats", "match_products0", "match_add0", "norm4_rstd", "norm4_apply",
    "match_products1", "norm1_rstd", "qkv", "xT4", "norm1_apply", "match_add1", "xsum", "route", "logit_max",
    "choose_flags", "lexp", "score0", "norm2_apply", "gate", "exp0", "choose_terms", "norm2_gain", "xT1",
    "in_quant0", "in_quant1", "choose", "in_quant2", "in_quant3", "score1", "score2", "in_quant4", "chosen_p",
    "exp1", "mixed0", "exp2", "in_quant5", "gated_sum", "z", "score3", "gated_rms", "mixed1", "conv1", "score4",
    "exp3", "xqT", "conv2", "mixed2", "conv3", "exp4", "hid0", "score5", "mixed3", "zT", "kq_square", "hid1",
    "kq_sum", "gated", "exp5", "kq_square_q", "score6", "ffn_norm", "kq", "mixed4", "gate_t", "score7", "exp6",
    "ffn_gain", "out_quant0", "gsT", "kq_rstd", "out_quant1", "out_quant2", "out_quant3", "mixed5",
    "out_quant4", "out_quant5", "exp7", "score8", "kq_exp", "y0", "y1", "y2", "mixed6", "yqT", "score9", "out2",
    "exp8", "mixed7", "exp9", "hidden0", "mixed8", "hidden1", "mixed9", "queries", "y3", "w", "keys",
    "softplus0", "y4", "y5", "w2_scale", "wp", "hidden2", "keys_norm", "tanh", "softplus1", "softplus2",
    "softplus3", "softplus4", "softplus5", "softplus6", "tanh_act", "softplus7", "softplus8", "angles", "w2",
    "ffn_mm", "softplus9", "ffn_bias", "proj", "softplus10", "softplus11", "softplus12", "proj_bias",
    "softplus13", "weighted", "out1", "ffn_out", "trig", "trig_out", "h1", "keep_x", "skip"]
assert sorted(ORDER) == sorted(LAG)


def layout(x):
    import numpy as np

    def arr(name):
        return np.asarray(x[name])

    def rows(v, n=T):
        return np.broadcast_to(v.reshape(1, -1), (n, v.size))

    def twice(v):
        return rows(np.concatenate([v.reshape(-1)] * 2))

    def part(w, p):
        return w.reshape(w.shape[0] // p, p, w.shape[1]).transpose(1, 0, 2)

    d = {}
    px = arr("x").reshape(B, C, NH, PS, NH, PS).transpose(2, 4, 3, 5, 1, 0)
    px = px.reshape(NG, PP, 2, 128, C, B).transpose(0, 3, 1, 4, 2, 5).reshape(NG, 128, PP * C * 2 * B)
    mw = arr("L0_tok_merge_weights")
    mws = np.broadcast_to(mw.reshape(NG, 1, PP * C), (NG, 128, PP * C))
    d["pixels"] = np.concatenate([px, mws], axis=2)
    dw = arr("L0_tok_decode_weights").reshape(NG, PP, D, 2, 128)
    d["dec_w"] = dw.transpose(0, 4, 1, 3, 2).reshape(NG, 128, PP * 2 * D)
    one = np.ones((1, NP_), np.float32)
    stat = np.concatenate([mw.T, arr("L0_tok_merge_biases").reshape(1, NP_), one])
    stat = np.broadcast_to(stat[:, :, None], (5, NP_, B)).reshape(5, NG, PP * B)
    d["bias_s"] = stat.transpose(1, 0, 2)
    db = arr("L0_tok_decode_biases")
    mov = np.stack([db, db, db, np.ones((NP_, D), np.float32), arr("L0_tok_pos_embedding")[1:]])
    d["bias_m"] = mov.reshape(5, NG, PP * D).transpose(1, 0, 2)
    cls = np.stack([arr("cls_tok").reshape(D), arr("L0_tok_cls_embedding"), arr("L0_tok_pos_embedding")[0]])
    d["cls"] = np.broadcast_to(cls[None], (B, 3, D))
    wi = arr("L0_attn_W_in")
    d["W_in"] = part(wi[:, 0:CONV + SKIP], HW)
    wh = np.zeros((D, GR + KH), np.float32)
    wh[:, 0:KH], wh[:, GR:] = wi[:, KH * HD:KH * HD + KH], wi[:, CONV + SKIP:]
    d["W_heads"] = part(wh, HW)
    cw = arr("L0_attn_conv_w").T
    q0 = KH * HD + KH
    d["conv_w"] = np.stack([cw[0:HW], cw[HW:2 * HW], cw[q0:q0 + HW], cw[q0 + HW:q0 + 2 * HW]], axis=1)
    d["conv_ws"] = cw[KH * HD:q0]
    d["k_norm"] = twice(np.broadcast_to(arr("L0_attn_k_norm_w"), (KH, HD)))
    d["tanh_scale"] = twice(np.broadcast_to(arr("L0_attn_tanh_scale")[:, None], (KH, HD)))
    d["theta"] = twice(arr("L0_attn_theta_raw"))
    qn = arr("L0_attn_q_norm_w").reshape(NQ, 1, HD, 2)
    qn = np.broadcast_to(qn, (NQ, 2, HD, 2)).transpose(3, 0, 1, 2)
    wi = np.broadcast_to(arr("L0_attn_w_int_raw").reshape(1, D), (2, D))
    d["q_norm"] = rows(np.concatenate([qn[0].reshape(-1)] * 2 + [qn[1].reshape(-1)] * 2)).reshape(T, 2, 2 * D)
    d["w_int"] = rows(np.concatenate([wi[0]] * 4)).reshape(T, 2, 2 * D)
    d["score_w"] = twice(arr("L0_attn_score_scale"))
    d["score_b"] = twice(arr("L0_attn_score_bias"))
    d["decay"] = twice(arr("L0_attn_decay_slopes"))
    left = np.arange(L - 1, -1, -1, dtype=np.float32).reshape(2, T).T
    d["dist"] = np.repeat(left, KH, axis=1)
    d["W_gate"] = arr("L0_attn_W_gate")
    ro, sk = arr("L0_attn_W_readout"), arr("L0_attn_W_skip")
    gn, hs = arr("L0_attn_gnorm_w").reshape(KH, 2 * HD), arr("L0_attn_highway_scale")
    wr = np.zeros((112, 6, 2 * HW), np.float32)
    wf = np.ones((112, 6, 2 * HW), np.float32)
    for k in range(KH):
        p, e = k // 2, k % 2
        for half in range(2):
            c0, s0 = half * HW + e * FS, half * FS
            wr[32 * e:32 * e + 32, p, c0:c0 + FS] = ro[k, :, s0:s0 + FS]
            wf[32 * e:32 * e + 32, p, c0:c0 + FS] = gn[k][:, None]
            wr[64:112, p, c0:c0 + FS] = sk[:, k * HW + s0:k * HW + s0 + FS]
            wf[64:112, p, c0:c0 + FS] = hs[k]
    d["W_read"], d["W_read_f"] = wr, wf
    d["W_out"] = part(arr("L0_attn_W_out"), HW)
    d["ffn_w1"] = part(arr("L0_ffn_w_in").T, HW)
    d["ffn_w2"] = part(arr("L0_ffn_w_out").T, 128)
    d["g_in"] = twice(arr("L0_ffn_g_in"))
    d["g_out"] = rows(arr("L0_ffn_g_out"))
    d["W_qkv"] = part(arr("L1_attn_W_qkv"), HW)
    d["mix_l"] = part(np.repeat(arr("L1_attn_W_l"), HD, axis=0), HW)
    mw2 = np.zeros((SR + 1, KH, NB), np.float32)
    for n in range(NB):
        mw2[n:SR:NB, :, n] = arr("L1_attn_W_w")
    mw2[SR] = arr("L1_attn_b_w")[:, None]
    d["mix_w"] = mw2.reshape(SR + 1, SR)
    d["b_l"] = np.tile(np.repeat(arr("L1_attn_b_l"), NB), NT).reshape(1, NT * SR)
    d["lam"] = np.repeat(arr("L1_attn_lamb").reshape(3, 4), 32, axis=1).T
    wp = np.zeros((3, 4, 32, D), np.float32)
    wp[:, :, 0:HD, :] = arr("L1_attn_W_proj").reshape(3, 4, HD, D)
    d["W_proj"] = wp.reshape(3, 128, D).transpose(1, 0, 2)
    d["b_proj"] = twice(arr("L1_attn_b_proj"))
    d["W_route"] = part(arr("L1_ffn_Wg").T, HW)
    d["W1"] = arr("L1_ffn_W1").reshape(NE, 2, HW, FM).transpose(0, 2, 1, 3).reshape(NE, HW, 2 * FM)
    d["W2"] = arr("L1_ffn_W2").reshape(NE, 6, 128, D).transpose(0, 2, 1, 3).reshape(NE, 128, 6 * D)
    d["b1"] = arr("L1_ffn_b1").reshape(NE, 6, 128).transpose(0, 2, 1)
    b2 = arr("L1_ffn_b2")
    d["b2"] = np.broadcast_to(np.concatenate([b2, b2], axis=1)[:, None, :], (NE, T, 2 * D))
    d["upper"] = np.triu(np.ones((T, T), np.float32))
    d["ident"] = np.eye(128, dtype=np.float32)
    return {k: np.ascontiguousarray(v) for k, v in d.items()}


def kernel(**inputs):
    import concourse.bacc as _bacc
    from concourse.bass_utils import run_bass_kernel_spmd as _run

    arrays = {f"in_{k}": v for k, v in layout(inputs).items()}
    nc = _bacc.Bacc("TRN2", target_bir_lowering=False, num_devices=1)
    a = {k[3:]: nc.dram_tensor(k, v.shape, mybir.dt.from_np(v.dtype), kind="ExternalInput").ap()
         for k, v in arrays.items()}
    out = nc.dram_tensor("out_tokens", (B, L, D), mybir.dt.float32, kind="ExternalOutput").ap()
    vit_program(nc, a, out)
    r = _run(nc, [arrays], core_ids=[0])
    return r.results[0]["out_tokens"]
```
